# Optimizing a Trainium2 kernel written in Bass

```python
import numpy as np
import jax
import jax.numpy as jnp

def _softmax(x, axis=-1):
    return jax.nn.softmax(x, axis=axis)

def _gelu(x):
    return jax.nn.gelu(x, approximate=True)

def _silu(x):
    return jax.nn.silu(x)

def _sigmoid(x):
    return jax.nn.sigmoid(x)

def _layernorm(x, axis=-1, eps=1e-05):
    m = jnp.mean(x, axis=axis, keepdims=True)
    v = jnp.var(x, axis=axis, keepdims=True)
    return (x - m) / jnp.sqrt(v + eps)

def _scatter_add(tgt, idx, src, axis=0):
    return tgt.at[idx].add(src)

def _segment_sum(src, seg, n):
    return jax.ops.segment_sum(src, seg, n)
kernel_name = 'mk_decoder_preln_d1_seqx_r4_2af991'

def setup_inputs(seed: int=0):
    np.random.seed(seed)
    _w = jnp.asarray

    def _rec_inputs():
        import jax
        import jax.numpy as jnp
        _rk = jax.random.key(seed)
        x = 7.22e-05 + 1 * jax.random.normal(jax.random.fold_in(_rk, 1), (4, 512, 512), jnp.float32)
        _lenS = 512 - jax.random.randint(jax.random.fold_in(_rk, 7), (4,), 0, max(1, 512 // 4) + 1, jnp.int32)
        _lenS2 = 64 - jax.random.randint(jax.random.fold_in(_rk, 8), (4,), 0, max(1, 64 // 4) + 1, jnp.int32)
        _ctx_2048P = jax.random.normal(jax.random.fold_in(_rk, 11), (4, 16, 512), jnp.float32)
        _ctx_2048c = jax.random.dirichlet(jax.random.fold_in(_rk, 511), 0.3 * jnp.ones((16,), jnp.float32), (4, 64))
        _ctx_2048t = jnp.einsum('bsk,bkd->bsd', _ctx_2048c, _ctx_2048P)
        _ctx_2048t = _ctx_2048t * jax.lax.rsqrt(jnp.mean(jnp.square(_ctx_2048t)) + 1e-12) * 0.953939
        ctx_2048 = -0.000514642 + 1.00011 * (_ctx_2048t + 0.3 * jax.random.normal(jax.random.fold_in(_rk, 611), (4, 64, 512), jnp.float32))
        return (x, ctx_2048)
    x, ctx_2048 = _rec_inputs()

    def _L0_attn_setup():
        import jax, jax.numpy as jnp
        import numpy as np
        DIM = 512
        H = 16
        DK = 128
        DV = 128
        KCONV = 4
        EPS = 1e-06
        B = 2
        S = 512
        KD = H * DK
        VD = H * DV

        def _causal_conv(x, w, b):
            Bb, Ss, C = x.shape
            xp = jnp.pad(x, ((0, 0), (KCONV - 1, 0), (0, 0)))
            out = b
            for j in range(KCONV):
                out = out + xp[:, j:j + Ss, :] * w[:, j]
            return jax.nn.silu(out)

        def _l2norm(x):
            n = jnp.sqrt(jnp.sum(x * x, axis=-1, keepdims=True))
            return x / jnp.maximum(n, 1e-12)

        def _forward(x, Wq, Wk, Wv, Wa, Wb, Wg, Wo, cw_q, cb_q, cw_k, cb_k, cw_v, cb_v, A_log, dt_bias, norm_w):
            Bb, Ss, _ = x.shape
            q = _causal_conv(x @ Wq.T, cw_q, cb_q)
            k = _causal_conv(x @ Wk.T, cw_k, cb_k)
            v = _causal_conv(x @ Wv.T, cw_v, cb_v)
            a = x @ Wa.T
            b = x @ Wb.T
            g = jnp.exp(-jnp.exp(A_log)[None, None, :] * jax.nn.softplus(a + dt_bias[None, None, :]))
            beta = jax.nn.sigmoid(b)
            q = _l2norm(q.reshape(Bb, Ss, H, DK))
            k = _l2norm(k.reshape(Bb, Ss, H, DK))
            v = v.reshape(Bb, Ss, H, DV)
            S0 = jnp.zeros((Bb, H, DK, DV), dtype=x.dtype)

            def step(Sstate, inputs):
                q_t, k_t, v_t, g_t, beta_t = inputs
                retrieved = jnp.einsum('bhkv,bhk->bhv', Sstate, k_t)
                error = v_t - g_t[..., None] * retrieved
                update = k_t[..., :, None] * (beta_t[..., None] * error)[..., None, :]
                Snew = g_t[..., None, None] * Sstate + update
                o_t = jnp.einsum('bhkv,bhk->bhv', Snew, q_t)
                return (Snew, o_t)
            xs = (q.transpose(1, 0, 2, 3), k.transpose(1, 0, 2, 3), v.transpose(1, 0, 2, 3), g.transpose(1, 0, 2), beta.transpose(1, 0, 2))
            _, o = jax.lax.scan(step, S0, xs)
            o = o.transpose(1, 0, 2, 3).reshape(Bb, Ss, VD)
            o = o * jax.lax.rsqrt(jnp.mean(o * o, axis=-1, keepdims=True) + EPS) * norm_w
            o = o * jax.nn.silu(x @ Wg.T)
            return o @ Wo.T
        key = jax.random.key(seed)
        ks = jax.random.split(key, 16)
        sc = 0.02
        inp = {'x': jax.random.normal(ks[0], (B, S, DIM), dtype=jnp.float32), 'Wq': jax.random.normal(ks[1], (KD, DIM), dtype=jnp.float32) * sc, 'Wk': jax.random.normal(ks[2], (KD, DIM), dtype=jnp.float32) * sc, 'Wv': jax.random.normal(ks[3], (VD, DIM), dtype=jnp.float32) * sc, 'Wa': jax.random.normal(ks[4], (H, DIM), dtype=jnp.float32) * sc, 'Wb': jax.random.normal(ks[5], (H, DIM), dtype=jnp.float32) * sc, 'Wg': jax.random.normal(ks[6], (VD, DIM), dtype=jnp.float32) * sc, 'Wo': jax.random.normal(ks[7], (DIM, VD), dtype=jnp.float32) * sc, 'cw_q': jax.random.normal(ks[8], (KD, KCONV), dtype=jnp.float32) * 0.3, 'cb_q': jnp.zeros((KD,), dtype=jnp.float32), 'cw_k': jax.random.normal(ks[9], (KD, KCONV), dtype=jnp.float32) * 0.3, 'cb_k': jnp.zeros((KD,), dtype=jnp.float32), 'cw_v': jax.random.normal(ks[10], (VD, KCONV), dtype=jnp.float32) * 0.3, 'cb_v': jnp.zeros((VD,), dtype=jnp.float32), 'A_log': jnp.zeros((H,), dtype=jnp.float32), 'dt_bias': jnp.zeros((H,), dtype=jnp.float32), 'norm_w': jnp.ones((VD,), dtype=jnp.float32)}
        return inp
    _L0_attn_all = _L0_attn_setup()
    _L0_attn_in = {k: v for k, v in _L0_attn_all.items() if k in ('Wq', 'Wk', 'Wv', 'Wa', 'Wb', 'Wg', 'Wo', 'cw_q', 'cb_q', 'cw_k', 'cb_k', 'cw_v', 'cb_v', 'A_log', 'dt_bias', 'norm_w')}
    del _L0_attn_all

    def _L0_xattn_setup():
        import jax, jax.numpy as jnp
        import numpy as np
        D_MODEL = 512
        NUM_HEADS = 16
        HEAD_DIM = D_MODEL // NUM_HEADS

        def _fq_sym(x, axis):
            s = jnp.max(jnp.abs(x), axis=axis, keepdims=True) / 127.0
            s = jnp.maximum(s, 1e-08)
            q = jnp.clip(jnp.round(x / s), -127.0, 127.0) * s
            return x + jax.lax.stop_gradient(q - x)

        def _fq_unsigned(x, axis):
            s = jnp.max(x, axis=axis, keepdims=True) / 255.0
            s = jnp.maximum(s, 1e-08)
            q = jnp.clip(jnp.round(x / s), 0.0, 255.0) * s
            return x + jax.lax.stop_gradient(q - x)
        key = jax.random.key(seed)
        ks = jax.random.split(key, 8)
        B, N, M, C = (2, 512, 128, D_MODEL)
        return {'x': jax.random.normal(ks[0], (B, N, C), jnp.float32), 'cond': jax.random.normal(ks[1], (B, M, C), jnp.float32), 'Wq': jax.random.normal(ks[2], (C, C), jnp.float32) * 0.02, 'bq': jnp.zeros((C,), jnp.float32), 'Wkv': jax.random.normal(ks[3], (C, 2 * C), jnp.float32) * 0.02, 'bkv': jnp.zeros((2 * C,), jnp.float32), 'Wp': jax.random.normal(ks[4], (C, C), jnp.float32) * 0.02, 'bp': jnp.zeros((C,), jnp.float32)}
    _L0_xattn_all = _L0_xattn_setup()
    _L0_xattn_in = {k: v for k, v in _L0_xattn_all.items() if k in ('Wq', 'bq', 'Wkv', 'bkv', 'Wp', 'bp')}
    del _L0_xattn_all

    def _L0_ffn_setup():
        import jax, jax.numpy as jnp
        import numpy as np
        D = 512
        H = 16
        KV = 4
        DH = 128
        RD = 64
        E = 8
        TOPK = 2
        I = 256
        EPS = 1e-06
        THETA = 1000000.0

        def rmsnorm(h, w, eps=EPS):
            dt = h.dtype
            h32 = h.astype(jnp.float32)
            var = jnp.mean(h32 * h32, axis=-1, keepdims=True)
            return (w * (h32 * jax.lax.rsqrt(var + eps))).astype(dt)

        def rotate_half(t):
            half = t.shape[-1] // 2
            return jnp.concatenate([-t[..., half:], t[..., :half]], axis=-1)
        key = jax.random.key(seed)
        ks = jax.random.split(key, 16)
        s = lambda k, shape, sc: jax.random.normal(k, shape, dtype=jnp.float32) * sc
        B, S = (1, 512)
        return {'x': s(ks[0], (B, S, D), 1.0), 'ln1_w': jnp.ones((D,), jnp.float32), 'ln2_w': jnp.ones((D,), jnp.float32), 'wq': s(ks[1], (D, H * DH), 0.02), 'wk': s(ks[2], (D, KV * DH), 0.02), 'wv': s(ks[3], (D, KV * DH), 0.02), 'wo': s(ks[4], (H * DH, D), 0.02), 'qnorm_w': jnp.ones((H * DH,), jnp.float32), 'knorm_w': jnp.ones((KV * DH,), jnp.float32), 'router_w': s(ks[5], (D, E), 0.02), 'router_bias': s(ks[6], (E,), 0.1), 'wg': s(ks[7], (E, D, I), 0.02), 'wu': s(ks[8], (E, D, I), 0.02), 'wd': s(ks[9], (E, I, D), 0.02)}
    _L0_ffn_all = _L0_ffn_setup()
    _L0_ffn_in = {k: v for k, v in _L0_ffn_all.items() if k in ('ln1_w', 'ln2_w', 'wq', 'wk', 'wv', 'wo', 'qnorm_w', 'knorm_w', 'router_w', 'router_bias', 'wg', 'wu', 'wd')}
    del _L0_ffn_all
    return {'x': x, 'ctx_2048': ctx_2048, 'L0_attn_Wq': _L0_attn_in['Wq'], 'L0_attn_Wk': _L0_attn_in['Wk'], 'L0_attn_Wv': _L0_attn_in['Wv'], 'L0_attn_Wa': _L0_attn_in['Wa'], 'L0_attn_Wb': _L0_attn_in['Wb'], 'L0_attn_Wg': _L0_attn_in['Wg'], 'L0_attn_Wo': _L0_attn_in['Wo'], 'L0_attn_cw_q': _L0_attn_in['cw_q'], 'L0_attn_cb_q': _L0_attn_in['cb_q'], 'L0_attn_cw_k': _L0_attn_in['cw_k'], 'L0_attn_cb_k': _L0_attn_in['cb_k'], 'L0_attn_cw_v': _L0_attn_in['cw_v'], 'L0_attn_cb_v': _L0_attn_in['cb_v'], 'L0_attn_A_log': _L0_attn_in['A_log'], 'L0_attn_dt_bias': _L0_attn_in['dt_bias'], 'L0_attn_norm_w': _L0_attn_in['norm_w'], 'L0_xattn_Wq': _L0_xattn_in['Wq'], 'L0_xattn_bq': _L0_xattn_in['bq'], 'L0_xattn_Wkv': _L0_xattn_in['Wkv'], 'L0_xattn_bkv': _L0_xattn_in['bkv'], 'L0_xattn_Wp': _L0_xattn_in['Wp'], 'L0_xattn_bp': _L0_xattn_in['bp'], 'L0_ffn_ln1_w': _L0_ffn_in['ln1_w'], 'L0_ffn_ln2_w': _L0_ffn_in['ln2_w'], 'L0_ffn_wq': _L0_ffn_in['wq'], 'L0_ffn_wk': _L0_ffn_in['wk'], 'L0_ffn_wv': _L0_ffn_in['wv'], 'L0_ffn_wo': _L0_ffn_in['wo'], 'L0_ffn_qnorm_w': _L0_ffn_in['qnorm_w'], 'L0_ffn_knorm_w': _L0_ffn_in['knorm_w'], 'L0_ffn_router_w': _L0_ffn_in['router_w'], 'L0_ffn_router_bias': _L0_ffn_in['router_bias'], 'L0_ffn_wg': _L0_ffn_in['wg'], 'L0_ffn_wu': _L0_ffn_in['wu'], 'L0_ffn_wd': _L0_ffn_in['wd']}

def reference(x, ctx_2048, L0_attn_Wq, L0_attn_Wk, L0_attn_Wv, L0_attn_Wa, L0_attn_Wb, L0_attn_Wg, L0_attn_Wo, L0_attn_cw_q, L0_attn_cb_q, L0_attn_cw_k, L0_attn_cb_k, L0_attn_cw_v, L0_attn_cb_v, L0_attn_A_log, L0_attn_dt_bias, L0_attn_norm_w, L0_xattn_Wq, L0_xattn_bq, L0_xattn_Wkv, L0_xattn_bkv, L0_xattn_Wp, L0_xattn_bp, L0_ffn_ln1_w, L0_ffn_ln2_w, L0_ffn_wq, L0_ffn_wk, L0_ffn_wv, L0_ffn_wo, L0_ffn_qnorm_w, L0_ffn_knorm_w, L0_ffn_router_w, L0_ffn_router_bias, L0_ffn_wg, L0_ffn_wu, L0_ffn_wd):
    import jax
    import jax.numpy as jnp

    def _L0_attn_ref(x, Wq, Wk, Wv, Wa, Wb, Wg, Wo, cw_q, cb_q, cw_k, cb_k, cw_v, cb_v, A_log, dt_bias, norm_w):
        import jax, jax.numpy as jnp
        import numpy as np
        DIM = 512
        H = 16
        DK = 128
        DV = 128
        KCONV = 4
        EPS = 1e-06
        B = 2
        S = 512
        KD = H * DK
        VD = H * DV

        def _causal_conv(x, w, b):
            Bb, Ss, C = x.shape
            xp = jnp.pad(x, ((0, 0), (KCONV - 1, 0), (0, 0)))
            out = b
            for j in range(KCONV):
                out = out + xp[:, j:j + Ss, :] * w[:, j]
            return jax.nn.silu(out)

        def _l2norm(x):
            n = jnp.sqrt(jnp.sum(x * x, axis=-1, keepdims=True))
            return x / jnp.maximum(n, 1e-12)

        def _forward(x, Wq, Wk, Wv, Wa, Wb, Wg, Wo, cw_q, cb_q, cw_k, cb_k, cw_v, cb_v, A_log, dt_bias, norm_w):
            Bb, Ss, _ = x.shape
            q = _causal_conv(x @ Wq.T, cw_q, cb_q)
            k = _causal_conv(x @ Wk.T, cw_k, cb_k)
            v = _causal_conv(x @ Wv.T, cw_v, cb_v)
            a = x @ Wa.T
            b = x @ Wb.T
            g = jnp.exp(-jnp.exp(A_log)[None, None, :] * jax.nn.softplus(a + dt_bias[None, None, :]))
            beta = jax.nn.sigmoid(b)
            q = _l2norm(q.reshape(Bb, Ss, H, DK))
            k = _l2norm(k.reshape(Bb, Ss, H, DK))
            v = v.reshape(Bb, Ss, H, DV)
            S0 = jnp.zeros((Bb, H, DK, DV), dtype=x.dtype)

            def step(Sstate, inputs):
                q_t, k_t, v_t, g_t, beta_t = inputs
                retrieved = jnp.einsum('bhkv,bhk->bhv', Sstate, k_t)
                error = v_t - g_t[..., None] * retrieved
                update = k_t[..., :, None] * (beta_t[..., None] * error)[..., None, :]
                Snew = g_t[..., None, None] * Sstate + update
                o_t = jnp.einsum('bhkv,bhk->bhv', Snew, q_t)
                return (Snew, o_t)
            xs = (q.transpose(1, 0, 2, 3), k.transpose(1, 0, 2, 3), v.transpose(1, 0, 2, 3), g.transpose(1, 0, 2), beta.transpose(1, 0, 2))
            _, o = jax.lax.scan(step, S0, xs)
            o = o.transpose(1, 0, 2, 3).reshape(Bb, Ss, VD)
            o = o * jax.lax.rsqrt(jnp.mean(o * o, axis=-1, keepdims=True) + EPS) * norm_w
            o = o * jax.nn.silu(x @ Wg.T)
            return o @ Wo.T
        return _forward(x, Wq, Wk, Wv, Wa, Wb, Wg, Wo, cw_q, cb_q, cw_k, cb_k, cw_v, cb_v, A_log, dt_bias, norm_w)

    def _L0_xattn_ref(x, cond, Wq, bq, Wkv, bkv, Wp, bp):
        import jax, jax.numpy as jnp
        import numpy as np
        D_MODEL = 512
        NUM_HEADS = 16
        HEAD_DIM = D_MODEL // NUM_HEADS

        def _fq_sym(x, axis):
            s = jnp.max(jnp.abs(x), axis=axis, keepdims=True) / 127.0
            s = jnp.maximum(s, 1e-08)
            q = jnp.clip(jnp.round(x / s), -127.0, 127.0) * s
            return x + jax.lax.stop_gradient(q - x)

        def _fq_unsigned(x, axis):
            s = jnp.max(x, axis=axis, keepdims=True) / 255.0
            s = jnp.maximum(s, 1e-08)
            q = jnp.clip(jnp.round(x / s), 0.0, 255.0) * s
            return x + jax.lax.stop_gradient(q - x)
        B, N, C = x.shape
        H, hd = (NUM_HEADS, HEAD_DIM)
        q = (x @ Wq + bq).reshape(1, B * N, H, hd)
        kv = (cond @ Wkv + bkv).reshape(1, -1, 2, H, hd)
        k, v = (kv[:, :, 0], kv[:, :, 1])
        scale = 1.0 / np.sqrt(hd).astype(np.float32)
        q = jnp.transpose(q * scale, (0, 2, 1, 3))
        k = jnp.transpose(k, (0, 2, 1, 3))
        v = jnp.transpose(v, (0, 2, 1, 3))
        q = _fq_sym(q, axis=-1)
        k = _fq_sym(k, axis=-1)
        v = _fq_sym(v, axis=2)
        attn = jnp.einsum('bhqd,bhkd->bhqk', q, k)
        attn = jax.nn.softmax(attn.astype(jnp.float32), axis=-1)
        attn = _fq_unsigned(attn, axis=-1)
        out = jnp.einsum('bhqk,bhkd->bhqd', attn, v)
        out = jnp.transpose(out, (0, 2, 1, 3)).reshape(B, N, C)
        return out @ Wp + bp

    def _L0_ffn_ref(x, ln1_w, ln2_w, wq, wk, wv, wo, qnorm_w, knorm_w, router_w, router_bias, wg, wu, wd):
        import jax, jax.numpy as jnp
        import numpy as np
        D = 512
        H = 16
        KV = 4
        DH = 128
        RD = 64
        E = 8
        TOPK = 2
        I = 256
        EPS = 1e-06
        THETA = 1000000.0

        def rmsnorm(h, w, eps=EPS):
            dt = h.dtype
            h32 = h.astype(jnp.float32)
            var = jnp.mean(h32 * h32, axis=-1, keepdims=True)
            return (w * (h32 * jax.lax.rsqrt(var + eps))).astype(dt)

        def rotate_half(t):
            half = t.shape[-1] // 2
            return jnp.concatenate([-t[..., half:], t[..., :half]], axis=-1)
        B, S, _ = x.shape
        res = x
        h = rmsnorm(x, ln1_w)
        q = h @ wq
        k = h @ wk
        v = h @ wv
        q = rmsnorm(q, qnorm_w)
        k = rmsnorm(k, knorm_w)
        q = q.reshape(B, S, H, DH).transpose(0, 2, 1, 3)
        k = k.reshape(B, S, KV, DH).transpose(0, 2, 1, 3)
        v = v.reshape(B, S, KV, DH).transpose(0, 2, 1, 3)
        pos = jnp.arange(S, dtype=jnp.float32)
        inv_freq = 1.0 / THETA ** (jnp.arange(0, RD, 2, dtype=jnp.float32) / RD)
        ang = pos[:, None] * inv_freq[None, :]
        emb = jnp.concatenate([ang, ang], axis=-1)
        cos, sin = (jnp.cos(emb), jnp.sin(emb))

        def rope(t):
            rot, pas = (t[..., :RD], t[..., RD:])
            rot = rot * cos + rotate_half(rot) * sin
            return jnp.concatenate([rot, pas], axis=-1)
        q, k = (rope(q), rope(k))
        rep = H // KV
        k = jnp.repeat(k, rep, axis=1)
        v = jnp.repeat(v, rep, axis=1)
        scores = jnp.einsum('bhqd,bhkd->bhqk', q, k) / np.sqrt(DH)
        causal = jnp.tril(jnp.ones((S, S), dtype=bool))
        scores = jnp.where(causal, scores, jnp.finfo(jnp.float32).min)
        attn = jax.nn.softmax(scores.astype(jnp.float32), axis=-1).astype(q.dtype)
        o = jnp.einsum('bhqk,bhkd->bhqd', attn, v)
        o = o.transpose(0, 2, 1, 3).reshape(B, S, H * DH) @ wo
        x1 = res + o
        h2 = rmsnorm(x1, ln2_w)
        t = h2.reshape(-1, D)
        T = t.shape[0]
        logits = t.astype(jnp.float32) @ router_w
        sig = jax.nn.sigmoid(logits)
        _, topi = jax.lax.top_k(sig + router_bias, TOPK)
        aff = jnp.take_along_axis(sig, topi, axis=-1)
        aff = aff / jnp.sum(aff, axis=-1, keepdims=True)
        combine = jnp.zeros((T, E), jnp.float32).at[jnp.arange(T)[:, None], topi].set(aff)
        gate = jnp.einsum('td,edi->tei', t, wg)
        up = jnp.einsum('td,edi->tei', t, wu)
        act = jax.nn.silu(gate) * up
        moe = jnp.einsum('te,tei,eid->td', combine.astype(t.dtype), act, wd)
        return x1 + moe.reshape(B, S, D)
    x = x + _L0_attn_ref(_layernorm(x, axis=-1), L0_attn_Wq, L0_attn_Wk, L0_attn_Wv, L0_attn_Wa, L0_attn_Wb, L0_attn_Wg, L0_attn_Wo, L0_attn_cw_q, L0_attn_cb_q, L0_attn_cw_k, L0_attn_cb_k, L0_attn_cw_v, L0_attn_cb_v, L0_attn_A_log, L0_attn_dt_bias, L0_attn_norm_w)
    x = x + _L0_xattn_ref(_layernorm(x, axis=-1), ctx_2048, L0_xattn_Wq, L0_xattn_bq, L0_xattn_Wkv, L0_xattn_bkv, L0_xattn_Wp, L0_xattn_bp)
    x = x + _L0_ffn_ref(_layernorm(x, axis=-1), L0_ffn_ln1_w, L0_ffn_ln2_w, L0_ffn_wq, L0_ffn_wk, L0_ffn_wv, L0_ffn_wo, L0_ffn_qnorm_w, L0_ffn_knorm_w, L0_ffn_router_w, L0_ffn_router_bias, L0_ffn_wg, L0_ffn_wu, L0_ffn_wd)
    return x

_drawn_inputs = setup_inputs


def setup_inputs(seed=0):
    import zlib

    import numpy as np

    out = dict(_drawn_inputs(seed))
    spreads = {'L0_attn_cb_q': (0.0, 0.1),
     'L0_attn_cb_k': (0.0, 0.1),
     'L0_attn_cb_v': (0.0, 0.1),
     'L0_attn_A_log': (0.0, 0.76),
     'L0_attn_dt_bias': (0.0, 0.8),
     'L0_attn_norm_w': (1.0, 0.2),
     'L0_xattn_bq': (0.0, 0.8),
     'L0_xattn_bkv': (0.0, 0.1),
     'L0_xattn_bp': (0.0, 0.1),
     'L0_ffn_ln1_w': (1.0, 0.6),
     'L0_ffn_ln2_w': (1.0, 0.6),
     'L0_ffn_qnorm_w': (1.0, 0.6),
     'L0_ffn_knorm_w': (1.0, 0.6)}
    factors = {'L0_xattn_Wq': 8.0,
     'L0_ffn_router_w': 5.478,
     'L0_ffn_router_bias': 5.595,
     'L0_ffn_wg': 4.343,
     'L0_ffn_wu': 4.218,
     'L0_ffn_wd': 4.231}
    for name, (base, spread) in spreads.items():
        noise = np.random.default_rng([zlib.crc32(name.encode()), seed]).standard_normal(out[name].shape)
        drawn = base * np.exp(spread * noise) if base else spread * noise
        out[name] = jnp.asarray(drawn.astype(out[name].dtype))
    for name, factor in factors.items():
        out[name] = (out[name] * factor).astype(out[name].dtype)
    return out
```

```python
from contextlib import ExitStack

import concourse.bass as bass
from concourse import mybir

ALU = mybir.AluOpType
ACT = mybir.ActivationFunctionType
AX = mybir.AxisListType
F32 = mybir.dt.float32
BF16 = mybir.dt.bfloat16

P = 128
B, SEQ, DIM = 4, 512, 512
TOK = B * SEQ
TILES = TOK // P
KT = DIM // P
CH = SEQ // P
HEADS = 16
BN = B * P
LN_EPS = 1e-5
RMS_EPS = 1e-6
MAGIC = 12582912.0
LEVELS = [2, 4, 8, 16, 32, 64]
NLV = len(LEVELS)

C_ID, C_UP, C_GT, C_M1, C_LV = 0, P, 2 * P, 3 * P, 4 * P
C_ONE = C_LV + 64 * NLV
C_NEG = C_ONE + P
C_W = C_NEG + P


def second(ap, m):
    return ap.rearrange("p b (g two m) -> p b g two m", two=2, m=m)[:, :, :, 1, :]


def first(ap, m):
    return ap.rearrange("p b (g two m) -> p b g two m", two=2, m=m)[:, :, :, 0, :]


def bc(col, n):
    return col.unsqueeze(2).to_broadcast([col.shape[0], col.shape[1], n])


def semaphores(nc, ctx, prefix):
    held = []

    def release():
        nc.clear_and_free_semaphores(held)
        nc.all_engine_barrier()

    def sem(name):
        held.append(nc.alloc_semaphore(f"{prefix}_{name}"))
        return held[-1]

    ctx.callback(release)
    return sem


def layernorm_transposed(nc, name, x_dram, const_dram, xnT, after_batch=None):
    with ExitStack() as ctx:
        sem = semaphores(nc, ctx, name)

        def sb(n, s, d=F32):
            return ctx.enter_context(nc.sbuf_tensor(f"{name}_{n}", s, d))


        ident = sb("ident", [P, P])
        xt = sb("xt", [P, CH, DIM])
        xn = sb("xn", [P, CH, DIM])
        stats = sb("stats", [P, CH, 6])
        mv = sb("mv", [P, CH, 2])
        eps = sb("eps", [P, 1])
        std = sb("std", [P, CH])
        rstd = sb("rstd", [P, CH])
        psT = [ctx.enter_context(nc.psum_tensor(f"{name}_psT{k}", [P, BN], F32)) for k in range(2)]
        ident_in, x_in, eps_set = sem("ident_in"), sem("x_in"), sem("eps_set")
        stat_done, var_done, std_done, rstd_done = sem("stat"), sem("var"), sem("std"), sem("rstd")
        xn_done, turned, copied = sem("xn"), sem("turned"), sem("copied")
        block = ctx.enter_context(nc.Block())

        @block.sync
        def _(sp):
            sp.dma_start(ident[:, :], const_dram[:, C_ID:C_ID + P]).then_inc(ident_in, 16)
            sp.sem_inc(xn_done, CH)
            for b in range(B):
                sp.wait_ge(xn_done, b * CH + CH)
                sp.dma_start(xt[:, :, :], x_dram[bass.ds(b * SEQ, SEQ), :].rearrange("(t p) d -> p t d", p=P)
                             ).then_inc(x_in, 16)

        @block.vector
        def _(dve):
            nc.vector.memset(eps[:, :], LN_EPS).then_inc(eps_set, 1)
            dve.sem_inc(turned, KT)
            for b in range(B):
                dve.wait_ge(x_in, b * 16 + 16)
                for t in range(CH):
                    nc.vector.bn_stats(stats[:, t, :], xt[:, t, :]).then_inc(stat_done, 1)
                for t in range(CH):
                    dve.wait_ge(stat_done, b * CH + t + 1)
                    nc.vector.bn_aggr(mv[:, t, :], stats[:, t, :]).then_inc(var_done, 1)
                dve.wait_ge(std_done, b + 1)
                nc.vector.reciprocal(rstd[:, :], std[:, :]).then_inc(rstd_done, 1)
                dve.wait_ge(rstd_done, b + 1)
                dve.wait_ge(turned, b * KT + KT)
                for t in range(CH):
                    nc.vector.tensor_scalar(xn[:, t, :], xt[:, t, :], mv[:, t, 0:1], rstd[:, t:t + 1],
                                            ALU.subtract, ALU.mult).then_inc(xn_done, 1)

        @block.scalar
        def _(act):
            act.wait_ge(eps_set, 1)
            for b in range(B):
                act.wait_ge(var_done, b * CH + CH)
                nc.scalar.activation(std[:, :], mv[:, :, 1], ACT.Sqrt, bias=eps[:, 0:1]).then_inc(std_done, 1)
                for k in range(KT):
                    act.wait_ge(turned, b * KT + k + 1 + KT)
                    nc.scalar.copy(xnT[:, k, bass.ds(b * SEQ, SEQ)], psT[k % 2][:, :]).then_inc(copied, 1)

        @block.tensor
        def _(pe):
            pe.wait_ge(ident_in, 16)
            pe.sem_inc(copied, 2)
            for b in range(B):
                pe.wait_ge(xn_done, b * CH + CH + CH)
                for k in range(KT):
                    pe.wait_ge(copied, b * KT + k + 1)
                    for t in range(CH):
                        tr = pe.transpose(psT[k % 2][:, t * P:(t + 1) * P], xn[:, t, k * P:(k + 1) * P], ident[:, :])
                    tr.then_inc(turned, 1)


PW = 68
PA = 32
PN = 64


def delta_gates(nc, xnT, A, const_dram, ptab):
    with ExitStack() as ctx:
        sem = semaphores(nc, ctx, "ga")

        def sb(n, s, d=F32):
            return ctx.enter_context(nc.sbuf_tensor(f"ga_{n}", s, d))


        def ps(n, s):
            return ctx.enter_context(nc.psum_tensor(f"ga_{n}", s, F32))

        G2 = 2 * HEADS
        cst = sb("cst", [P, 2 * P])
        wab = sb("wab", [G2, DIM])
        wabT = sb("wabT", [P, KT, G2])
        ab = sb("ab", [G2, BN])
        abt = sb("abt", [P, B, CH, G2])
        alog = sb("alog", [P, HEADS])
        dtb = sb("dtb", [P, HEADS])
        ea = sb("ea", [P, HEADS])
        gsh = [P, B, CH, HEADS]
        z, az, rz, ez, lz = (sb(n, gsh) for n in ("z", "az", "rz", "ez", "lz"))
        beta = sb("beta", gsh)
        gam = sb("gam", [P, HEADS, TILES])
        psW = ps("psW", [P, KT, G2])
        psAB = ps("psAB", [G2, BN])
        psT = ps("psT", [P, CH, G2])
        psG = ps("psG", [P, HEADS, TILES])
        small_in, par_in = sem("small_in"), sem("par_in")
        w_turned, w_copied = sem("w_turned"), sem("w_copied")
        ab_done, ab_copied, ab_turned, abt_copied = sem("ab_done"), sem("ab_copied"), sem("ab_turned"), sem("abt_copied")
        rstep = sem("rstep")
        vstep, astep, g_done, tab_done = sem("vstep"), sem("astep"), sem("g_done"), sem("tab_done")
        block = ctx.enter_context(nc.Block())
        NPAR = 7

        @block.sync
        def _(sp):
            sp.dma_start(cst[:, :], const_dram[:, 0:2 * P]).then_inc(small_in, 16)
            sp.dma_start(wab[0:HEADS, :], A["Wa"]).then_inc(small_in, 16)
            sp.dma_start(wab[HEADS:G2, :], A["Wb"]).then_inc(small_in, 16)
            sp.dma_start(alog[:, :], A["A_log"].partition_broadcast(P)).then_inc(small_in, 16)
            sp.dma_start(dtb[:, :], A["dt_bias"].partition_broadcast(P)).then_inc(small_in, 16)
            for j, n in enumerate(("k", "q", "v")):
                sp.dma_start(ptab[:, :, 4 * j:4 * j + 4], A["cw_" + n].rearrange("(h p) j -> p h j", p=P)).then_inc(par_in, 16)
                sp.dma_start(ptab[:, :, 12 + j], A["cb_" + n].rearrange("(h p) -> p h", p=P),
                             allow_slow_non_contiguous=True).then_inc(par_in, 16)
            sp.dma_start(ptab[:, :, PN], A["norm_w"].rearrange("(h p) -> p h", p=P),
                             allow_slow_non_contiguous=True).then_inc(par_in, 16)
            sp.wait_ge(par_in, 16 * NPAR)

        @block.tensor
        def _(pe):
            pe.wait_ge(small_in, 16 * 5)
            for k in range(KT):
                tr = pe.transpose(psW[:, k, :], wab[:, k * P:(k + 1) * P], cst[0:G2, 0:G2])
            tr.then_inc(w_turned, 1)
            pe.wait_ge(w_copied, 1)
            pe.sem_inc(abt_copied, 1)
            for b in range(B):
                for k in range(KT):
                    mm = pe.matmul(psAB[:, :], wabT[:, k, :], xnT[:, k, bass.ds(b * SEQ, SEQ)], start=(k == 0), stop=(k == KT - 1))
                mm.then_inc(ab_done, 1)
                pe.wait_ge(ab_copied, b + 1)
                pe.wait_ge(abt_copied, b + 1)
                for c in range(CH):
                    tr = pe.transpose(psT[:, c, :], ab[:, c * P:(c + 1) * P], cst[0:G2, 0:G2])
                tr.then_inc(ab_turned, 1)
            pe.wait_ge(tab_done, 1)
            pe.matmul(psG[:, :, :], cst[:, C_UP:C_UP + P], ptab[:, :, 16:32], start=True, stop=True).then_inc(g_done, 1)

        @block.scalar
        def _(act):
            act.wait_ge(small_in, 16 * 5)
            nc.scalar.activation(ea[:, :], alog[:, :], ACT.Exp).then_inc(astep, 1)
            act.wait_ge(vstep, 2)
            nc.scalar.activation(ez[:], az[:], ACT.Exp, scale=-1.0).then_inc(astep, 1)
            act.wait_ge(astep, 2)
            nc.scalar.activation(lz[:], ez[:], ACT.Ln, bias=1.0).then_inc(astep, 1)
            act.wait_ge(g_done, 1)
            nc.scalar.activation(gam[:], psG[:, :, :], ACT.Exp).then_inc(astep, 1)
            nc.scalar.activation(beta[:], abt[:, :, :, HEADS:G2], ACT.Sigmoid).then_inc(astep, 1)

        @block.vector
        def _(dve):
            nc.vector.memset(ptab[:, :, 15:16], 0.0)
            nc.vector.memset(ptab[:, :, PN + 1:PW], 0.0)
            dve.wait_ge(w_turned, 1)
            nc.vector.tensor_copy(wabT[:], psW[:, :, :]).then_inc(w_copied, 1)
            for b in range(B):
                dve.wait_ge(ab_done, b + 1)
                nc.vector.tensor_copy(ab[:, :], psAB[:, :]).then_inc(ab_copied, 1)
                dve.wait_ge(ab_turned, b + 1)
                nc.vector.tensor_copy(abt[:, bass.ds(b, 1), :, :].rearrange("p o c g -> p (o c) g"), psT[:, :, :]
                                      ).then_inc(abt_copied, 1)
            dve.wait_ge(abt_copied, B + 1)
            dve.wait_ge(small_in, 16 * 5)
            dt_all = dtb[:, :].unsqueeze(1).to_broadcast([P, B * CH, HEADS])
            flat = "p b c h -> p (b c) h"
            nc.vector.tensor_tensor(z[:].rearrange(flat), abt[:, :, :, 0:HEADS].rearrange(flat), dt_all, ALU.add).then_inc(vstep, 1)
            dve.wait_ge(vstep, 1)
            nc.vector.tensor_scalar(az[:], z[:], -1.0, None, ALU.mult).then_inc(rstep, 1)
            dve.wait_ge(rstep, 1)
            nc.vector.tensor_tensor(az[:], az[:], z[:], ALU.max).then_inc(vstep, 1)
            nc.vector.tensor_scalar(rz[:], z[:], 0.0, None, ALU.max).then_inc(rstep, 1)
            dve.wait_ge(astep, 3)
            dve.wait_ge(rstep, 2)
            nc.vector.tensor_tensor(rz[:], rz[:], lz[:], ALU.add).then_inc(rstep, 1)
            dve.wait_ge(rstep, 3)
            ea_all = ea[:, :].unsqueeze(1).to_broadcast([P, B * CH, HEADS])
            nc.vector.tensor_tensor(rz[:].rearrange(flat), rz[:].rearrange(flat), ea_all, ALU.mult).then_inc(rstep, 1)
            dve.wait_ge(rstep, 4)
            dve.wait_ge(par_in, 16 * NPAR)
            by_tok = "p h (c b) -> p b c h"
            for b in range(B):
                ts = nc.vector.tensor_scalar(ptab[:, :, 16:32].rearrange(by_tok, c=CH)[:, b], rz[:, b], -1.0, None, ALU.mult)
            ts.then_inc(tab_done, 1)
            dve.wait_ge(astep, 5)
            for b in range(B):
                nc.vector.tensor_copy(ptab[:, :, 32:48].rearrange(by_tok, c=CH)[:, b], beta[:, b]).then_inc(rstep, 1)
            dve.wait_ge(rstep, 4 + B)
            nc.vector.scalar_tensor_tensor(out=ptab[:, :, 48:64], in0=gam[:], scalar=-1.0, in1=ptab[:, :, 32:48],
                                           op0=ALU.mult, op1=ALU.mult).then_inc(vstep, 1)



def delta_heads(nc, xnT, A, const_dram, ptab, osq, og_dram):
    with ExitStack() as ctx:
        sem = semaphores(nc, ctx, "gd")

        def sb(n, s, d=F32):
            return ctx.enter_context(nc.sbuf_tensor(f"gd_{n}", s, d))

        cst = sb("cst", [P, C_W])
        ident, upper, later = cst[:, C_ID:C_ID + P], cst[:, C_UP:C_UP + P], cst[:, C_GT:C_GT + P]
        ones = cst[:, C_ONE:C_ONE + P]
        wraw = sb("wraw", [P, 4, DIM])
        wT = sb("wT", [P, 4, KT, P])
        cur_a = sb("cur_a", [P, PN])
        cur_w = sb("cur_w", [P, PW - PN])
        cur_lg = sb("cur_lg", [P, B])
        cur_beta = sb("cur_beta", [P, 2, B])
        pre = sb("pre", [P, 2, 3, B, 3 + P])
        conv = sb("conv", [P, 3, B, P])
        kT = sb("kT", [P, 2, BN])
        rawq = sb("rawq", [P, BN])
        qT = sb("qT", [P, BN])
        vT = sb("vT", [P, BN])
        gate = sb("gate", [P, 2, BN])
        sq = sb("sq", [P, 2, BN])
        root = sb("root", [P, 2, B])
        rn = sb("rn", [P, 2, B])
        rdiag = sb("rdiag", [P, B, P])
        brk = sb("brk", [P, 2, B])
        lgm = sb("lgm", [P, B, P])
        D = sb("D", [P, B, P])
        Dm = sb("Dm", [P, B, P])
        gbc = sb("gbc", [P, 2, B, P])
        AT = sb("AT", [P, B, P])
        PT = sb("PT", [P, B, P])
        Kd = sb("Kd", [P, B, P])
        Vb = sb("Vb", [P, B, P])
        Lo = sb("Lo", [P, B, P])
        T = sb("T", [P, B, P])
        W = sb("W", [P, B, P])
        Y = sb("Y", [P, NLV, B, P])
        R = sb("R", [P, B, P])
        U = sb("U", [P, B, P])
        S = sb("S", [P, B, P])
        qg = sb("qg", [P, B, P])
        o2 = sb("o2", [P, BN])
        og = sb("og", [P, 2, BN])
        PJ = ctx.enter_context(nc.psum_tensor("gd_PJ", [P, 2, BN], F32))
        Bk = [ctx.enter_context(nc.psum_tensor(f"gd_B{k}", [P, B, P], F32)) for k in range(6)]
        half = [Bk[k][:, 0:2, :].rearrange("p a (h c) -> p (a h) c", h=2) for k in range(6)]
        sums = Bk[5][:, 0, 0:2 * B].rearrange("p (j b) -> p j b", j=2)

        cst_in, w_in = sem("cst_in"), sem("w_in")
        og_out = [sem("og_out0"), sem("og_out1")]
        w_turned, w_copied = sem("w_turned"), sem("w_copied")
        projected, pre_done, tap_done, silu_done = (sem(x) for x in ("projected", "pre", "tap", "silu"))
        sq_done, sums_done, root_done, max_done, rnorm_done, brk_ready, diag_ready, spread_done, q_ready = (
            sem(x) for x in ("sq", "sums", "root", "max", "rnorm", "brk", "diag", "spread", "q"))
        head_a, head_b, decay_in, zeroed, halo_done, osq_zero = (
            sem(x) for x in ("head_a", "head_b", "decay_in", "zeroed", "halo", "osq_zero"))
        darg, garg, kk_done, kq_done, k_turned, v_turned, l_turned = (
            sem(x) for x in ("darg", "garg", "kk", "kq", "ktr", "vtr", "ltr"))
        d_exp, g_exp, d_cut, dm_ready, qg_ready, at_ready, pt_ready, kd_ready, vb_ready, l_ready = (
            sem(x) for x in ("dexp", "gexp", "dcut", "dm", "qg", "at", "pt", "kd", "vb", "l"))
        t_mask, t_ready, w2_turned, w_first = sem("tmask"), sem("t2"), sem("w2t"), sem("w2")
        y_sum, y_ready, wup, w_ready, tup, t_next = (sem(x) for x in ("ysum", "y", "wup", "w", "tup", "t"))
        ks_done, r_ready, u_sum, u_ready, o_sum, og_ready, o2_ready, osq_done, s_sum, s_ready = (
            sem(x) for x in ("ks", "r", "usum", "u", "osum", "og", "o2", "osq", "ssum", "s"))
        block = ctx.enter_context(nc.Block())
        LAST = HEADS - 1

        def heads(eng, slot):
            with eng.Fori(0, LAST) as i:
                for c in range(CH):
                    slot(i, c, True)
            for c in range(CH):
                slot(LAST, c, c < CH - 1)

        @block.sync
        def _(sp):
            def load_weights(i):
                for j, n in enumerate(("Wk", "Wq", "Wv", "Wg")):
                    sp.dma_start(wraw[:, j, :], A[n][bass.ds(i * P, P), :]).then_inc(w_in, 16)

            sp.dma_start(cst[:, :], const_dram).then_inc(cst_in, 16)
            load_weights(0)
            sp.wait_ge(w_turned, 4)
            load_weights(1)

            def store(i, c):
                n = i * CH + c
                sp.wait_ge(og_ready, n + 1)
                dst = og_dram[bass.ds(i * P, P), :].rearrange("p (b c t) -> p c b t", b=B, c=CH)[:, c]
                sp.dma_start(dst, og[:, c % 2, :].rearrange("p (b t) -> p b t", b=B)).then_inc(og_out[c % 2], 16)

            with sp.Fori(0, HEADS - 2) as i:
                for c in range(CH):
                    store(i, c)
                sp.wait_ge(w_turned, i * 4 + 8)
                load_weights(i + 2)
            for i in (HEADS - 2, HEADS - 1):
                for c in range(CH):
                    store(i, c)
            for s in range(2):
                sp.wait_ge(og_out[s], 16 + 8 * HEADS * CH)

        @block.tensor
        def _(pe):
            def turn_weights(h):
                pe.wait_ge(w_in, h * 64 + 64)
                for j in range(4):
                    if j >= 2:
                        pe.wait_ge(w_copied, h * 4 + j - 1)
                    for k in range(KT):
                        tr = pe.transpose(PJ[:, j % 2, k * P:(k + 1) * P], wraw[:, j, k * P:(k + 1) * P], ident)
                    tr.then_inc(w_turned, 1)

            def project(m, h, cm, lo, hi):
                for f in range(lo, hi):
                    j, k = f // KT, f % KT
                    if k == 0:
                        if cm == 0:
                            pe.wait_ge(w_copied, h * 4 + j + 1 if j >= 2 else h * 4 + 4)
                        if j >= 2:
                            pe.wait_ge(pre_done, m * 3 + j - 1)
                    rhs = xnT[:, k, :].rearrange("p (b c t) -> p c b t", b=B, c=CH)[:, cm]
                    mm = pe.matmul(PJ[:, j % 2, :].rearrange("p (b t) -> p b t", b=B), wT[:, j, k, :], rhs,
                                   start=(k == 0), stop=(k == KT - 1))
                    if k == KT - 1:
                        mm.then_inc(projected, 1)

            def chunk_decays(m):
                pe.wait_ge(decay_in, m + 1)
                for b in range(B):
                    mm = pe.matmul(Bk[1][:, b, :], lgm[:, b, :], upper, start=True, stop=True)
                mm.then_inc(darg, 1)

            def start_decays(m):
                for b in range(B):
                    mm = pe.matmul(Bk[5][:, b, :], cur_lg[:, b:b + 1].to_broadcast([P, P]), upper, start=True, stop=True)
                mm.then_inc(garg, 1)

            def key_sums(m):
                pe.wait_ge(sq_done, m * 2 + 2)
                pe.wait_ge(g_exp, m + 1)
                for j in range(2):
                    for b in range(B):
                        mm = pe.matmul(sums[:, j, b:b + 1], sq[:, j, b * P:(b + 1) * P], ones[:, 0:1], start=True, stop=True)
                mm.then_inc(sums_done, 1)

            def spread(m):
                pe.wait_ge(diag_ready, m + 1)
                pe.wait_ge(pre_done, m * 3 + 3)
                pe.matmul(PJ[:, 0, :], ones, rdiag[:], start=True, stop=True).then_inc(spread_done, 1)

            def key_products(k_c):
                for b in range(B):
                    mm = pe.matmul(Bk[2][:, b, :], k_c[b], k_c[b], start=True, stop=True)
                mm.then_inc(kk_done, 1)

            def turn_keys(k_c):
                for b in range(B):
                    tr = pe.transpose(Bk[4][:, b, :], k_c[b], ident)
                tr.then_inc(k_turned, 1)

            def query_products(m, k_c):
                pe.wait_ge(q_ready, m + 1)
                for b in range(B):
                    mm = pe.matmul(Bk[3][:, b, :], k_c[b], qT[:, b * P:(b + 1) * P], start=True, stop=True)
                mm.then_inc(kq_done, 1)

            def turn_products(m):
                pe.wait_ge(at_ready, m + 1)
                for b in range(B):
                    tr = pe.transpose(Bk[0][:, b, :], AT[:, b, :], ident)
                tr.then_inc(l_turned, 1)

            def keys(par):
                return [kT[:, par, b * P:(b + 1) * P] for b in range(B)]

            def slot(i, c, nxt):
                n = i * CH + c
                m, hm, cm, parm = n + 1, (i + 1 if c == CH - 1 else i), (c + 1) % CH, (c + 1) % 2
                k_c, k_m = keys(c % 2), keys(parm)

                def proj(lo, hi):
                    if nxt:
                        project(m, hm, cm, lo, hi)

                pe.wait_ge(silu_done, n * 4 + 4)
                pe.wait_ge(o2_ready, n + 1)
                for b in range(B):
                    tr = pe.transpose(Bk[5][:, b, :], vT[:, b * P:(b + 1) * P], ident)
                tr.then_inc(v_turned, 1)
                if nxt and c == CH - 1:
                    turn_weights(hm)
                proj(0, 2)
                pe.wait_ge(t_ready, n + 1)
                pe.wait_ge(s_ready, n + 1)
                for b in range(B):
                    tr = pe.transpose(Bk[1][:, b, :], T[:, b, :], ident)
                tr.then_inc(w2_turned, 1)
                pe.wait_ge(kd_ready, n + 1)
                if c > 0:
                    for b in range(B):
                        mm = pe.matmul(Bk[4][:, b, :], k_c[b], S[:, b, :], start=True, stop=True)
                    mm.then_inc(ks_done, 1)
                proj(2, 4)
                pe.wait_ge(w_first, n + 1)
                pe.wait_ge(pt_ready, n + 1)
                for l, s in enumerate(LEVELS):
                    if l > 0:
                        pe.wait_ge(w_ready, n * NLV + l)
                    for b in range(B):
                        mm = pe.matmul(half[2][:, b, :], Lo[:, b, :], second(W, s)[:, b], start=True, stop=True)
                    mm.then_inc(y_sum, 1)
                    for what in AHEAD[l][0]:
                        ahead(what, m, proj, nxt)
                    pe.wait_ge(y_ready, n * NLV + l + 1)
                    if l > 0:
                        pe.wait_ge(t_next, n * (NLV - 1) + l)
                    for b in range(B):
                        mm = pe.matmul(half[3][:, b, :], T[:, b, :], second(Y[:, l], s)[:, b], start=True, stop=True)
                    mm.then_inc(wup, 1)
                    if l < NLV - 1:
                        for b in range(B):
                            mm = pe.matmul(half[0][:, b, :], Y[:, l, b, :], first(T, s)[:, b], start=True, stop=True)
                        mm.then_inc(tup, 1)
                    for what in AHEAD[l][1]:
                        ahead(what, m, proj, nxt)
                if nxt:
                    key_products(k_m)
                if c > 0:
                    pe.wait_ge(r_ready, i * (CH - 1) + c)
                else:
                    pe.wait_ge(vb_ready, n + 1)
                if nxt:
                    turn_keys(k_m)
                    pe.wait_ge(d_exp, m + 1)
                pe.wait_ge(w_ready, n * NLV + NLV)
                for b in range(B):
                    mm = pe.matmul(Bk[1][:, b, :], W[:, b, :], (R if c > 0 else Vb)[:, b, :], start=True, stop=True)
                mm.then_inc(u_sum, 1)
                if nxt:
                    query_products(m, k_m)
                    turn_products(m)
                    pe.wait_ge(root_done, m + 1)
                else:
                    pe.wait_ge(vb_ready, n + 1)
                pe.wait_ge(qg_ready, n + 1)
                pe.wait_ge(u_ready, n + 1)
                for b in range(B):
                    if c > 0:
                        pe.matmul(Bk[5][:, b, :], S[:, b, :], qg[:, b, :], start=True, stop=False)
                    mm = pe.matmul(Bk[5][:, b, :], U[:, b, :], PT[:, b, :], start=(c == 0), stop=True)
                mm.then_inc(o_sum, 1)
                for b in range(B):
                    mm = pe.matmul(Bk[1][:, b, :], Kd[:, b, :], U[:, b, :], start=True, stop=True)
                mm.then_inc(s_sum, 1)

            AHEAD = [((4, 5), ("chunk",)), ((6,), ("start",)), ((7, 8), (9,)), ((10,), ("sums", 11)),
                     ((12, 13), (14,)), ((15,), ("spread",))]

            def ahead(what, m, proj, nxt):
                if not nxt:
                    return
                if what == "chunk":
                    chunk_decays(m)
                elif what == "start":
                    pe.wait_ge(vb_ready, m)
                    start_decays(m)
                elif what == "sums":
                    key_sums(m)
                elif what == "spread":
                    spread(m)
                else:
                    proj(what, what + 1)

            pe.wait_ge(cst_in, 16)
            turn_weights(0)
            chunk_decays(0)
            start_decays(0)
            project(0, 0, 0, 0, 16)
            key_sums(0)
            spread(0)
            key_products(keys(0))
            turn_keys(keys(0))
            query_products(0, keys(0))
            turn_products(0)
            heads(pe, slot)

        @block.vector
        def _(dve):
            def copy_weights(h):
                for j in range(4):
                    dve.wait_ge(w_turned, h * 4 + j + 1)
                    nc.vector.tensor_copy(wT[:, j].rearrange("p k n -> p (k n)"), PJ[:, j % 2, :]).then_inc(w_copied, 1)

            def taps(m, parm, j):
                dve.wait_ge(halo_done, m + 1)
                dve.wait_ge(pre_done, m * 3 + j + 1)
                for d in range(3):
                    if d > 0:
                        dve.wait_ge(tap_done, m * 9 + j * 3 + d)
                    nc.vector.scalar_tensor_tensor(out=conv[:, j], in0=pre[:, parm, j, :, d:d + P],
                                                   scalar=cur_a[:, 4 * j + d:4 * j + d + 1], in1=conv[:, j],
                                                   op0=ALU.mult, op1=ALU.add).then_inc(tap_done, 1)

            def inverse_norms(m, cm):
                dve.wait_ge(root_done, m + 1)
                nc.vector.tensor_scalar(root[:], root[:], 1e-12, None, ALU.max).then_inc(max_done, 1)
                dve.wait_ge(max_done, m + 1)
                nc.vector.reciprocal(rn[:], root[:]).then_inc(rnorm_done, 1)
                dve.wait_ge(rnorm_done, m + 1)
                for j in range(2):
                    tt = nc.vector.tensor_tensor(brk[:, j, :], cur_a[:, 32 + 16 * j + cm * B:32 + 16 * j + cm * B + B],
                                                 rn[:, 0, :], ALU.mult)
                tt.then_inc(brk_ready, 1)

            def level(n, l):
                s = LEVELS[l]
                dve.wait_ge(y_sum, n * NLV + l + 1)
                mask = cst[:, C_LV + 64 * l:C_LV + 64 * l + 64].rearrange("p (g m) -> p g m", m=s)
                ps = half[2].rearrange("p b (g m) -> p b g m", m=s)
                nc.vector.tensor_tensor(second(Y[:, l], s), ps, mask.unsqueeze(1).to_broadcast([P, B, 64 // s, s]),
                                        ALU.mult).then_inc(y_ready, 1)
                dve.wait_ge(wup, n * NLV + l + 1)
                nc.vector.tensor_tensor(second(W, s), second(W, s), half[3].rearrange("p b (g m) -> p b g m", m=s),
                                        ALU.add).then_inc(w_ready, 1)
                if l < NLV - 1:
                    dve.wait_ge(tup, n * (NLV - 1) + l + 1)
                    nc.vector.tensor_tensor(first(T, s), first(T, s), half[0].rearrange("p b (g m) -> p b g m", m=s),
                                            ALU.add).then_inc(t_next, 1)

            def decayed_products(m):
                dve.wait_ge(kk_done, m + 1)
                dve.wait_ge(dm_ready, m + 1)
                nc.vector.tensor_tensor(AT[:], Bk[2][:, :, :], Dm[:], ALU.mult).then_inc(at_ready, 1)

            def queries(m):
                dve.wait_ge(spread_done, m + 1)
                nc.vector.tensor_tensor(qT[:, :], rawq[:, :], PJ[:, 0, :], ALU.mult).then_inc(q_ready, 1)

            def first_inverse(m):
                dve.wait_ge(l_turned, m + 1)
                dve.wait_ge(brk_ready, m + 1)
                nc.vector.tensor_tensor(Lo[:], Bk[0][:, :, :], bc(brk[:, 0, :], P), ALU.mult).then_inc(l_ready, 1)
                dve.wait_ge(l_ready, m + 1)
                nc.vector.tensor_tensor(T[:], Lo[:], cst[:, C_M1:C_M1 + P].unsqueeze(1).to_broadcast([P, B, P]), ALU.mult).then_inc(t_mask, 1)
                dve.wait_ge(t_mask, m + 1)
                nc.vector.tensor_tensor(T[:], T[:], ident.unsqueeze(1).to_broadcast([P, B, P]), ALU.add).then_inc(t_ready, 1)

            def query_weights(m):
                dve.wait_ge(kq_done, m + 1)
                nc.vector.tensor_tensor(PT[:], Bk[3][:, :, :], Dm[:], ALU.mult).then_inc(pt_ready, 1)

            def decayed_keys(m):
                dve.wait_ge(k_turned, m + 1)
                nc.vector.tensor_tensor(Kd[:], Bk[4][:, :, :], bc(Dm[:, :, P - 1], P), ALU.mult).then_inc(kd_ready, 1)

            def slot(i, c, nxt):
                n = i * CH + c
                m, hm, cm, parm = n + 1, (i + 1 if c == CH - 1 else i), (c + 1) % CH, (c + 1) % 2
                if nxt and c == CH - 1:
                    copy_weights(hm)
                dve.wait_ge(w_first, n + 1)
                level(n, 0)
                if nxt:
                    taps(m, parm, 0)
                level(n, 1)
                level(n, 2)
                if nxt:
                    taps(m, parm, 1)
                if c > 0:
                    dve.wait_ge(vb_ready, n + 1)
                    dve.wait_ge(ks_done, i * (CH - 1) + c)
                    for b in range(B):
                        st = nc.vector.scalar_tensor_tensor(out=R[:, b, :], in0=Bk[4][:, b, :], scalar=brk[:, 1, b:b + 1],
                                                            in1=Vb[:, b, :], op0=ALU.mult, op1=ALU.add)
                    st.then_inc(r_ready, 1)
                level(n, 3)
                if nxt:
                    taps(m, parm, 2)
                level(n, 4)
                if nxt:
                    inverse_norms(m, cm)
                level(n, 5)
                if nxt:
                    dve.wait_ge(qg_ready, n + 1)
                    queries(m)
                    decayed_products(m)
                    first_inverse(m)
                dve.wait_ge(o_sum, n + 1)
                dve.wait_ge(head_b, i + 1)
                dve.wait_ge(og_out[c % 2], i * (8 * CH) + (c // 2) * 16 + 16)
                nc.vector.scalar_tensor_tensor(out=og[:, c % 2, :], in0=Bk[5][:, :, :].rearrange("p b t -> p (b t)"),
                                               scalar=cur_w[:, 0:1], in1=gate[:, c % 2, :],
                                               op0=ALU.mult, op1=ALU.mult).then_inc(og_ready, 1)
                if nxt:
                    query_weights(m)
                dve.wait_ge(s_sum, n + 1)
                if c > 0:
                    for b in range(B):
                        st = nc.vector.scalar_tensor_tensor(out=S[:, b, :], in0=S[:, b, :], scalar=gbc[:, c % 2, b, P - 1:P],
                                                            in1=Bk[1][:, b, :], op0=ALU.mult, op1=ALU.add)
                    st.then_inc(s_ready, 1)
                else:
                    nc.vector.tensor_copy(S[:], Bk[1][:, :, :]).then_inc(s_ready, 1)
                if nxt:
                    decayed_keys(m)

            nc.vector.memset(Y[:], 0.0).then_inc(zeroed, 1)
            dve.wait_ge(zeroed, 1)
            dve.sem_inc(s_ready, 1)
            for s in range(2):
                dve.sem_inc(og_out[s], 16)
            dve.wait_ge(cst_in, 16)
            copy_weights(0)
            for j in range(3):
                taps(0, 0, j)
            inverse_norms(0, 0)
            queries(0)
            decayed_products(0)
            first_inverse(0)
            query_weights(0)
            decayed_keys(0)
            heads(dve, slot)

        @block.scalar
        def _(act):
            def copy_pre(m, h, parm, cm, j):
                act.wait_ge(projected, m * 4 + j + 1)
                nc.scalar.copy(pre[:, parm, j, :, 3:3 + P], PJ[:, j % 2, :].rearrange("p (b t) -> p b t", b=B))
                if cm == 0:
                    act.wait_ge(head_a, h + 1)
                nc.scalar.activation(conv[:, j], PJ[:, j % 2, :].rearrange("p (b t) -> p b t", b=B), ACT.Identity,
                                     scale=cur_a[:, 4 * j + 3:4 * j + 4], bias=cur_a[:, 12 + j:13 + j]).then_inc(pre_done, 1)

            def silu(m, j, dst):
                act.wait_ge(tap_done, m * 9 + j * 3 + 3)
                nc.scalar.activation(dst, conv[:, j].rearrange("p b t -> p (b t)"), ACT.Silu).then_inc(silu_done, 1)

            def decays(m, parm):
                act.wait_ge(darg, m + 1)
                nc.scalar.activation(D[:], Bk[1][:, :, :], ACT.Exp).then_inc(d_exp, 1)
                act.wait_ge(garg, m + 1)
                nc.scalar.activation(gbc[:, parm], Bk[5][:, :, :], ACT.Exp).then_inc(g_exp, 1)

            def roots(m):
                act.wait_ge(sums_done, m + 1)
                nc.scalar.activation(root[:], sums, ACT.Sqrt).then_inc(root_done, 1)

            def gates(m, parm):
                act.wait_ge(projected, m * 4 + 4)
                nc.scalar.activation(gate[:, parm, :], PJ[:, 1, :], ACT.Silu).then_inc(silu_done, 1)

            def slot(i, c, nxt):
                n = i * CH + c
                m, hm, cm, parm = n + 1, (i + 1 if c == CH - 1 else i), (c + 1) % CH, (c + 1) % 2
                act.wait_ge(v_turned, n + 1)
                act.wait_ge(decay_in, n + 1)
                for b in range(B):
                    vb = nc.scalar.activation(Vb[:, b, :], Bk[5][:, b, :], ACT.Copy, scale=cur_beta[:, c % 2, b:b + 1])
                vb.then_inc(vb_ready, 1)
                act.wait_ge(w2_turned, n + 1)
                nc.scalar.copy(W[:], Bk[1][:, :, :]).then_inc(w_first, 1)
                if nxt:
                    copy_pre(m, hm, parm, cm, 0)
                    decays(m, parm)
                    silu(m, 0, kT[:, parm, :])
                    copy_pre(m, hm, parm, cm, 1)
                    silu(m, 1, rawq[:, :])
                    roots(m)
                    copy_pre(m, hm, parm, cm, 2)
                    silu(m, 2, vT[:, :])
                    gates(m, parm)
                act.wait_ge(u_sum, n + 1)
                nc.scalar.copy(U[:], Bk[1][:, :, :]).then_inc(u_ready, 1)
                act.wait_ge(og_ready, n + 1)
                nc.scalar.activation(o2[:, :], Bk[5][:, :, :].rearrange("p b t -> p (b t)"), ACT.Square).then_inc(o2_ready, 1)

            act.sem_inc(o2_ready, 1)
            act.wait_ge(halo_done, 1)
            decays(0, 0)
            for j in range(3):
                copy_pre(0, 0, 0, 0, j)
            silu(0, 0, kT[:, 0, :])
            silu(0, 1, rawq[:, :])
            silu(0, 2, vT[:, :])
            gates(0, 0)
            roots(0)
            heads(act, slot)

        @block.gpsimd
        def _(pool):
            def head_params(h):
                nc.gpsimd.tensor_copy(cur_a[:, :], ptab[:, bass.ds(h, 1), 0:PN].rearrange("p o n -> p (o n)")).then_inc(head_a, 1)
                pool.wait_ge(head_a, h + 1)

            def log_decays(parm, cm):
                cols = cur_a[:, 16 + cm * B:16 + cm * B + B]
                nc.gpsimd.tensor_tensor(lgm[:], bc(cols, P), later.unsqueeze(1).to_broadcast([P, B, P]), ALU.mult)
                nc.gpsimd.tensor_copy(cur_lg[:, :], cols)
                nc.gpsimd.tensor_copy(cur_beta[:, parm, :], cur_a[:, 32 + cm * B:32 + cm * B + B]).then_inc(decay_in, 1)

            def halo(parm, cm):
                nxt = pre[:, 1 - parm, :, :, 0:3]
                if cm == CH - 1:
                    nc.gpsimd.memset(nxt, 0.0).then_inc(halo_done, 1)
                else:
                    for j in range(3):
                        cp = nc.gpsimd.tensor_copy(pre[:, 1 - parm, j, :, 0:3], pre[:, parm, j, :, P:P + 3])
                    cp.then_inc(halo_done, 1)

            def square(m, j, src):
                pool.wait_ge(silu_done, m * 4 + j + 1)
                nc.gpsimd.tensor_tensor(sq[:, j, :], src, src, ALU.mult).then_inc(sq_done, 1)

            def next_step(m, parm, cm):
                square(m, 0, kT[:, parm, :])
                pool.wait_ge(d_exp, m + 1)
                nc.gpsimd.tensor_tensor(D[:], D[:], upper.unsqueeze(1).to_broadcast([P, B, P]), ALU.mult).then_inc(d_cut, 1)
                square(m, 1, rawq[:, :])
                pool.wait_ge(rnorm_done, m + 1)
                pool.wait_ge(d_cut, m + 1)
                nc.gpsimd.tensor_tensor(Dm[:], D[:], bc(rn[:, 0, :], P), ALU.mult).then_inc(dm_ready, 1)
                pool.wait_ge(pre_done, m * 3 + 3)
                nc.gpsimd.tensor_tensor(rdiag[:], ident.unsqueeze(1).to_broadcast([P, B, P]), bc(rn[:, 1, :], P),
                                        ALU.mult).then_inc(diag_ready, 1)
                halo(parm, cm)

            def slot(i, c, nxt):
                n = i * CH + c
                m, hm, cm, parm = n + 1, (i + 1 if c == CH - 1 else i), (c + 1) % CH, (c + 1) % 2
                pool.wait_ge(s_ready, n + 1)
                pool.wait_ge(q_ready, n + 1)
                pool.wait_ge(g_exp, n + 1)
                nc.gpsimd.tensor_tensor(qg[:], qT[:, :].rearrange("p (b t) -> p b t", b=B), gbc[:, c % 2], ALU.mult).then_inc(qg_ready, 1)
                if c == 0:
                    nc.gpsimd.tensor_copy(cur_w[:, :], ptab[:, bass.ds(i, 1), PN:PW].rearrange("p o n -> p (o n)")).then_inc(head_b, 1)
                if nxt:
                    if c == CH - 1:
                        head_params(hm)
                    log_decays(parm, cm)
                    pool.wait_ge(kd_ready, n + 1)
                    next_step(m, parm, cm)
                pool.wait_ge(o2_ready, n + 2)
                nc.gpsimd.tensor_tensor(osq[:, c, :], osq[:, c, :], o2[:, :], ALU.add).then_inc(osq_done, 1)

            nc.gpsimd.memset(osq[:], 0.0).then_inc(osq_zero, 1)
            nc.gpsimd.memset(pre[:, 0, :, :, 0:3], 0.0).then_inc(halo_done, 1)
            pool.wait_ge(osq_zero, 1)
            pool.wait_ge(cst_in, 16)
            head_params(0)
            log_decays(0, 0)
            next_step(0, 0, 0)
            heads(pool, slot)


def delta_out(nc, A, x_dram, const_dram, osq, og_dram, out_dram):
    with ExitStack() as ctx:
        sem = semaphores(nc, ctx, "go")

        def sb(n, s, d=F32):
            return ctx.enter_context(nc.sbuf_tensor(f"go_{n}", s, d))


        cst = sb("cst", [P, C_W])
        wo = sb("wo", [P, KT, HEADS * P])
        woT = sb("woT", [P, HEADS, DIM])
        ogt = sb("ogt", [P, 2, HEADS, P])
        xt = sb("xt", [P, 2, DIM])
        yt = sb("yt", [P, 2, DIM])
        eps = sb("eps", [P, 1])
        rs = sb("rs", [P, B, CH])
        psW = [ctx.enter_context(nc.psum_tensor(f"go_psW{k}", [P, DIM], F32)) for k in range(2)]
        psY = [ctx.enter_context(nc.psum_tensor(f"go_psY{k}", [P, DIM], F32)) for k in range(2)]
        psS = ctx.enter_context(nc.psum_tensor("go_psS", [P, B, CH], F32))
        cst_in, wo_in, eps_set = sem("cst_in"), sem("wo_in"), sem("eps_set")
        tile_in, tile_out = [sem("tile_in0"), sem("tile_in1")], [sem("tile_out0"), sem("tile_out1")]
        turned, copied, ssq_done, root_done, rs_ready = (sem(x) for x in ("turned", "copied", "ssq", "root", "rs"))
        y_sum, y_ready = sem("y_sum"), sem("y_ready")
        block = ctx.enter_context(nc.Block())
        og_tiles = og_dram.rearrange("(h p) t -> p h t", p=P)

        @block.sync
        def _(sp):
            sp.dma_start(cst[:, :], const_dram).then_inc(cst_in, 16)
            for j in range(KT):
                sp.dma_start(wo[:, j, :], A["Wo"][j * P:(j + 1) * P, :]).then_inc(wo_in, 16)
            sp.sem_inc(y_ready, 2)
            with sp.Fori(0, TILES // 2) as i:
                for s in range(2):
                    t = i * 2 + s
                    sp.wait_ge(y_ready, t + 1)
                    sp.dma_start(ogt[:, s], og_tiles[:, :, bass.ds(t * P, P)]).then_inc(tile_in[s], 16)
                    sp.dma_start(xt[:, s, :], x_dram[bass.ds(t * P, P), :]).then_inc(tile_in[s], 16)

        @block.tensor
        def _(pe):
            pe.wait_ge(cst_in, 16)
            for b in range(B):
                for c in range(CH):
                    mm = pe.matmul(psS[:, b, c:c + 1], osq[:, c, b * P:(b + 1) * P], cst[:, C_ONE:C_ONE + 1], start=True, stop=True)
            mm.then_inc(ssq_done, 1)
            pe.wait_ge(wo_in, 16 * KT)
            for h in range(HEADS):
                if h >= 2:
                    pe.wait_ge(copied, h - 1)
                for j in range(KT):
                    tr = pe.transpose(psW[h % 2][:, j * P:(j + 1) * P], wo[:, j, h * P:(h + 1) * P], cst[:, C_ID:C_ID + P])
                tr.then_inc(turned, 1)
            pe.wait_ge(copied, HEADS)
            with pe.Fori(0, TILES // 2) as i:
                for s in range(2):
                    t = i * 2 + s
                    pe.wait_ge(tile_in[s], i * 32 + 32)
                    pe.wait_ge(y_ready, t + 1)
                    for h in range(HEADS):
                        mm = pe.matmul(psY[s][:, :], ogt[:, s, h, :], woT[:, h, :], start=(h == 0), stop=(h == HEADS - 1))
                    mm.then_inc(y_sum, 1)

        @block.scalar
        def _(act):
            act.wait_ge(eps_set, 1)
            act.wait_ge(ssq_done, 1)
            nc.scalar.activation(rs[:], psS[:, :, :], ACT.Sqrt, bias=eps[:, 0:1], scale=1.0 / (HEADS * P)).then_inc(root_done, 1)
            for h in range(HEADS):
                act.wait_ge(turned, h + 1)
                nc.scalar.copy(woT[:, h, :], psW[h % 2][:, :]).then_inc(copied, 1)
            with act.Fori(0, TILES // 2) as i:
                for s in range(2):
                    t = i * 2 + s
                    act.wait_ge(y_ready, t + 3)
                    act.dma_start(out_dram[bass.ds(t * P, P), :], yt[:, s, :]).then_inc(tile_out[s], 16)
            for s in range(2):
                act.wait_ge(tile_out[s], 16 + 8 * TILES)

        @block.vector
        def _(dve):
            nc.vector.memset(eps[:, :], RMS_EPS).then_inc(eps_set, 1)
            dve.wait_ge(root_done, 1)
            nc.vector.reciprocal(rs[:], rs[:]).then_inc(rs_ready, 1)
            dve.wait_ge(rs_ready, 1)
            for s in range(2):
                dve.sem_inc(tile_out[s], 16)
            rs_flat = rs[:].rearrange("p b c -> p (b c)")
            with dve.Fori(0, TILES // 2) as i:
                for s in range(2):
                    t = i * 2 + s
                    dve.wait_ge(y_sum, t + 1)
                    dve.wait_ge(tile_out[s], i * 16 + 16)
                    nc.vector.scalar_tensor_tensor(out=yt[:, s, :], in0=psY[s][:, :], scalar=rs_flat[:, bass.ds(t, 1)],
                                                   in1=xt[:, s, :], op0=ALU.mult, op1=ALU.add).then_inc(y_ready, 1)


def stage_attn(nc, I, const_dram, og_dram, out_dram):
    A = {k[len("L0_attn_"):]: v for k, v in I.items() if k.startswith("L0_attn_")}
    with ExitStack() as ctx:
        osq = ctx.enter_context(nc.sbuf_tensor("osq", [P, CH, BN], F32))
        with ExitStack() as inner:
            xnT = inner.enter_context(nc.sbuf_tensor("xnT", [P, KT, TOK], F32))
            ptab = inner.enter_context(nc.sbuf_tensor("ptab", [P, HEADS, PW], F32))
            layernorm_transposed(nc, "la", I["x"], const_dram, xnT)
            delta_gates(nc, xnT, A, const_dram, ptab)
            delta_heads(nc, xnT, A, const_dram, ptab, osq, og_dram)
        delta_out(nc, A, I["x"], const_dram, osq, og_dram, out_dram)


XH, XD = 16, 32
KEYS = 256
KTL = KEYS // P
GR = DIM // P
GH = XH // GR
QMAX, PMAX, SMIN = 127.0, 255.0, 1e-8
LN_PMAX = 5.541263545158426


def cross_setup(nc, X, ctx_dram, x_dram, const_dram, xres, rstd, mean, wq, wp, kbd, vq, bqb, bpb):
    with ExitStack() as ctx:
        sem = semaphores(nc, ctx, "xs")

        def sb(n, s, d=F32):
            return ctx.enter_context(nc.sbuf_tensor(f"xs_{n}", s, d))


        cst = sb("cst", [P, C_W])
        ident = cst[:, C_ID:C_ID + P]
        identb = sb("identb", [P, P], BF16)
        cx = sb("cx", [P, KTL, DIM])
        cxT = sb("cxT", [P, KT, KEYS])
        wkv = sb("wkv", [P, KT, 2 * DIM])
        bkb = sb("bkb", [P, DIM])
        bvc = sb("bvc", [P, GR])
        stats = sb("stats", [P, TILES, 6])
        mv = sb("mv", [P, TILES, 2])
        eps = sb("eps", [P, 1])
        kf = sb("kf", [P, KTL, XH, XD])
        ks = sb("ks", [P, KTL, XH])
        kr = sb("kr", [P, KTL, XH])
        kT = sb("kT", [P, GR, KEYS])
        vT = sb("vT", [P, GR, KEYS])
        vi = sb("vi", [P, GR, KEYS], BF16)
        vs = sb("vs", [P, GR])
        vr = sb("vr", [P, GR])
        parts = [sb(f"part{k}", [P, GR, KEYS], BF16) for k in range(3)]
        bank = [ctx.enter_context(nc.psum_tensor(f"xs_b{k}", [P, DIM], F32)) for k in range(6)]
        bankv = [ctx.enter_context(nc.psum_tensor(f"xs_v{k}", [P, 2 * DIM], BF16)) for k in range(2)]
        cx_in, cst_in, w_in, x_in = sem("cx_in"), sem("cst_in"), sem("w_in"), sem("x_in")
        cx_turned, cxT_ready, k_sum, v_sum, ident_ready = (sem(x) for x in ("cxt", "cxT", "ksum", "vsum", "identb"))
        k_done, k_turned, v_done, v_turned = (sem(x) for x in ("kdone", "kturned", "vdone", "vturned"))
        step, stat, var_done, root, zeroed = (sem(x) for x in ("step", "stat", "var", "root", "zeroed"))
        block = ctx.enter_context(nc.Block())

        @block.sync
        def _(sp):
            sp.dma_start(cst[:, :], const_dram).then_inc(cst_in, 16)
            sp.dma_start(cx[:, :, :], ctx_dram.rearrange("(t p) d -> p t d", p=P)).then_inc(cx_in, 16)
            sp.dma_start(wkv[:, :, :], X["Wkv"].rearrange("(k p) n -> p k n", p=P)).then_inc(w_in, 16)
            sp.dma_start(bkb[:, :], X["bkv"][0:DIM].partition_broadcast(P)).then_inc(w_in, 16)
            sp.dma_start(bvc[:, :], X["bkv"][DIM:2 * DIM].rearrange("(g p) -> p g", p=P), allow_slow_non_contiguous=True).then_inc(w_in, 16)
            sp.dma_start(wp[:, :, :], X["Wp"].rearrange("(g p) n -> p g n", p=P)).then_inc(w_in, 16)
            sp.dma_start(wq[:, :, :], X["Wq"].rearrange("(k p) n -> p k n", p=P)).then_inc(w_in, 16)
            sp.dma_start(bqb[:, :], X["bq"].partition_broadcast(P)).then_inc(w_in, 16)
            sp.dma_start(bpb[:, :], X["bp"].partition_broadcast(P)).then_inc(w_in, 16)
            for b in range(B):
                sp.dma_start(xres[:, b * CH:(b + 1) * CH, :], x_dram[b * SEQ:(b + 1) * SEQ, :].rearrange("(t p) d -> p t d", p=P)).then_inc(x_in, 16)
            sp.wait_ge(w_in, 16 * 7)

        @block.tensor
        def _(pe):
            pe.wait_ge(cst_in, 16)
            pe.wait_ge(cx_in, 16)
            for k in range(KT):
                for t in range(KTL):
                    tr = pe.transpose(bank[k % 2][:, t * P:(t + 1) * P] if k < 2 else bank[k][:, t * P:(t + 1) * P],
                                      cx[:, t, k * P:(k + 1) * P], ident)
                tr.then_inc(cx_turned, 1)
            pe.wait_ge(w_in, 16 * 7)
            pe.wait_ge(cxT_ready, KT)
            for t in range(KTL):
                for k in range(KT):
                    mm = pe.matmul(bank[4 + t][:, :], cxT[:, k, t * P:(t + 1) * P], wkv[:, k, 0:DIM], start=(k == 0), stop=(k == KT - 1))
                mm.then_inc(k_sum, 1)
            for g in range(GR):
                for k in range(KT):
                    mm = pe.matmul(bank[g][:, 0:KEYS], wkv[:, k, DIM + g * P:DIM + (g + 1) * P], cxT[:, k, :], start=(k == 0), stop=(k == KT - 1))
                mm.then_inc(v_sum, 1)
            pe.wait_ge(k_done, 1)
            for g in range(GR):
                for t in range(KTL):
                    tr = pe.transpose(bank[4 + g // 2][:, (g % 2) * KEYS + t * P:(g % 2) * KEYS + (t + 1) * P],
                                      kf[:, t].rearrange("p h d -> p (h d)")[:, g * P:(g + 1) * P], ident)
            tr.then_inc(k_turned, 1)
            pe.wait_ge(v_done, 1)
            pe.wait_ge(ident_ready, 1)
            for t in range(KTL):
                for g in range(GR):
                    tr = pe.transpose(bankv[t][:, g * P:(g + 1) * P], vi[:, g, t * P:(t + 1) * P], identb[:, :])
            tr.then_inc(v_turned, 1)

        @block.scalar
        def _(act):
            for k in range(KT):
                act.wait_ge(cx_turned, k + 1)
                nc.scalar.copy(cxT[:, k, :], bank[k % 2 if k < 2 else k][:, 0:KEYS]).then_inc(cxT_ready, 1)
            act.wait_ge(var_done, TILES)
            nc.scalar.activation(rstd[:, :], mv[:, :, 1], ACT.Sqrt, bias=eps[:, 0:1]).then_inc(root, 1)

        @block.gpsimd
        def _(pool):
            for part in range(3):
                nc.gpsimd.memset(kbd[:, part], 0.0).then_inc(zeroed, 1)

        @block.vector
        def _(dve):
            n = [0]

            def then(ins):
                n[0] += 1
                ins.then_inc(step, 1)
                dve.wait_ge(step, n[0])

            nc.vector.memset(eps[:, :], LN_EPS)
            dve.wait_ge(cst_in, 16)
            nc.vector.tensor_copy(identb[:, :], ident).then_inc(ident_ready, 1)
            dve.wait_ge(k_sum, KTL)
            for t in range(KTL):
                then(nc.vector.tensor_tensor(kf[:, t].rearrange("p h d -> p (h d)"), bank[4 + t][:, :], bkb[:, :], ALU.add))
            then(nc.vector.tensor_reduce(ks[:], kf[:], AX.X, ALU.max, apply_absolute_value=True))
            then(nc.vector.tensor_scalar(ks[:], ks[:], 1.0 / QMAX, SMIN, ALU.mult, ALU.max))
            then(nc.vector.reciprocal(kr[:], ks[:]))
            def all_heads(a):
                return a.rearrange("p t h -> p (t h)").unsqueeze(2).to_broadcast([P, KTL * XH, XD])
            kflat = kf[:].rearrange("p t h d -> p (t h) d")
            then(nc.vector.tensor_tensor(kflat, kflat, all_heads(kr[:]), ALU.mult))
            then(nc.vector.tensor_scalar(kflat, kflat, MAGIC, MAGIC, ALU.add, ALU.subtract))
            then(nc.vector.tensor_tensor(kflat, kflat, all_heads(ks[:]), ALU.mult))
            dve.sem_inc(k_done, 1)
            for g in range(GR):
                dve.wait_ge(v_sum, g + 1)
                then(nc.vector.tensor_scalar(vT[:, g, :], bank[g][:, 0:KEYS], bvc[:, g:g + 1], None, ALU.add))
            then(nc.vector.tensor_reduce(vs[:, :], vT[:], AX.X, ALU.max, apply_absolute_value=True))
            then(nc.vector.tensor_scalar(vs[:, :], vs[:, :], 1.0 / QMAX, SMIN, ALU.mult, ALU.max))
            then(nc.vector.reciprocal(vr[:, :], vs[:, :]))
            then(nc.vector.tensor_tensor(vT[:], vT[:], bc(vr[:, :], KEYS), ALU.mult))
            then(nc.vector.tensor_scalar(vi[:], vT[:], MAGIC, MAGIC, ALU.add, ALU.subtract))
            dve.sem_inc(v_done, 1)
            for g in range(GR):
                nc.vector.tensor_scalar(wp[:, g, :], wp[:, g, :], vs[:, g:g + 1], None, ALU.mult)
            dve.wait_ge(k_turned, 1)
            for h in range(2):
                then(nc.vector.tensor_copy(kT[:, 2 * h:2 * h + 2, :], bank[4 + h][:, :].rearrange("p (g n) -> p g n", g=2)))
            dve.wait_ge(zeroed, 3)
            for part in range(3):
                then(nc.vector.tensor_copy(parts[part][:], kT[:]))
                if part < 2:
                    then(nc.vector.tensor_tensor(kT[:], kT[:], parts[part][:], ALU.subtract))
                for j in range(GH):
                    nc.vector.tensor_copy(kbd[j * XD:(j + 1) * XD, part, :, j * KEYS:(j + 1) * KEYS],
                                          parts[part][j * XD:(j + 1) * XD, :, :])
            dve.wait_ge(v_turned, 1)
            for t in range(KTL):
                nc.vector.tensor_copy(vq[:, t, :], bankv[t][:, 0:DIM])
            for b in range(B):
                dve.wait_ge(x_in, 16 * B)
                for t in range(b * CH, (b + 1) * CH):
                    then(nc.vector.bn_stats(stats[:, t, :], xres[:, t, :]))
                    nc.vector.bn_aggr(mv[:, t, :], stats[:, t, :]).then_inc(var_done, 1)
            dve.wait_ge(var_done, TILES)
            nc.vector.tensor_copy(mean[:, :], mv[:, :, 0])
            dve.wait_ge(root, 1)
            nc.vector.reciprocal(rstd[:, :], rstd[:, :])


def cross_tiles(nc, const_dram, xres, rstd, mean, wq, wp, kbd, vq, bqb, bpb, out_dram):
    with ExitStack() as ctx:
        sem = semaphores(nc, ctx, "xt")

        def sb(n, s, d=F32):
            return ctx.enter_context(nc.sbuf_tensor(f"xt_{n}", s, d))


        ident = sb("ident", [P, P])
        identb = sb("identb", [P, P], BF16)
        xt = sb("xt", [P, 2, DIM])
        xn = sb("xn", [P, DIM])
        xT = sb("xT", [P, KT, P])
        st = sb("st", [P, 2])
        qf = sb("qf", [P, XH, XD])
        am = sb("am", [P, XH])
        qr = sb("qr", [P, XH])
        qs = sb("qs", [P, 2, XH])
        qi = sb("qi", [P, DIM], BF16)
        qT = sb("qT", [P, 2, GR, P], BF16)
        mx = sb("mx", [P, 2, GH])
        nb = sb("nb", [P, 2, GH])
        E = sb("E", [P, 2, GH, KEYS])
        Pi = sb("Pi", [P, 2, GH * KEYS], BF16)
        PT = sb("PT", [P, 2, GH * KTL, P], BF16)
        sums = sb("sums", [P, 2, XH])
        rec = sb("rec", [P, XH])
        o = sb("o", [P, XH, XD])
        oT = sb("oT", [P, GR, P])
        y = sb("y", [P, 2, DIM])
        psS = [ctx.enter_context(nc.psum_tensor(f"xt_S{k}", [P, GH, KEYS], F32)) for k in range(2)]
        psP = ctx.enter_context(nc.psum_tensor("xt_P", [P, GH * KTL, P], BF16))
        psO = ctx.enter_context(nc.psum_tensor("xt_O", [P, XH, XD], F32))
        psT = ctx.enter_context(nc.psum_tensor("xt_T", [P, DIM], F32))
        psQ = ctx.enter_context(nc.psum_tensor("xt_Q", [P, DIM], F32))
        psTb = psT[:, :].bitcast(BF16)
        ident_in, ident_ready, out_done = sem("ident_in"), sem("identb"), [sem("out0"), sem("out1")]
        tile_ready, xn_ready, x_turned, xT_ready, q_sum, qf_ready, am_ready, qs_ready, qr_ready, qn_ready, qi_ready, q_turned, qT_ready = (
            sem(x) for x in ("tile", "xn", "xtr", "xT", "qsum", "qf", "am", "qs", "qr", "qn", "qi", "qtr", "qT"))
        s_sum, mx_ready, nm_ready, nb_ready, exp_done, p_ready, p_turned, pT_ready, pv_sum = (
            sem(x) for x in ("ssum", "mx", "nm", "nb", "exp", "p", "ptr", "pT", "pv"))
        rec_ready, o_ready, o_turned, oT_ready, y_sum, bias_ready, y_ready, st_ready = (
            sem(x) for x in ("rec", "o", "otr", "oT", "ysum", "bias", "y", "st"))
        block = ctx.enter_context(nc.Block())
        SCALE = 1.0 / XD ** 0.5

        def tiles(eng, slot):
            with eng.Fori(0, TILES // 2 - 1) as i:
                for s in range(2):
                    slot(i * 2 + s, i, s, True)
            slot(TILES - 2, TILES // 2 - 1, 0, True)
            slot(TILES - 1, TILES // 2 - 1, 1, False)

        @block.sync
        def _(sp):
            sp.dma_start(ident[:, :], const_dram[:, C_ID:C_ID + P]).then_inc(ident_in, 16)

            def slot(t, i, s, nxt):
                sp.wait_ge(y_ready, t + 2)
                sp.dma_start(out_dram[bass.ds(t * P, P), :], y[:, s, :]).then_inc(out_done[s], 16)

            tiles(sp, slot)
            for s in range(2):
                sp.wait_ge(out_done[s], 16 + 8 * TILES)

        @block.gpsimd
        def _(pool):
            def fetch(t, par):
                nc.gpsimd.tensor_tensor(xt[:, par, :], xres[:, bass.ds(t, 1), :].rearrange("p o d -> p (o d)"), bpb[:, :], ALU.add).then_inc(bias_ready, 1)

            def slot(t, i, s, nxt):
                if nxt:
                    pool.wait_ge(y_ready, t + 1)
                    fetch(t + 1, 1 - s)

            pool.wait_ge(ident_in, 16)
            fetch(0, 0)
            tiles(pool, slot)

        @block.tensor
        def _(pe):
            def turn_x(t):
                pe.wait_ge(xn_ready, t + 1)
                for k in range(KT):
                    tr = pe.transpose(psT[:, k * P:(k + 1) * P], xn[:, k * P:(k + 1) * P], ident[:, :])
                tr.then_inc(x_turned, 1)

            def queries(t):
                pe.wait_ge(xT_ready, t + 1)
                for k in range(KT):
                    mm = pe.matmul(psQ[:, :], xT[:, k, :], wq[:, k, :], start=(k == 0), stop=(k == KT - 1))
                mm.then_inc(q_sum, 1)

            def turn_q(t):
                pe.wait_ge(qi_ready, t + 1)
                for g in range(GR):
                    tr = pe.transpose(psTb[:, g * P:(g + 1) * P], qi[:, g * P:(g + 1) * P], identb[:, :])
                tr.then_inc(q_turned, 1)

            def scores(t, par, g):
                for half in range(2):
                    cols = slice(half * DIM, (half + 1) * DIM)
                    for part in range(3):
                        mm = pe.matmul(psS[g % 2][:, :, :].rearrange("p h n -> p (h n)")[:, cols], qT[:, par, g, :],
                                       kbd[:, part, g, cols], start=(part == 0), stop=(part == 2))
                mm.then_inc(s_sum, 1)

            def turn_p(t, g):
                pe.wait_ge(p_ready, t * GR + g + 1)
                pe.wait_ge(pT_ready, t * GR + g + 1)
                for c in range(GH * KTL):
                    tr = pe.transpose(psP[:, c, :], Pi[:, g % 2, c * P:(c + 1) * P], identb[:, :])
                tr.then_inc(p_turned, 1)

            def values(t, g):
                pe.wait_ge(pT_ready, t * GR + g + 2)
                for j in range(GH):
                    h = g * GH + j
                    for k in range(KTL):
                        mm = pe.matmul(psO[:, h, :], PT[:, g % 2, j * KTL + k, :], vq[:, k, h * XD:(h + 1) * XD],
                                       start=(k == 0), stop=(k == KTL - 1))
                mm.then_inc(pv_sum, 1)

            def slot(t, i, s, nxt):
                pe.wait_ge(qT_ready, t + 1)
                for g in range(2):
                    scores(t, s, g)
                if nxt:
                    turn_x(t + 1)
                turn_p(t, 0)
                if nxt:
                    queries(t + 1)
                pe.wait_ge(o_ready, t + 1)
                values(t, 0)
                for g in range(1, GR):
                    if g + 1 < GR:
                        pe.wait_ge(exp_done, t * GR + g)
                        scores(t, s, g + 1)
                    turn_p(t, g)
                    values(t, g)
                    if g == 1 and nxt:
                        turn_q(t + 1)
                pe.wait_ge(o_ready, t + 2)
                if nxt:
                    pe.wait_ge(qT_ready, t + 2)
                for g in range(GR):
                    tr = pe.transpose(psT[:, g * P:(g + 1) * P], o[:].rearrange("p h d -> p (h d)")[:, g * P:(g + 1) * P], ident[:, :])
                tr.then_inc(o_turned, 1)
                pe.wait_ge(oT_ready, t + 1)
                if nxt:
                    pe.wait_ge(qf_ready, t + 2)
                for g in range(GR):
                    mm = pe.matmul(psQ[:, :], oT[:, g, :], wp[:, g, :], start=(g == 0), stop=(g == GR - 1))
                mm.then_inc(y_sum, 1)

            pe.wait_ge(ident_in, 16)
            pe.wait_ge(ident_ready, 1)
            turn_x(0)
            queries(0)
            turn_q(0)
            tiles(pe, slot)

        @block.scalar
        def _(act):
            def copy_xT(t):
                act.wait_ge(x_turned, t + 1)
                nc.scalar.copy(xT[:].rearrange("p k n -> p (k n)"), psT[:, :]).then_inc(xT_ready, 1)

            def copy_qT(t, par):
                act.wait_ge(q_turned, t + 1)
                nc.scalar.copy(qT[:, par].rearrange("p g n -> p (g n)"), psTb[:, 0:DIM]).then_inc(qT_ready, 1)

            def exps(t, s, g):
                act.wait_ge(nb_ready, t * GR + g + 1)
                for j in range(GH):
                    h = g * GH + j
                    ex = nc.scalar.activation(E[:, g % 2, j, :], psS[g % 2][:, j, :], ACT.Exp, scale=qs[:, s, h:h + 1],
                                              bias=nb[:, g % 2, j:j + 1], accum_out=sums[:, s, h:h + 1])
                ex.then_inc(exp_done, 1)

            def slot(t, i, s, nxt):
                exps(t, s, 0)
                if nxt:
                    copy_xT(t + 1)
                exps(t, s, 1)
                exps(t, s, 2)
                if nxt:
                    copy_qT(t + 1, 1 - s)
                exps(t, s, 3)
                act.wait_ge(o_turned, t + 1)
                nc.scalar.copy(oT[:].rearrange("p g n -> p (g n)"), psT[:, :]).then_inc(oT_ready, 1)

            copy_xT(0)
            copy_qT(0, 0)
            tiles(act, slot)

        @block.vector
        def _(dve):
            def normalise(t):
                nc.vector.tensor_copy(st[:, 0:1], mean[:, bass.ds(t, 1)])
                nc.vector.tensor_copy(st[:, 1:2], rstd[:, bass.ds(t, 1)]).then_inc(st_ready, 1)
                dve.wait_ge(st_ready, t + 1)
                nc.vector.tensor_scalar(xn[:, :], xres[:, bass.ds(t, 1), :].rearrange("p o d -> p (o d)"), st[:, 0:1], st[:, 1:2],
                                        ALU.subtract, ALU.mult).then_inc(xn_ready, 1)

            def quantise(t, par):
                dve.wait_ge(q_sum, t + 1)
                nc.vector.tensor_tensor(qf[:].rearrange("p h d -> p (h d)"), psQ[:, :], bqb[:, :], ALU.add).then_inc(qf_ready, 1)
                dve.wait_ge(qf_ready, t + 1)
                nc.vector.tensor_reduce(am[:, :], qf[:], AX.X, ALU.max, apply_absolute_value=True).then_inc(am_ready, 1)
                dve.wait_ge(am_ready, t + 1)
                nc.vector.tensor_scalar(qs[:, par, :], am[:, :], SCALE / QMAX, SMIN, ALU.mult, ALU.max).then_inc(qs_ready, 1)
                dve.wait_ge(qs_ready, t + 1)
                nc.vector.reciprocal(qr[:, :], qs[:, par, :]).then_inc(qr_ready, 1)
                dve.wait_ge(qr_ready, t + 1)
                nc.vector.tensor_tensor(qf[:], qf[:], bc(qr[:, :], XD), ALU.mult).then_inc(qn_ready, 1)
                dve.wait_ge(qn_ready, t * 2 + 1)
                nc.vector.tensor_scalar(qf[:], qf[:], SCALE, MAGIC, ALU.mult, ALU.add).then_inc(qn_ready, 1)
                dve.wait_ge(qn_ready, t * 2 + 2)
                nc.vector.tensor_scalar(qi[:, :], qf[:].rearrange("p h d -> p (h d)"), MAGIC, None, ALU.subtract).then_inc(qi_ready, 1)

            def maxima(t, s, g):
                dve.wait_ge(s_sum, t * GR + g + 1)
                nc.vector.tensor_reduce(mx[:, g % 2, :], psS[g % 2][:, :, :], AX.X, ALU.max).then_inc(mx_ready, 1)
                dve.wait_ge(mx_ready, t * GR + g + 1)
                nc.vector.scalar_tensor_tensor(out=nb[:, g % 2, :], in0=mx[:, g % 2, :], scalar=-1.0,
                                               in1=qs[:, s, g * GH:(g + 1) * GH], op0=ALU.mult, op1=ALU.mult).then_inc(nm_ready, 1)
                dve.wait_ge(nm_ready, t * GR + g + 1)
                nc.vector.tensor_scalar(nb[:, g % 2, :], nb[:, g % 2, :], LN_PMAX, None, ALU.add).then_inc(nb_ready, 1)

            def integers(t, g):
                dve.wait_ge(exp_done, t * GR + g + 1)
                nc.vector.tensor_scalar(Pi[:, g % 2, :], E[:, g % 2].rearrange("p h n -> p (h n)"), MAGIC, MAGIC,
                                        ALU.add, ALU.subtract).then_inc(p_ready, 1)

            def copy_p(t, g):
                dve.wait_ge(p_turned, t * GR + g + 1)
                nc.vector.tensor_copy(PT[:, g % 2], psP[:, :, :]).then_inc(pT_ready, 1)

            def slot(t, i, s, nxt):
                maxima(t, s, 0)
                if nxt:
                    normalise(t + 1)
                maxima(t, s, 1)
                integers(t, 0)
                copy_p(t, 0)
                integers(t, 1)
                if nxt:
                    quantise(t + 1, 1 - s)
                maxima(t, s, 2)
                copy_p(t, 1)
                integers(t, 2)
                maxima(t, s, 3)
                copy_p(t, 2)
                integers(t, 3)
                nc.vector.reciprocal(rec[:, :], sums[:, s, :]).then_inc(rec_ready, 1)
                dve.wait_ge(rec_ready, t + 1)
                copy_p(t, 3)
                dve.wait_ge(pv_sum, t * GR + GR)
                nc.vector.tensor_tensor(o[:], psO[:, :, :], bc(rec[:, :], XD), ALU.mult).then_inc(o_ready, 1)
                dve.wait_ge(y_sum, t + 1)
                dve.wait_ge(bias_ready, t + 1)
                dve.wait_ge(out_done[s], i * 16 + 16)
                nc.vector.tensor_tensor(y[:, s, :], psQ[:, :], xt[:, s, :], ALU.add).then_inc(y_ready, 1)

            dve.sem_inc(pT_ready, 1)
            dve.sem_inc(o_ready, 1)
            dve.sem_inc(y_ready, 1)
            for s in range(2):
                dve.sem_inc(out_done[s], 16)
            dve.wait_ge(ident_in, 16)
            nc.vector.tensor_copy(identb[:, :], ident[:, :]).then_inc(ident_ready, 1)
            normalise(0)
            quantise(0, 0)
            tiles(dve, slot)


def stage_xattn(nc, I, x_dram, const_dram, out_dram):
    X = {k[len("L0_xattn_"):]: v for k, v in I.items() if k.startswith("L0_xattn_")}
    with ExitStack() as ctx:
        def sb(n, s, d=F32):
            return ctx.enter_context(nc.sbuf_tensor(f"x_{n}", s, d))

        xres, rstd, mean = sb("xres", [P, TILES, DIM]), sb("rstd", [P, TILES]), sb("mean", [P, TILES])
        wq, wp = sb("wq", [P, KT, DIM]), sb("wp", [P, GR, DIM])
        kbd = sb("kbd", [P, 3, GR, GH * KEYS], BF16)
        vq = sb("vq", [P, KTL, DIM], BF16)
        bqb, bpb = sb("bqb", [P, DIM]), sb("bpb", [P, DIM])
        cross_setup(nc, X, I["ctx_2048"], x_dram, const_dram, xres, rstd, mean, wq, wp, kbd, vq, bqb, bpb)
        cross_tiles(nc, const_dram, xres, rstd, mean, wq, wp, kbd, vq, bqb, bpb, out_dram)


DH = 128
KV = 4
REP = HEADS // KV
ROT = 64
QN = HEADS * DH // DIM
RT = QN + 1
EXPERTS, INNER = 8, 256
IT = INNER // P
E_AT = [P * i * (i + 1) // 2 for i in range(CH)]
E_W = P * CH * (CH + 1) // 2
PT_AT = [0, 4 * P, 8 * P, 7 * P]
S_BANKS = [(0, [(3, 0)]), (1, [(2, 0), (0, 3 * P)]), (2, [(1, 0)])]
P_BANKS = [(3, [0]), (4, [1, 3]), (5, [2])]


def self_setup(nc, F, x_dram, const_dram, stat, wq, wk, wv, wo, qnw, knw):
    with ExitStack() as ctx:
        sem = semaphores(nc, ctx, "ss")

        def sb(n, s, d=F32):
            return ctx.enter_context(nc.sbuf_tensor(f"ss_{n}", s, d))


        xt = sb("xt", [P, CH, DIM])
        bns = sb("bns", [P, TILES, 6])
        mv = sb("mv", [P, TILES, 2])
        ln1 = sb("ln1", [P, KT])
        eps = sb("eps", [P, 2])
        ms = sb("ms", [P, TILES])
        w_in, wo_in, x_in, bn_done, var_done, step, root, eps_set = (
            sem(x) for x in ("w_in", "wo_in", "x_in", "bn", "var", "step", "root", "eps"))
        block = ctx.enter_context(nc.Block())

        @block.sync
        def _(sp):
            for b in range(B):
                if b > 0:
                    sp.wait_ge(bn_done, b * CH)
                sp.dma_start(xt[:, :, :], x_dram[b * SEQ:(b + 1) * SEQ, :].rearrange("(t p) d -> p t d", p=P)).then_inc(x_in, 16)
            sp.wait_ge(w_in, 16 * 6)
            sp.wait_ge(wo_in, 16)

        @block.scalar
        def _(act):
            act.dma_start(wq[:, :, :], F["wq"].rearrange("(k p) n -> p k n", p=P)).then_inc(w_in, 16)
            act.dma_start(wk[:, :, :], F["wk"].rearrange("(k p) n -> p k n", p=P)).then_inc(w_in, 16)
            act.dma_start(wv[:, :, :], F["wv"].rearrange("(k p) n -> p k n", p=P)).then_inc(w_in, 16)
            act.dma_start(ln1[:, :], F["ln1_w"].rearrange("(k p) -> p k", p=P), allow_slow_non_contiguous=True).then_inc(w_in, 16)
            act.dma_start(qnw[:, :], F["qnorm_w"].partition_broadcast(P)).then_inc(w_in, 16)
            act.dma_start(knw[:, :], F["knorm_w"].partition_broadcast(P)).then_inc(w_in, 16)
            act.dma_start(wo[:, :, :], F["wo"].rearrange("(h p) n -> p h n", p=P)).then_inc(wo_in, 16)
            act.wait_ge(eps_set, 1)
            act.wait_ge(var_done, TILES)
            nc.scalar.activation(stat[:, 1, :], mv[:, :, 1], ACT.Sqrt, bias=eps[:, 0:1]).then_inc(root, 1)
            act.wait_ge(step, 3)
            nc.scalar.activation(ms[:, :], ms[:, :], ACT.Sqrt, bias=eps[:, 1:2]).then_inc(root, 1)

        @block.vector
        def _(dve):
            nc.vector.memset(eps[:, 0:1], LN_EPS)
            nc.vector.memset(eps[:, 1:2], RMS_EPS).then_inc(eps_set, 1)
            for b in range(B):
                dve.wait_ge(x_in, 16 * (b + 1))
                for t in range(CH):
                    nc.vector.bn_stats(bns[:, b * CH + t, :], xt[:, t, :]).then_inc(bn_done, 1)
                for t in range(b * CH, (b + 1) * CH):
                    dve.wait_ge(bn_done, t + 1)
                    nc.vector.bn_aggr(mv[:, t, :], bns[:, t, :]).then_inc(var_done, 1)
            dve.wait_ge(var_done, TILES)
            nc.vector.tensor_copy(stat[:, 0, :], mv[:, :, 0])
            dve.wait_ge(root, 1)
            nc.vector.reciprocal(stat[:, 1, :], stat[:, 1, :]).then_inc(step, 1)
            dve.wait_ge(step, 1)
            nc.vector.tensor_tensor(ms[:, :], stat[:, 1, :], stat[:, 1, :], ALU.mult).then_inc(step, 1)
            dve.wait_ge(step, 2)
            nc.vector.tensor_tensor(ms[:, :], ms[:, :], mv[:, :, 1], ALU.mult).then_inc(step, 1)
            dve.wait_ge(root, 2)
            nc.vector.reciprocal(stat[:, 2, :], ms[:, :])
            dve.wait_ge(w_in, 16 * 6)
            for w in (wq, wk, wv):
                for k in range(KT):
                    nc.vector.tensor_scalar(w[:, k, :], w[:, k, :], ln1[:, k:k + 1], None, ALU.mult)


def self_attention(nc, x_dram, const_dram, rope_dram, stat, wq, wk, wv, wo, qnw, knw, x1_dram):
    turns = [("h", 0, 0), ("h", 1, 0)]
    for i in range(CH):
        if i >= 1:
            turns += [("h", i + 1, 0)] * (i + 1 < CH) + [("q", i - 1, r) for r in range(RT)]
    turns += [("q", CH - 1, r) for r in range(RT)]
    at = {x: n for n, x in enumerate(turns)}
    NT = len(turns)
    with ExitStack() as ctx:
        sem = semaphores(nc, ctx, "sa")

        def sb(n, s, d=F32):
            return ctx.enter_context(nc.sbuf_tensor(f"sa_{n}", s, d))


        ident = sb("ident", [P, P])
        neg = sb("neg", [P, P])
        identb = sb("identb", [P, P], BF16)
        negb = sb("negb", [P, P], BF16)
        rope = sb("rope", [P, CH, 2, ROT])
        st = sb("st", [P, 3, CH])
        xt = sb("xt", [P, CH, DIM])
        hn = sb("hn", [P, 2, DIM])
        hT = sb("hT", [P, 2, KT, P])
        ssq = sb("ssq", [P, RT])
        qss = sb("qss", [P, 1])
        rq = sb("rq", [P, 2])
        sqo = sb("sqo", [P, DIM])
        qk = sb("qk", [P, HEADS + KV, DH])
        sw = sb("sw", [P, HEADS + KV, ROT])
        qT = sb("qT", [P, HEADS, SEQ])
        kT = sb("kT", [P, KV, SEQ])
        v = sb("v", [P, CH, KV * DH])
        nmax = sb("nmax", [P, 2, CH])
        E = sb("E", [P, 2, E_W])
        sums = sb("sums", [P, 2, CH])
        rec = sb("rec", [P, CH])
        PT = sb("PT", [P, E_W])
        x1 = sb("x1", [P, 2, DIM])
        eps = sb("eps", [P, 2])
        Bk = [ctx.enter_context(nc.psum_tensor(f"sa_B{k}", [P, DIM], F32)) for k in range(8)]
        cst_in, cst_ready, x_in = sem("cst_in"), sem("cst"), sem("x_in")
        x1_out = [sem("x1_out0"), sem("x1_out1")]
        st_ready, xn_ready, h_ready, turned, turn_copied = (sem(x) for x in ("st", "xn", "h", "turned", "turncp"))
        q_sum, k_sum, v_sum, sq_done, ss_ready, root, rq_ready, qw_ready, v_ready = (
            sem(x) for x in ("qsum", "ksum", "vsum", "sq", "ss", "root", "rq", "qw", "v"))
        swapped, cosined, rotated = sem("swapped"), sem("cosined"), sem("rotated")
        s_sum, nmax_ready, exp_done, rec_ready, e_ready, p_turned, pt_ready, o_sum, o_ready = (
            sem(x) for x in ("ssum", "nmax", "exp", "rec", "e", "ptr", "pt", "osum", "o"))
        y_sum, x1_ready = sem("ysum"), sem("x1")
        block = ctx.enter_context(nc.Block())

        @block.sync
        def _(sp):
            sp.dma_start(ident[:, :], const_dram[:, C_ID:C_ID + P]).then_inc(cst_in, 16)
            sp.dma_start(neg[:, :], const_dram[:, C_NEG:C_NEG + P]).then_inc(cst_in, 16)
            sp.dma_start(rope[:, :, :, :], rope_dram.rearrange("(t p) a n -> p t a n", p=P)).then_inc(cst_in, 16)
            with sp.Fori(0, B) as b:
                sp.wait_ge(x1_ready, b * CH + CH)
                sp.dma_start(xt[:, :, :], x_dram[bass.ds(b * SEQ, SEQ), :].rearrange("(t p) d -> p t d", p=P)).then_inc(x_in, 16)
                for i in range(CH):
                    sp.wait_ge(x1_ready, b * CH + i + 1 + CH)
                    sp.dma_start(x1_dram[bass.ds(b * SEQ + i * P, P), :], x1[:, i % 2, :]).then_inc(x1_out[i % 2], 16)
            for s in range(2):
                sp.wait_ge(x1_out[s], 16 + 8 * TILES)

        @block.tensor
        def _(pe):
            def bank_of_turn(b, n):
                pe.wait_ge(turn_copied, b * NT + n + 1)
                return Bk[6 + n % 2]

            def turn_h(b, i):
                n = at["h", i, 0]
                pe.wait_ge(h_ready, b * CH + i + 1)
                bank = bank_of_turn(b, n)
                for k in range(KT):
                    tr = pe.transpose(bank[:, k * P:(k + 1) * P], hn[:, i % 2, k * P:(k + 1) * P], ident[:, :])
                tr.then_inc(turned, 1)

            def turn_qk(b, i):
                pe.wait_ge(rotated, b * CH + i + 1)
                for r in range(RT):
                    bank = bank_of_turn(b, at["q", i, r])
                    for j in range(REP):
                        tr = pe.transpose(bank[:, j * P:(j + 1) * P], qk[:, r * REP + j, :], ident[:, :])
                    tr.then_inc(turned, 1)

            def project(bank, i, w):
                for k in range(KT):
                    mm = pe.matmul(bank[:, :], hT[:, i % 2, k, :], w[:, k], start=(k == 0), stop=(k == KT - 1))
                return mm

            def scores(n, h):
                for r, (bank, tiles) in enumerate(S_BANKS):
                    pe.wait_ge(exp_done, n * 3 + r + 1)
                    for i, col in tiles:
                        w = (i + 1) * P
                        pe.matmul(Bk[bank][:, col:col + w], qT[:, h, i * P:(i + 1) * P], kT[:, h // REP, 0:w], start=True, stop=False)
                        mm = pe.matmul(Bk[bank][:, col + i * P:col + w], identb[:, :], negb[:, :], start=False, stop=True)
                    mm.then_inc(s_sum, 1)

            def turn_p(n, par):
                pe.wait_ge(e_ready, n + 1)
                for r, (bank, keys) in enumerate(P_BANKS):
                    pe.wait_ge(pt_ready, n * 3 + r + 1)
                    for kk in keys:
                        col = PT_AT[kk] - PT_AT[keys[0]]
                        for i in range(kk, CH):
                            tr = pe.transpose(Bk[bank][:, col + (i - kk) * P:col + (i - kk + 1) * P],
                                              E[:, par, E_AT[i] + kk * P:E_AT[i] + (kk + 1) * P], ident[:, :])
                    tr.then_inc(p_turned, 1)

            def values(n, h):
                pe.wait_ge(pt_ready, n * 3 + 6)
                pe.wait_ge(o_ready, n + 1)
                kv = h // REP
                for kk in range(CH):
                    w = (CH - kk) * P
                    mm = pe.matmul(Bk[6 + h % 2][:, kk * P:SEQ], v[:, kk, kv * DH:(kv + 1) * DH], PT[:, PT_AT[kk]:PT_AT[kk] + w],
                                   start=(kk == 0), stop=(kk == CH - 1), skip_group_check=True)
                mm.then_inc(o_sum, 1)

            pe.wait_ge(cst_in, 48)
            pe.wait_ge(cst_ready, 1)
            with pe.Fori(0, B) as b:
                turn_h(b, 0)
                turn_h(b, 1)
                for i in range(CH):
                    pe.wait_ge(turn_copied, b * NT + at["h", i, 0] + 3)
                    pe.wait_ge(x1_ready, b * CH + CH)
                    pe.wait_ge(qw_ready, (b * CH + i) * RT + RT)
                    for s in range(QN):
                        project(Bk[s], i, wq[:, :, s * DIM:(s + 1) * DIM]).then_inc(q_sum, 1)
                    if 1 <= i and i + 1 < CH:
                        turn_h(b, i + 1)
                    if i >= 1:
                        turn_qk(b, i - 1)
                    project(Bk[4], i, wk).then_inc(k_sum, 1)
                    pe.wait_ge(v_ready, b * CH + i + 1)
                    project(Bk[5], i, wv).then_inc(v_sum, 1)
                turn_qk(b, CH - 1)
                pe.wait_ge(turn_copied, b * NT + NT + 2)
                pe.wait_ge(v_ready, b * CH + CH + 1)
                scores(b * HEADS, 0)
                for h in range(HEADS):
                    n = b * HEADS + h
                    if h + 1 < HEADS:
                        scores(n + 1, h + 1)
                    turn_p(n, h % 2)
                    values(n, h)
                pe.wait_ge(o_ready, b * HEADS + HEADS + 2)
                for i in range(CH):
                    for h in range(HEADS):
                        mm = pe.matmul(Bk[i][:, :], qT[:, h, i * P:(i + 1) * P], wo[:, h, :], start=(h == 0), stop=(h == HEADS - 1))
                    mm.then_inc(y_sum, 1)

        @block.scalar
        def _(act):
            def copy_turn(b, x):
                kind, i, r = x
                n = at[x]
                act.wait_ge(turned, b * NT + n + 1)
                src = Bk[6 + n % 2][:, :]
                if kind == "h":
                    dst = hT[:, i % 2].rearrange("p k n -> p (k n)")
                else:
                    dst = (qT[:, r * REP:(r + 1) * REP, i * P:(i + 1) * P] if r < QN else kT[:, :, i * P:(i + 1) * P])
                    src = src.rearrange("p (h n) -> p h n", h=REP)
                nc.scalar.copy(dst, src).then_inc(turn_copied, 1)

            def square(t, src, col):
                if col > 0:
                    act.wait_ge(sq_done, t * RT + col)
                nc.scalar.activation(sqo[:, :], src, ACT.Square, accum_out=ssq[:, col:col + 1]).then_inc(sq_done, 1)

            def exps(n, par):
                for r, (bank, tiles) in enumerate(S_BANKS):
                    act.wait_ge(nmax_ready, n * 3 + r + 1)
                    for i, col in tiles:
                        w = (i + 1) * P
                        ex = nc.scalar.activation(E[:, par, E_AT[i]:E_AT[i] + w], Bk[bank][:, col:col + w], ACT.Exp,
                                                  bias=nmax[:, par, i:i + 1], accum_out=sums[:, par, i:i + 1])
                    ex.then_inc(exp_done, 1)

            def copy_out(n, h):
                act.wait_ge(p_turned, n * 3 + 2)
                act.wait_ge(pt_ready, n * 3 + 4)
                nc.scalar.copy(PT[:, 4 * P:8 * P], Bk[4][:, :]).then_inc(pt_ready, 1)
                act.wait_ge(o_sum, n + 1)
                nc.scalar.copy(qT[:, h, :], Bk[6 + h % 2][:, :]).then_inc(o_ready, 1)

            act.sem_inc(turn_copied, 2)
            act.sem_inc(v_ready, 1)
            act.sem_inc(exp_done, 3)
            act.sem_inc(o_ready, 2)
            act.wait_ge(cst_ready, 1)
            with act.Fori(0, B) as b:
                copy_turn(b, ("h", 0, 0))
                copy_turn(b, ("h", 1, 0))
                for i in range(CH):
                    t = b * CH + i
                    for s in range(QN):
                        act.wait_ge(q_sum, t * QN + s + 1)
                        square(t, Bk[s][:, :], s)
                    act.wait_ge(ss_ready, t + 1)
                    nc.scalar.activation(rq[:, 0:1], qss[:, 0:1], ACT.Sqrt, scale=DH / (HEADS * DH), bias=eps[:, 0:1]).then_inc(root, 1)
                    if 1 <= i and i + 1 < CH:
                        copy_turn(b, ("h", i + 1, 0))
                    if i >= 1:
                        for r in range(RT):
                            copy_turn(b, ("q", i - 1, r))
                    act.wait_ge(k_sum, t + 1)
                    square(t, Bk[4][:, :], QN)
                    act.wait_ge(sq_done, t * RT + RT)
                    nc.scalar.activation(rq[:, 1:2], ssq[:, QN:RT], ACT.Sqrt, scale=1.0 / (KV * DH), bias=eps[:, 1:2]).then_inc(root, 1)
                    act.wait_ge(v_sum, t + 1)
                    nc.scalar.copy(v[:, i, :], Bk[5][:, :]).then_inc(v_ready, 1)
                for r in range(RT):
                    copy_turn(b, ("q", CH - 1, r))
                for h in range(HEADS):
                    n = b * HEADS + h
                    exps(n, h % 2)
                    if h >= 1:
                        copy_out(n - 1, h - 1)
                copy_out(b * HEADS + HEADS - 1, HEADS - 1)

        @block.gpsimd
        def _(pool):
            half = ROT // 2
            with pool.Fori(0, B) as b:
                for i in range(CH):
                    t = b * CH + i
                    pool.wait_ge(qw_ready, t * RT + RT + RT)
                    for lo, hi in ((0, half), (half, ROT)):
                        src = (lo + half) % ROT
                        tt = nc.gpsimd.tensor_tensor(sw[:, :, lo:hi], qk[:, :, src:src + half],
                                                     rope[:, i, 1, lo:hi].unsqueeze(1).to_broadcast([P, HEADS + KV, half]), ALU.mult)
                    tt.then_inc(swapped, 1)
                    pool.wait_ge(swapped, t + 1)
                    nc.gpsimd.tensor_tensor(qk[:, :, 0:ROT], qk[:, :, 0:ROT],
                                            rope[:, i, 0, :].unsqueeze(1).to_broadcast([P, HEADS + KV, ROT]), ALU.mult).then_inc(cosined, 1)
                    pool.wait_ge(cosined, t + 1)
                    nc.gpsimd.tensor_tensor(qk[:, :, 0:ROT], qk[:, :, 0:ROT], sw[:, :, :], ALU.add).then_inc(rotated, 1)

        @block.vector
        def _(dve):
            def norms(b, i):
                t = b * CH + i
                nc.vector.tensor_scalar(xt[:, i, :], xt[:, i, :], st[:, 0, i:i + 1], st[:, 1, i:i + 1],
                                        ALU.subtract, ALU.mult).then_inc(xn_ready, 1)
                dve.wait_ge(xn_ready, t + 1)
                nc.vector.tensor_scalar(hn[:, i % 2, :], xt[:, i, :], st[:, 2, i:i + 1], None, ALU.mult).then_inc(h_ready, 1)

            def weigh(b, i):
                t = b * CH + i
                dve.wait_ge(sq_done, t * RT + QN)
                nc.vector.tensor_reduce(qss[:, 0:1], ssq[:, 0:QN], AX.X, ALU.add).then_inc(ss_ready, 1)
                dve.wait_ge(root, t * 2 + 1)
                nc.vector.reciprocal(rq[:, 0:1], rq[:, 0:1]).then_inc(rq_ready, 1)
                dve.wait_ge(rq_ready, t * 2 + 1)
                if i > 0:
                    dve.wait_ge(turned, b * NT + at["q", i - 1, RT - 1] + 1)
                flat = qk[:].rearrange("p h d -> p (h d)")
                for s in range(QN):
                    nc.vector.scalar_tensor_tensor(out=flat[:, s * DIM:(s + 1) * DIM], in0=Bk[s][:, :], scalar=rq[:, 0:1],
                                                   in1=qnw[:, s * DIM:(s + 1) * DIM], op0=ALU.mult, op1=ALU.mult).then_inc(qw_ready, 1)
                dve.wait_ge(root, t * 2 + 2)
                nc.vector.reciprocal(rq[:, 1:2], rq[:, 1:2]).then_inc(rq_ready, 1)
                dve.wait_ge(rq_ready, t * 2 + 2)
                nc.vector.scalar_tensor_tensor(out=flat[:, QN * DIM:RT * DIM], in0=Bk[4][:, :], scalar=rq[:, 1:2],
                                               in1=knw[:, :], op0=ALU.mult, op1=ALU.mult).then_inc(qw_ready, 1)

            def maxima(n, par):
                for r, (bank, tiles) in enumerate(S_BANKS):
                    dve.wait_ge(s_sum, n * 3 + r + 1)
                    for i, col in tiles:
                        mx = nc.vector.tensor_reduce(nmax[:, par, i:i + 1], Bk[bank][:, col:col + (i + 1) * P], AX.X, ALU.max, negate=True)
                    mx.then_inc(nmax_ready, 1)

            def copy_p(n):
                dve.wait_ge(p_turned, n * 3 + 1)
                nc.vector.tensor_copy(PT[:, 0:4 * P], Bk[3][:, :]).then_inc(pt_ready, 1)
                dve.wait_ge(p_turned, n * 3 + 3)
                dve.wait_ge(pt_ready, n * 3 + 5)
                nc.vector.tensor_copy(PT[:, 8 * P:10 * P], Bk[5][:, 0:2 * P]).then_inc(pt_ready, 1)

            def probabilities(n, par):
                dve.wait_ge(exp_done, n * 3 + 6)
                nc.vector.reciprocal(rec[:, :], sums[:, par, :]).then_inc(rec_ready, 1)
                dve.wait_ge(rec_ready, n + 1)
                for i in range(CH):
                    cols = slice(E_AT[i], E_AT[i] + (i + 1) * P)
                    ts = nc.vector.tensor_scalar(E[:, par, cols], E[:, par, cols], rec[:, i:i + 1], None, ALU.mult)
                ts.then_inc(e_ready, 1)

            dve.wait_ge(cst_in, 48)
            nc.vector.memset(eps[:, 0:1], DH * RMS_EPS)
            nc.vector.memset(eps[:, 1:2], RMS_EPS)
            nc.vector.tensor_copy(identb[:, :], ident[:, :])
            nc.vector.tensor_copy(negb[:, :], neg[:, :]).then_inc(cst_ready, 1)
            dve.sem_inc(qw_ready, RT)
            dve.sem_inc(pt_ready, 3)
            dve.sem_inc(x1_ready, CH)
            for s in range(2):
                dve.sem_inc(x1_out[s], 16)
            with dve.Fori(0, B) as b:
                dve.wait_ge(x1_ready, b * CH + CH)
                nc.vector.tensor_copy(st[:], stat[:, :, bass.ds(b * CH, CH)]).then_inc(st_ready, 1)
                dve.wait_ge(st_ready, b + 1)
                dve.wait_ge(x_in, b * 16 + 16)
                norms(b, 0)
                norms(b, 1)
                for i in range(CH):
                    weigh(b, i)
                    if i + 2 < CH:
                        dve.wait_ge(turned, b * NT + at["h", i, 0] + 1)
                        norms(b, i + 2)
                for h in range(HEADS):
                    n = b * HEADS + h
                    maxima(n, h % 2)
                    if h >= 1:
                        copy_p(n - 1)
                    probabilities(n, h % 2)
                copy_p(b * HEADS + HEADS - 1)
                for i in range(CH):
                    dve.wait_ge(y_sum, b * CH + i + 1)
                    dve.wait_ge(x1_out[i % 2], b * 32 + (i // 2) * 16 + 16)
                    nc.vector.tensor_tensor(x1[:, i % 2, :], Bk[i][:, :], xt[:, i, :], ALU.add).then_inc(x1_ready, 1)


def moe_route(nc, F, x_dram, x1_dram, const_dram, h2T, acc, comb):
    with ExitStack() as ctx:
        sem = semaphores(nc, ctx, "mr")

        def sb(n, s, d=F32):
            return ctx.enter_context(nc.sbuf_tensor(f"mr_{n}", s, d))


        ident = sb("ident", [P, P])
        ln2 = sb("ln2", [P, KT])
        rw = sb("rw", [P, KT, EXPERTS])
        rb = sb("rb", [P, EXPERTS])
        rank = sb("rank", [P, EXPERTS])
        x1 = sb("x1", [P, TILES, DIM])
        hn = sb("hn", [P, CH, DIM])
        sqo = sb("sqo", [P, DIM])
        ms = sb("ms", [P, TILES])
        rs = sb("rs", [P, TILES])
        eps = sb("eps", [P, 1])
        gsh = [P, TILES, EXPERTS]
        sig, key, eq, pick, two = (sb(n, gsh) for n in ("sig", "key", "eq", "pick", "two"))
        top = sb("top", [P, TILES])
        psT = [ctx.enter_context(nc.psum_tensor(f"mr_T{k}", [P, SEQ], F32)) for k in range(2)]
        psL = ctx.enter_context(nc.psum_tensor("mr_L", [P, TILES, EXPERTS, 4], F32))
        small_in, x1_in, x_in = sem("small_in"), sem("x1_in"), sem("x_in")
        rank_set, eps_set, sq_done, root, rs_ready, hn_ready, turned, copied, logits, sig_done, added, step = (
            sem(x) for x in ("rank", "eps", "sq", "root", "rs", "hn", "turned", "copied", "logits", "sig", "added", "step"))
        block = ctx.enter_context(nc.Block())

        @block.sync
        def _(sp):
            sp.dma_start(x1[:, :, :], x1_dram.rearrange("(t p) d -> p t d", p=P)).then_inc(x1_in, 16)
            sp.dma_start(acc[:, :, :], x_dram.rearrange("(t p) d -> p t d", p=P)).then_inc(x_in, 16)
            sp.dma_start(ident[:, :], const_dram[:, C_ID:C_ID + P]).then_inc(small_in, 16)
            sp.dma_start(rw[:, :, :], F["router_w"].rearrange("(k p) e -> p k e", p=P)).then_inc(small_in, 16)
            sp.dma_start(rb[:, :], F["router_bias"].partition_broadcast(P)).then_inc(small_in, 16)
            sp.dma_start(ln2[:, :], F["ln2_w"].rearrange("(k p) -> p k", p=P), allow_slow_non_contiguous=True).then_inc(small_in, 16)
            sp.wait_ge(small_in, 64)

        @block.gpsimd
        def _(pool):
            for e in range(EXPERTS):
                nc.gpsimd.memset(rank[:, e:e + 1], float(EXPERTS - e)).then_inc(rank_set, 1)
            pool.wait_ge(x1_in, 16)
            pool.wait_ge(x_in, 16)
            for b in range(B):
                tiles = slice(b * CH, (b + 1) * CH)
                nc.gpsimd.tensor_tensor(acc[:, tiles, :], acc[:, tiles, :], x1[:, tiles, :], ALU.add).then_inc(added, 1)

        @block.scalar
        def _(act):
            act.wait_ge(x1_in, 16)
            act.wait_ge(eps_set, 1)
            for t in range(TILES):
                if t > 0:
                    act.wait_ge(sq_done, t)
                nc.scalar.activation(sqo[:, :], x1[:, t, :], ACT.Square, accum_out=ms[:, t:t + 1]).then_inc(sq_done, 1)
            act.wait_ge(sq_done, TILES)
            nc.scalar.activation(ms[:, :], ms[:, :], ACT.Sqrt, scale=1.0 / DIM, bias=eps[:, 0:1]).then_inc(root, 1)
            act.wait_ge(small_in, 64)
            for b in range(B):
                for k in range(KT):
                    act.wait_ge(turned, b * KT + k + 1)
                    nc.scalar.activation(h2T[:, k, b * SEQ:(b + 1) * SEQ], psT[k % 2][:, :], ACT.Copy, scale=ln2[:, k:k + 1]).then_inc(copied, 1)
            act.wait_ge(logits, 1)
            nc.scalar.activation(sig[:], psL[:, :, :, 0], ACT.Sigmoid).then_inc(sig_done, 1)

        @block.tensor
        def _(pe):
            pe.wait_ge(small_in, 64)
            for b in range(B):
                pe.wait_ge(hn_ready, (b + 1) * CH)
                for k in range(KT):
                    n = b * KT + k
                    if n >= 2:
                        pe.wait_ge(copied, n - 1)
                    for t in range(CH):
                        tr = pe.transpose(psT[k % 2][:, t * P:(t + 1) * P], hn[:, t, k * P:(k + 1) * P], ident[:, :])
                    tr.then_inc(turned, 1)
            pe.wait_ge(copied, B * KT)
            for t in range(TILES):
                for k in range(KT):
                    mm = pe.matmul(psL[:, t, :, 0], h2T[:, k, t * P:(t + 1) * P], rw[:, k, :], start=(k == 0), stop=(k == KT - 1))
            mm.then_inc(logits, 1)

        @block.vector
        def _(dve):
            nc.vector.memset(eps[:, :], RMS_EPS).then_inc(eps_set, 1)
            dve.wait_ge(root, 1)
            nc.vector.reciprocal(rs[:, :], ms[:, :]).then_inc(rs_ready, 1)
            dve.wait_ge(rs_ready, 1)
            for b in range(B):
                if b > 0:
                    dve.wait_ge(turned, b * KT)
                for t in range(CH):
                    nc.vector.tensor_scalar(hn[:, t, :], x1[:, b * CH + t, :], rs[:, b * CH + t:b * CH + t + 1], None, ALU.mult).then_inc(hn_ready, 1)
            n = [0]

            def then(ins):
                n[0] += 1
                ins.then_inc(step, 1)
                dve.wait_ge(step, n[0])

            dve.wait_ge(sig_done, 1)
            dve.wait_ge(small_in, 64)
            dve.wait_ge(rank_set, EXPERTS)
            def per_expert(a):
                return a[:, :].unsqueeze(1).to_broadcast(gsh)
            then(nc.vector.tensor_tensor(key[:], sig[:], per_expert(rb), ALU.add))
            for turn in range(2):
                then(nc.vector.tensor_reduce(top[:, :], key[:], AX.X, ALU.max))
                then(nc.vector.tensor_tensor(eq[:], key[:], bc(top[:, :], EXPERTS), ALU.is_equal))
                then(nc.vector.tensor_tensor(eq[:], eq[:], per_expert(rank), ALU.mult))
                then(nc.vector.tensor_reduce(top[:, :], eq[:], AX.X, ALU.max))
                then(nc.vector.tensor_tensor(pick[:], eq[:], bc(top[:, :], EXPERTS), ALU.is_equal))
                if turn == 0:
                    then(nc.vector.tensor_copy(two[:], pick[:]))
                    then(nc.vector.tensor_scalar(pick[:], pick[:], -1e30, None, ALU.mult))
                    then(nc.vector.tensor_tensor(key[:], key[:], pick[:], ALU.add))
                else:
                    then(nc.vector.tensor_tensor(two[:], two[:], pick[:], ALU.add))
            then(nc.vector.tensor_tensor(two[:], two[:], sig[:], ALU.mult))
            then(nc.vector.tensor_reduce(top[:, :], two[:], AX.X, ALU.add))
            then(nc.vector.reciprocal(top[:, :], top[:, :]))
            then(nc.vector.tensor_tensor(comb[:], two[:], bc(top[:, :], EXPERTS), ALU.mult))


def moe_experts(nc, F, h2T, acc, comb, out_dram):
    with ExitStack() as ctx:
        sem = semaphores(nc, ctx, "me")

        def sb(n, s, d=F32):
            return ctx.enter_context(nc.sbuf_tensor(f"me_{n}", s, d))


        wg = sb("wg", [P, 2, KT, INNER])
        wu = sb("wu", [P, 2, KT, INNER])
        wd = sb("wd", [P, 2, IT, DIM])
        sg = sb("sg", [P, IT, SEQ])
        a = sb("a", [P, 2, IT, SEQ])
        psG = [ctx.enter_context(nc.psum_tensor(f"me_G{k}", [P, SEQ], F32)) for k in range(IT)]
        psU = [ctx.enter_context(nc.psum_tensor(f"me_U{k}", [P, SEQ], F32)) for k in range(IT)]
        psD = [ctx.enter_context(nc.psum_tensor(f"me_D{k}", [P, DIM], F32)) for k in range(4)]
        w_in = [sem("w_in0"), sem("w_in1")]
        g_sum, u_sum, silu_done, a_ready, d_sum, added, out_done = (
            sem(x) for x in ("gsum", "usum", "silu", "a", "dsum", "added", "out"))
        block = ctx.enter_context(nc.Block())
        STEPS = EXPERTS * B

        @block.sync
        def _(sp):
            def load(e, par):
                sp.dma_start(wg[:, par], F["wg"][bass.ds(e, 1)].rearrange("o (k p) n -> p (o k) n", p=P)).then_inc(w_in[par], 16)
                sp.dma_start(wu[:, par], F["wu"][bass.ds(e, 1)].rearrange("o (k p) n -> p (o k) n", p=P)).then_inc(w_in[par], 16)
                sp.dma_start(wd[:, par], F["wd"][bass.ds(e, 1)].rearrange("o (k p) n -> p (o k) n", p=P)).then_inc(w_in[par], 16)

            load(0, 0)
            load(1, 1)
            with sp.Fori(0, EXPERTS // 2 - 1) as i:
                for s in range(2):
                    e = i * 2 + s
                    sp.wait_ge(d_sum, (e * B + B) * CH)
                    load(e + 2, s)
            for b in range(B):
                sp.wait_ge(added, (STEPS - B + b + 1) * CH + CH)
                sp.dma_start(out_dram[b * SEQ:(b + 1) * SEQ, :].rearrange("(t p) d -> p t d", p=P), acc[:, b * CH:(b + 1) * CH, :]).then_inc(out_done, 16)
            sp.wait_ge(out_done, 16 * B)

        @block.tensor
        def _(pe):
            def up(i, s, b):
                e = i * 2 + s
                n = e * B + b
                if b == 0:
                    pe.wait_ge(w_in[s], i * 48 + 48)
                for w, bank, done, used in ((wg, psG, g_sum, silu_done), (wu, psU, u_sum, a_ready)):
                    for j in range(IT):
                        pe.wait_ge(used, n * IT + j + 1)
                        for k in range(KT):
                            mm = pe.matmul(bank[j][:, :], w[:, s, k, j * P:(j + 1) * P], h2T[:, k, b * SEQ:(b + 1) * SEQ],
                                           start=(k == 0), stop=(k == KT - 1))
                        mm.then_inc(done, 1)

            def down(i, s, b):
                n = (i * 2 + s) * B + b
                pe.wait_ge(a_ready, n * IT + 2 * IT)
                for t in range(CH):
                    pe.wait_ge(added, n * CH + t + 1)
                    for j in range(IT):
                        mm = pe.matmul(psD[t][:, :], a[:, b % 2, j, t * P:(t + 1) * P], wd[:, s, j, :], start=(j == 0), stop=(j == IT - 1))
                    mm.then_inc(d_sum, 1)

            def pair(i, more):
                for s in range(2):
                    for b in range(B):
                        if s == 1 or b > 0:
                            up(i, s, b)
                        prev = (i, s, b - 1) if b else (i, 0, B - 1)
                        if s == 1 or b > 0:
                            down(*prev)
                if more:
                    up(i + 1, 0, 0)
                down(i, 1, B - 1)

            up(0, 0, 0)
            with pe.Fori(0, EXPERTS // 2 - 1) as i:
                pair(i, True)
            pair(EXPERTS // 2 - 1, False)

        @block.scalar
        def _(act):
            act.sem_inc(silu_done, IT)
            with act.Fori(0, EXPERTS // 2) as i:
                for s in range(2):
                    for b in range(B):
                        n = (i * 2 + s) * B + b
                        for j in range(IT):
                            act.wait_ge(g_sum, n * IT + j + 1)
                            act.wait_ge(a_ready, n * IT + j + 1)
                            nc.scalar.activation(sg[:, j, :], psG[j][:, :], ACT.Silu).then_inc(silu_done, 1)

        @block.vector
        def _(dve):
            def gated(i, s, b):
                n = (i * 2 + s) * B + b
                for j in range(IT):
                    dve.wait_ge(silu_done, n * IT + j + 1 + IT)
                    dve.wait_ge(u_sum, n * IT + j + 1)
                    nc.vector.tensor_tensor(a[:, b % 2, j, :], psU[j][:, :], sg[:, j, :], ALU.mult).then_inc(a_ready, 1)

            def add(i, s, b):
                e = i * 2 + s
                n = e * B + b
                for t in range(CH):
                    dve.wait_ge(d_sum, n * CH + t + 1)
                    tile = b * CH + t
                    nc.vector.scalar_tensor_tensor(out=acc[:, tile, :], in0=psD[t][:, :], scalar=comb[:, tile, bass.ds(e, 1)],
                                                   in1=acc[:, tile, :], op0=ALU.mult, op1=ALU.add).then_inc(added, 1)

            def pair(i, more):
                for s in range(2):
                    for b in range(B):
                        if s == 1 or b > 0:
                            gated(i, s, b)
                            add(*((i, s, b - 1) if b else (i, 0, B - 1)))
                if more:
                    gated(i + 1, 0, 0)
                add(i, 1, B - 1)

            dve.sem_inc(a_ready, IT)
            dve.sem_inc(added, CH)
            gated(0, 0, 0)
            with dve.Fori(0, EXPERTS // 2 - 1) as i:
                pair(i, True)
            pair(EXPERTS // 2 - 1, False)


def stage_ffn(nc, I, x_dram, const_dram, rope_dram, x1_dram, out_dram):
    F = {k[len("L0_ffn_"):]: v for k, v in I.items() if k.startswith("L0_ffn_")}
    with ExitStack() as ctx:
        def sb(n, s, d=F32):
            return ctx.enter_context(nc.sbuf_tensor(f"f_{n}", s, d))

        stat = sb("stat", [P, 3, TILES])
        wq, wk, wv = sb("wq", [P, KT, HEADS * DH]), sb("wk", [P, KT, KV * DH]), sb("wv", [P, KT, KV * DH])
        wo = sb("wo", [P, HEADS, DIM])
        qnw, knw = sb("qnw", [P, HEADS * DH]), sb("knw", [P, KV * DH])
        self_setup(nc, F, x_dram, const_dram, stat, wq, wk, wv, wo, qnw, knw)
        self_attention(nc, x_dram, const_dram, rope_dram, stat, wq, wk, wv, wo, qnw, knw, x1_dram)
    with ExitStack() as ctx:
        h2T = ctx.enter_context(nc.sbuf_tensor("m_h2T", [P, KT, TOK], F32))
        acc = ctx.enter_context(nc.sbuf_tensor("m_acc", [P, TILES, DIM], F32))
        comb = ctx.enter_context(nc.sbuf_tensor("m_comb", [P, TILES, EXPERTS], F32))
        moe_route(nc, F, x_dram, x1_dram, const_dram, h2T, acc, comb)
        moe_experts(nc, F, h2T, acc, comb, out_dram)


def build(nc, I, out):
    og_dram = nc.dram_tensor("gated_outputs", (HEADS * P, TOK), F32, kind="Internal").ap()
    xa_dram, xb_dram, x1_dram = (nc.dram_tensor(n, (TOK, DIM), F32, kind="Internal").ap() for n in ("after_delta", "after_cross", "x1"))
    stage_attn(nc, I, I["const"], og_dram, xa_dram)
    stage_xattn(nc, I, xa_dram, I["const"], xb_dram)
    stage_ffn(nc, I, xb_dram, I["const"], I["rope"], x1_dram, out)


def shape_constants():
    import numpy as np
    r = np.arange(P)
    c = np.zeros((P, C_W), np.float32)
    c[:, C_ID:C_ID + P] = np.eye(P)
    c[:, C_UP:C_UP + P] = r[:, None] <= r[None, :]
    c[:, C_GT:C_GT + P] = r[:, None] > r[None, :]
    c[:, C_M1:C_M1 + P] = -((r[:, None] == r[None, :] + 1) & (r[:, None] % 2 == 1)).astype(np.float32)
    for l, m in enumerate(LEVELS):
        cols = r[(r // m) % 2 == 1]
        hit = (r[:, None] // (2 * m) == cols[None, :] // (2 * m)) & ((r[:, None] // m) % 2 == 0)
        c[:, C_LV + 64 * l:C_LV + 64 * l + 64] = -hit.astype(np.float32)
    c[:, C_ONE:C_ONE + P] = 1.0
    c[:, C_NEG:C_NEG + P] = np.where(r[None, :] > r[:, None], np.float32(-1e30), np.float32(0))
    return c


def rope_table():
    import numpy as np
    half = np.arange(0, 64, 2, dtype=np.float32) / np.float32(64)
    freq = np.float32(1.0) / np.power(np.float32(1000000.0), half)
    ang = np.arange(SEQ, dtype=np.float32)[:, None] * freq[None, :].astype(np.float32)
    cos, sin = np.cos(ang), np.sin(ang)
    return np.stack([np.concatenate([cos, cos], 1), np.concatenate([-sin, sin], 1)], 1).astype(np.float32)


def kernel(**inputs):
    import numpy as np
    import concourse.bacc as bacc
    from concourse.bass_utils import run_bass_kernel_spmd as run

    nc = bacc.Bacc("TRN2", target_bir_lowering=False, num_devices=1)
    arrays, I = {}, {}

    def give(name, a):
        arrays[f"in_{name}"] = a
        I[name] = nc.dram_tensor(f"in_{name}", a.shape, mybir.dt.from_np(a.dtype), kind="ExternalInput").ap()

    for name, a in inputs.items():
        a = np.ascontiguousarray(a)
        if name in ("x", "ctx_2048"):
            a = a.reshape(-1, DIM)
        give(name, a)
    give("const", shape_constants())
    give("rope", rope_table())
    out = nc.dram_tensor("out", (TOK, DIM), F32, kind="ExternalOutput").ap()
    build(nc, I, out)
    got = run(nc, [arrays], core_ids=[0]).results[0]["out"]
    return got.reshape(B, SEQ, DIM)
```

```python
from contextlib import ExitStack

import concourse.bass as bass
from concourse import mybir

ALU = mybir.AluOpType
ACT = mybir.ActivationFunctionType
AX = mybir.AxisListType
F32 = mybir.dt.float32
F32R = mybir.dt.float32r
BF16 = mybir.dt.bfloat16

P = 128
B, SEQ, DIM = 4, 512, 512
TOK = B * SEQ
TILES = TOK // P
KT = DIM // P
CH = SEQ // P
HEADS = 16
BN = B * P
LN_EPS = 1e-5
RMS_EPS = 1e-6
MAGIC = 12582912.0
LEVELS = [2, 4, 8, 16, 32, 64]
NLV = len(LEVELS)

C_ID, C_UP, C_GT, C_M1, C_LV = 0, P, 2 * P, 3 * P, 4 * P
C_ONE = C_LV + 64 * NLV
C_NEG = C_ONE + P
C_W = C_NEG + P


def second(ap, m):
    return ap.rearrange("p b (g two m) -> p b g two m", two=2, m=m)[:, :, :, 1, :]


def first(ap, m):
    return ap.rearrange("p b (g two m) -> p b g two m", two=2, m=m)[:, :, :, 0, :]


def bc(col, n):
    return col.unsqueeze(2).to_broadcast([col.shape[0], col.shape[1], n])


def semaphores(nc, ctx, prefix):
    held = []

    def release():
        nc.clear_and_free_semaphores(held)
        nc.all_engine_barrier()

    def sem(name):
        held.append(nc.alloc_semaphore(f"{prefix}_{name}"))
        return held[-1]

    ctx.callback(release)
    return sem


def layernorm_transposed(nc, name, x_dram, const_dram, xnT, parts=None):
    with ExitStack() as ctx:
        sem = semaphores(nc, ctx, name)

        def sb(n, s, d=F32):
            return ctx.enter_context(nc.sbuf_tensor(f"{name}_{n}", s, d))


        ident = sb("ident", [P, P])
        xt = sb("xt", [P, CH, DIM])
        xn = sb("xn", [P, CH, DIM])
        stats = sb("stats", [P, CH, 6])
        mv = sb("mv", [P, CH, 2])
        eps = sb("eps", [P, 1])
        std = sb("std", [P, CH])
        rstd = sb("rstd", [P, CH])
        psT = [ctx.enter_context(nc.psum_tensor(f"{name}_psT{k}", [P, BN], F32)) for k in range(2)]
        ident_in, x_in, eps_set = sem("ident_in"), sem("x_in"), sem("eps_set")
        stat_done, var_done, std_done, rstd_done = sem("stat"), sem("var"), sem("std"), sem("rstd")
        xn_done, turned, copied, lead_done, rest_done = (sem(x) for x in ("xn", "turned", "copied", "lead", "rest"))
        block = ctx.enter_context(nc.Block())

        @block.sync
        def _(sp):
            sp.dma_start(ident[:, :], const_dram[:, C_ID:C_ID + P]).then_inc(ident_in, 16)
            sp.sem_inc(xn_done, CH)
            for b in range(B):
                sp.wait_ge(xn_done, b * CH + CH)
                sp.dma_start(xt[:, :, :], x_dram[bass.ds(b * SEQ, SEQ), :].rearrange("(t p) d -> p t d", p=P)
                             ).then_inc(x_in, 16)

        @block.vector
        def _(dve):
            nc.vector.memset(eps[:, :], LN_EPS).then_inc(eps_set, 1)
            dve.sem_inc(turned, KT)
            for b in range(B):
                dve.wait_ge(x_in, b * 16 + 16)
                for t in range(CH):
                    nc.vector.bn_stats(stats[:, t, :], xt[:, t, :]).then_inc(stat_done, 1)
                for t in range(CH):
                    dve.wait_ge(stat_done, b * CH + t + 1)
                    nc.vector.bn_aggr(mv[:, t, :], stats[:, t, :]).then_inc(var_done, 1)
                dve.wait_ge(std_done, b + 1)
                nc.vector.reciprocal(rstd[:, :], std[:, :]).then_inc(rstd_done, 1)
                dve.wait_ge(rstd_done, b + 1)
                dve.wait_ge(turned, b * KT + KT)
                for t in range(CH):
                    nc.vector.tensor_scalar(xn[:, t, :], xt[:, t, :], mv[:, t, 0:1], rstd[:, t:t + 1],
                                            ALU.subtract, ALU.mult).then_inc(xn_done, 1)

        @block.scalar
        def _(act):
            act.wait_ge(eps_set, 1)
            for b in range(B):
                act.wait_ge(var_done, b * CH + CH)
                nc.scalar.activation(std[:, :], mv[:, :, 1], ACT.Sqrt, bias=eps[:, 0:1]).then_inc(std_done, 1)
                for k in range(KT):
                    act.wait_ge(turned, b * KT + k + 1 + KT)
                    nc.scalar.copy(xnT[:, k, bass.ds(b * SEQ, SEQ)], psT[k % 2][:, :]).then_inc(copied, 1)
                    if parts:
                        act.wait_ge(copied, b * KT + k + 3)
                        nc.scalar.copy(parts[0][:, k, bass.ds(b * SEQ, SEQ)], xnT[:, k, bass.ds(b * SEQ, SEQ)]).then_inc(lead_done, 1)

        @block.gpsimd
        def _(pool):
            if parts:
                for b in range(B):
                    cols = bass.ds(b * SEQ, SEQ)
                    for k in range(KT):
                        pool.wait_ge(lead_done, b * KT + k + 1)
                        nc.gpsimd.tensor_tensor(parts[1][:, k, cols], xnT[:, k, cols], parts[0][:, k, cols].bitcast(F32),
                                                ALU.subtract).then_inc(rest_done, 1)

        @block.tensor
        def _(pe):
            pe.wait_ge(ident_in, 16)
            pe.sem_inc(copied, 2)
            for b in range(B):
                pe.wait_ge(xn_done, b * CH + CH + CH)
                for k in range(KT):
                    pe.wait_ge(copied, b * KT + k + 1)
                    for t in range(CH):
                        tr = pe.transpose(psT[k % 2][:, t * P:(t + 1) * P], xn[:, t, k * P:(k + 1) * P], ident[:, :])
                    tr.then_inc(turned, 1)


P_LG, P_BETA, P_NBD, P_G, P_END = 16, 32, 48, 64, 80
PN = 96
PW = 100


def delta_gates(nc, xnT, A, const_dram, ptab):
    with ExitStack() as ctx:
        sem = semaphores(nc, ctx, "ga")

        def sb(n, s, d=F32):
            return ctx.enter_context(nc.sbuf_tensor(f"ga_{n}", s, d))


        def ps(n, s):
            return ctx.enter_context(nc.psum_tensor(f"ga_{n}", s, F32))

        G2 = 2 * HEADS
        cst = sb("cst", [P, 2 * P])
        ones = sb("ones", [P, P])
        wab = sb("wab", [G2, DIM])
        wabT = sb("wabT", [P, KT, G2])
        ab = sb("ab", [G2, BN])
        abt = sb("abt", [P, B, CH, G2])
        alog = sb("alog", [P, HEADS])
        dtb = sb("dtb", [P, HEADS])
        ea = sb("ea", [P, HEADS])
        gsh = [P, B, CH, HEADS]
        z, az, rz, ez, lz = (sb(n, gsh) for n in ("z", "az", "rz", "ez", "lz"))
        beta = sb("beta", gsh)
        psW = ps("psW", [P, KT, G2])
        psAB = ps("psAB", [G2, BN])
        psT = ps("psT", [P, CH, G2])
        psG = ps("psG", [P, 2, HEADS, TILES])
        small_in, par_in = sem("small_in"), sem("par_in")
        w_turned, w_copied = sem("w_turned"), sem("w_copied")
        ab_done, ab_copied, ab_turned, abt_copied = sem("ab_done"), sem("ab_copied"), sem("ab_turned"), sem("abt_copied")
        rstep = sem("rstep")
        vstep, astep, g_done, tab_done = sem("vstep"), sem("astep"), sem("g_done"), sem("tab_done")
        block = ctx.enter_context(nc.Block())
        NPAR = 7

        @block.sync
        def _(sp):
            sp.dma_start(cst[:, :], const_dram[:, 0:2 * P]).then_inc(small_in, 16)
            sp.dma_start(ones[:, :], const_dram[:, C_ONE:C_ONE + P]).then_inc(small_in, 16)
            sp.dma_start(wab[0:HEADS, :], A["Wa"]).then_inc(small_in, 16)
            sp.dma_start(wab[HEADS:G2, :], A["Wb"]).then_inc(small_in, 16)
            sp.dma_start(alog[:, :], A["A_log"].partition_broadcast(P)).then_inc(small_in, 16)
            sp.dma_start(dtb[:, :], A["dt_bias"].partition_broadcast(P)).then_inc(small_in, 16)
            for j, n in enumerate(("k", "q", "v")):
                sp.dma_start(ptab[:, :, 4 * j:4 * j + 4], A["cw_" + n].rearrange("(h p) j -> p h j", p=P)).then_inc(par_in, 16)
                sp.dma_start(ptab[:, :, 12 + j], A["cb_" + n].rearrange("(h p) -> p h", p=P),
                             allow_slow_non_contiguous=True).then_inc(par_in, 16)
            sp.dma_start(ptab[:, :, PN], A["norm_w"].rearrange("(h p) -> p h", p=P),
                             allow_slow_non_contiguous=True).then_inc(par_in, 16)
            sp.wait_ge(par_in, 16 * NPAR)

        @block.tensor
        def _(pe):
            pe.wait_ge(small_in, 16 * 6)
            for k in range(KT):
                tr = pe.transpose(psW[:, k, :], wab[:, k * P:(k + 1) * P], cst[0:G2, 0:G2])
            tr.then_inc(w_turned, 1)
            pe.wait_ge(w_copied, 1)
            pe.sem_inc(abt_copied, 1)
            for b in range(B):
                for k in range(KT):
                    mm = pe.matmul(psAB[:, :], wabT[:, k, :], xnT[:, k, bass.ds(b * SEQ, SEQ)], start=(k == 0), stop=(k == KT - 1))
                mm.then_inc(ab_done, 1)
                pe.wait_ge(ab_copied, b + 1)
                pe.wait_ge(abt_copied, b + 1)
                for c in range(CH):
                    tr = pe.transpose(psT[:, c, :], ab[:, c * P:(c + 1) * P], cst[0:G2, 0:G2])
                tr.then_inc(ab_turned, 1)
            pe.wait_ge(tab_done, 1)
            pe.matmul(psG[:, 0], cst[:, C_UP:C_UP + P], ptab[:, :, P_LG:P_BETA], start=True, stop=True)
            pe.matmul(psG[:, 1], ones[:, :], ptab[:, :, P_LG:P_BETA], start=True, stop=True).then_inc(g_done, 1)

        @block.scalar
        def _(act):
            act.wait_ge(small_in, 16 * 6)
            nc.scalar.activation(ea[:, :], alog[:, :], ACT.Exp).then_inc(astep, 1)
            act.wait_ge(vstep, 2)
            nc.scalar.activation(ez[:], az[:], ACT.Exp, scale=-1.0).then_inc(astep, 1)
            act.wait_ge(astep, 2)
            nc.scalar.activation(lz[:], ez[:], ACT.Ln, bias=1.0).then_inc(astep, 1)
            act.wait_ge(g_done, 1)
            for j, col in enumerate((P_G, P_END)):
                ex = nc.scalar.activation(ptab[:, :, col:col + TILES], psG[:, j], ACT.Exp)
            ex.then_inc(astep, 1)
            nc.scalar.activation(beta[:], abt[:, :, :, HEADS:G2], ACT.Sigmoid).then_inc(astep, 1)

        @block.vector
        def _(dve):
            nc.vector.memset(ptab[:, :, 15:16], 0.0)
            nc.vector.memset(ptab[:, :, PN + 1:PW], 0.0)
            dve.wait_ge(w_turned, 1)
            nc.vector.tensor_copy(wabT[:], psW[:, :, :]).then_inc(w_copied, 1)
            for b in range(B):
                dve.wait_ge(ab_done, b + 1)
                nc.vector.tensor_copy(ab[:, :], psAB[:, :]).then_inc(ab_copied, 1)
                dve.wait_ge(ab_turned, b + 1)
                nc.vector.tensor_copy(abt[:, bass.ds(b, 1), :, :].rearrange("p o c g -> p (o c) g"), psT[:, :, :]
                                      ).then_inc(abt_copied, 1)
            dve.wait_ge(abt_copied, B + 1)
            dve.wait_ge(small_in, 16 * 6)
            dt_all = dtb[:, :].unsqueeze(1).to_broadcast([P, B * CH, HEADS])
            flat = "p b c h -> p (b c) h"
            nc.vector.tensor_tensor(z[:].rearrange(flat), abt[:, :, :, 0:HEADS].rearrange(flat), dt_all, ALU.add).then_inc(vstep, 1)
            dve.wait_ge(vstep, 1)
            nc.vector.tensor_scalar(az[:], z[:], -1.0, None, ALU.mult).then_inc(rstep, 1)
            dve.wait_ge(rstep, 1)
            nc.vector.tensor_tensor(az[:], az[:], z[:], ALU.max).then_inc(vstep, 1)
            nc.vector.tensor_scalar(rz[:], z[:], 0.0, None, ALU.max).then_inc(rstep, 1)
            dve.wait_ge(astep, 3)
            dve.wait_ge(rstep, 2)
            nc.vector.tensor_tensor(rz[:], rz[:], lz[:], ALU.add).then_inc(rstep, 1)
            dve.wait_ge(rstep, 3)
            ea_all = ea[:, :].unsqueeze(1).to_broadcast([P, B * CH, HEADS])
            nc.vector.tensor_tensor(rz[:].rearrange(flat), rz[:].rearrange(flat), ea_all, ALU.mult).then_inc(rstep, 1)
            dve.wait_ge(rstep, 4)
            dve.wait_ge(par_in, 16 * NPAR)
            by_tok = "p h (c b) -> p b c h"
            for b in range(B):
                ts = nc.vector.tensor_scalar(ptab[:, :, P_LG:P_BETA].rearrange(by_tok, c=CH)[:, b], rz[:, b], -1.0, None, ALU.mult)
            ts.then_inc(tab_done, 1)
            dve.wait_ge(astep, 5)
            for b in range(B):
                nc.vector.tensor_copy(ptab[:, :, P_BETA:P_NBD].rearrange(by_tok, c=CH)[:, b], beta[:, b]).then_inc(rstep, 1)
            dve.wait_ge(rstep, 4 + B)
            nc.vector.scalar_tensor_tensor(out=ptab[:, :, P_NBD:P_G], in0=ptab[:, :, P_G:P_END], scalar=-1.0, in1=ptab[:, :, P_BETA:P_NBD],
                                           op0=ALU.mult, op1=ALU.mult).then_inc(vstep, 1)



def delta_heads(nc, xn_parts, A, const_dram, ptab, osq, og_dram):
    with ExitStack() as ctx:
        sem = semaphores(nc, ctx, "gd")

        def sb(n, s, d=F32):
            return ctx.enter_context(nc.sbuf_tensor(f"gd_{n}", s, d))

        cst = sb("cst", [P, C_W])
        ident, upper, later = cst[:, C_ID:C_ID + P], cst[:, C_UP:C_UP + P], cst[:, C_GT:C_GT + P]
        ones = cst[:, C_ONE:C_ONE + P]
        wraw = sb("wraw", [P, 4, DIM])
        w_parts = [sb(n, [P, 4, KT, P], F32R) for n in ("w_lead", "w_rest")]
        cur_a = sb("cur_a", [P, PN])
        cur_s = sb("cur_s", [P, 2, 2, B])
        pre = sb("pre", [P, 2, 3, B, 3 + P])
        conv = sb("conv", [P, 3, B, P])
        kT = sb("kT", [P, 2, BN])
        qT = sb("qT", [P, 2, BN])
        vT = sb("vT", [P, BN])
        gate = sb("gate", [P, 2, BN])
        diag = sb("diag", [P, 2, B, P])
        root = sb("root", [P, 2, B])
        rn = sb("rn", [P, 2, 2, B])
        brk = sb("brk", [P, 2, B])
        grq = sb("grq", [P, 2, B])
        lgm = sb("lgm", [P, B, P])
        D = sb("D", [P, B, P])
        Dm = sb("Dm", [P, B, P])
        AT = sb("AT", [P, B, P])
        PT = sb("PT", [P, B, P])
        Kd = sb("Kd", [P, B, P])
        Vb = sb("Vb", [P, B, P])
        Lo = sb("Lo", [P, B, P])
        T = sb("T", [P, B, P])
        W = sb("W", [P, B, P])
        Y = sb("Y", [P, NLV, B, P])
        R = sb("R", [P, B, P])
        U = sb("U", [P, B, P])
        S = sb("S", [P, B, P])
        oi = sb("oi", [P, B, P])
        o = sb("o", [P, B, P])
        osqr = sb("osqr", [P, B, P])
        o2 = sb("o2", [P, B])
        og = sb("og", [P, 2, BN])
        PJ = ctx.enter_context(nc.psum_tensor("gd_PJ", [P, 2, BN], F32))
        Bk = [ctx.enter_context(nc.psum_tensor(f"gd_B{k}", [P, B, P], F32)) for k in range(6)]
        half = [Bk[k][:, 0:2, :].rearrange("p a (h c) -> p (a h) c", h=2) for k in range(6)]

        cst_in, w_in = sem("cst_in"), sem("w_in")
        og_out = [sem("og_out0"), sem("og_out1")]
        w_turned, w_lead, w_copied = sem("w_turned"), sem("w_lead"), sem("w_copied")
        projected, pre_done, tap_done, silu_done = (sem(x) for x in ("projected", "pre", "tap", "silu"))
        kdiag, qdiag, lengths2, root_done, max_done, rnorm_done, brk_ready = (
            sem(x) for x in ("kdiag", "qdiag", "len2", "root", "max", "rnorm", "brk"))
        head_a, decay_in, zeroed, halo_done, osq_zero = (
            sem(x) for x in ("head_a", "decay_in", "zeroed", "halo", "osq_zero"))
        darg, kk_done, kq_done, qq_done, k_turned, v_turned, l_turned, o_turned = (
            sem(x) for x in ("darg", "kk", "kq", "qq", "ktr", "vtr", "ltr", "otr"))
        d_exp, d_cut, dm_ready, at_ready, pt_ready, kd_ready, vb_ready, l_ready = (
            sem(x) for x in ("dexp", "dcut", "dm", "at", "pt", "kd", "vb", "l"))
        oi_sum, oi_ready, o_ready = sem("oisum"), sem("oi"), sem("o")
        t_mask, t_ready, w2_turned, w_first = sem("tmask"), sem("t2"), sem("w2t"), sem("w2")
        y_sum, y_ready, wup, w_ready, tup, t_next = (sem(x) for x in ("ysum", "y", "wup", "w", "tup", "t"))
        ks_done, r_ready, u_sum, u_ready, o_sum, og_ready, o2_ready, osq_done, s_sum, s_ready = (
            sem(x) for x in ("ks", "r", "usum", "u", "osum", "og", "o2", "osq", "ssum", "s"))
        block = ctx.enter_context(nc.Block())
        LAST = HEADS - 1
        W_BANK = (0, 0, 0, 1)

        def heads(eng, slot):
            with eng.Fori(0, LAST) as i:
                for c in range(CH):
                    slot(i, c, True, True)
            for c in range(CH):
                slot(LAST, c, c < CH - 1, False)

        @block.sync
        def _(sp):
            def load_weights(i):
                for j, n in enumerate(("Wk", "Wq", "Wv", "Wg")):
                    sp.dma_start(wraw[:, j, :], A[n][bass.ds(i * P, P), :]).then_inc(w_in, 16)

            sp.dma_start(cst[:, :], const_dram).then_inc(cst_in, 16)
            load_weights(0)
            sp.wait_ge(w_turned, 4)
            load_weights(1)

            def store(i, c):
                n = i * CH + c
                sp.wait_ge(og_ready, n + 2)
                dst = og_dram[bass.ds(i * P, P), :].rearrange("p (b c t) -> p c b t", b=B, c=CH)[:, c]
                sp.dma_start(dst, og[:, c % 2, :].rearrange("p (b t) -> p b t", b=B)).then_inc(og_out[c % 2], 16)

            with sp.Fori(0, HEADS - 2) as i:
                for c in range(CH):
                    store(i, c)
                sp.wait_ge(w_turned, i * 4 + 8)
                load_weights(i + 2)
            for i in (HEADS - 2, HEADS - 1):
                for c in range(CH):
                    store(i, c)
            for s in range(2):
                sp.wait_ge(og_out[s], 16 + 8 * HEADS * CH)

        @block.tensor
        def _(pe):
            def turn_weights(h, j):
                if j == 0:
                    pe.wait_ge(w_in, h * 64 + 64)
                elif W_BANK[j] == W_BANK[j - 1]:
                    pe.wait_ge(w_copied, h * 4 + j)
                for k in range(KT):
                    tr = pe.transpose(PJ[:, W_BANK[j], k * P:(k + 1) * P], wraw[:, j, k * P:(k + 1) * P], ident)
                tr.then_inc(w_turned, 1)

            def project(m, h, cm, lo, hi):
                for f in range(lo, hi):
                    j, k = f // KT, f % KT
                    if k == 0:
                        if cm == 0:
                            pe.wait_ge(w_copied, h * 4 + 3 + j % 2)
                        if j >= 2:
                            pe.wait_ge(pre_done, m * 3 + j - 1)
                    for wp, xp in ((1, 0), (0, 1), (0, 0)):
                        rhs = xn_parts[xp][:, k, :].rearrange("p (b c t) -> p c b t", b=B, c=CH)[:, cm]
                        mm = pe.matmul(PJ[:, j % 2, :].rearrange("p (b t) -> p b t", b=B), w_parts[wp][:, j, k, :], rhs,
                                       start=(k == 0 and wp == 1), stop=(k == KT - 1 and wp + xp == 0))
                    if k == KT - 1:
                        mm.then_inc(projected, 1)

            def chunk_decays(m):
                pe.wait_ge(decay_in, m + 1)
                for b in range(B):
                    mm = pe.matmul(Bk[1][:, b, :], lgm[:, b, :], upper, start=True, stop=True)
                mm.then_inc(darg, 1)

            def key_products(m, k_c):
                pe.wait_ge(silu_done, m * 4 + 1)
                for b in range(B):
                    mm = pe.matmul(Bk[4][:, b, :], k_c[b], k_c[b], start=True, stop=True)
                mm.then_inc(kk_done, 1)

            def query_squares(m, q_c):
                pe.wait_ge(silu_done, m * 4 + 2)
                for b in range(B):
                    mm = pe.matmul(Bk[5][:, b, :], q_c[b], q_c[b], start=True, stop=True)
                mm.then_inc(qq_done, 1)

            def query_products(k_c, q_c):
                for b in range(B):
                    mm = pe.matmul(Bk[3][:, b, :], k_c[b], q_c[b], start=True, stop=True)
                mm.then_inc(kq_done, 1)

            def turn_keys(k_c):
                for b in range(B):
                    tr = pe.transpose(Bk[2][:, b, :], k_c[b], ident)
                tr.then_inc(k_turned, 1)

            def turn_products(m):
                pe.wait_ge(at_ready, m + 1)
                for b in range(B):
                    tr = pe.transpose(Bk[0][:, b, :], AT[:, b, :], ident)
                tr.then_inc(l_turned, 1)

            def of(x, par):
                return [x[:, par, b * P:(b + 1) * P] for b in range(B)]

            def slot(i, c, nxt, more):
                n = i * CH + c
                m, hm, cm, parm = n + 1, (i + 1 if c == CH - 1 else i), (c + 1) % CH, (c + 1) % 2
                k_c, q_c, k_m, q_m = of(kT, c % 2), of(qT, c % 2), of(kT, parm), of(qT, parm)

                def values():
                    pe.wait_ge(silu_done, n * 4 + 4)
                    for b in range(B):
                        tr = pe.transpose(Bk[5][:, b, :], vT[:, b * P:(b + 1) * P], ident)
                    tr.then_inc(v_turned, 1)

                def retrieved():
                    if c > 0:
                        for b in range(B):
                            mm = pe.matmul(Bk[4][:, b, :], k_c[b], S[:, b, :], start=True, stop=True)
                        mm.then_inc(ks_done, 1)

                def state_outputs():
                    if c > 0:
                        if nxt:
                            pe.wait_ge(d_exp, m + 1)
                        for b in range(B):
                            mm = pe.matmul(Bk[1][:, b, :], q_c[b], S[:, b, :], start=True, stop=True)
                        mm.then_inc(oi_sum, 1)

                def own(what):
                    if what == "values":
                        values()
                    elif what == "state":
                        state_outputs()
                    elif nxt and what == "chunk":
                        chunk_decays(m)
                    elif nxt and what == "keys":
                        if c > 0:
                            pe.wait_ge(r_ready, i * (CH - 1) + c)
                        key_products(m, k_m)
                    elif nxt and what == "queries":
                        pe.wait_ge(vb_ready, n + 1)
                        query_squares(m, q_m)
                    elif what == "weights":
                        if more and c == CH - 2:
                            pe.wait_ge(pre_done, m * 3 + 3)
                            turn_weights(i + 1, 0)
                    elif nxt:
                        project(m, hm, cm, what, what + 1)

                pe.wait_ge(silu_done, n * 4 + 3)
                if more and c == CH - 1:
                    turn_weights(hm, 3)
                own(0)
                own(1)
                pe.wait_ge(t_ready, n + 1)
                pe.wait_ge(o_ready, n + 1)
                for b in range(B):
                    tr = pe.transpose(Bk[5][:, b, :], T[:, b, :], ident)
                tr.then_inc(w2_turned, 1)
                for f in range(2, KT):
                    own(f)
                pe.wait_ge(s_ready, n + 1)
                retrieved()
                pe.wait_ge(w_first, n + 1)
                pe.wait_ge(kd_ready, n + 1)
                pe.wait_ge(pt_ready, n + 1)
                pe.wait_ge(og_ready, n + 1)
                for l, s in enumerate(LEVELS):
                    for b in range(B):
                        mm = pe.matmul(half[2][:, b, :], Lo[:, b, :], second(W, s)[:, b], start=True, stop=True)
                    mm.then_inc(y_sum, 1)
                    for what in BETWEEN[l][0]:
                        own(what)
                    pe.wait_ge(y_ready, n * NLV + l + 1)
                    if l > 0:
                        pe.wait_ge(t_next, n * (NLV - 1) + l)
                    for b in range(B):
                        mm = pe.matmul(half[3][:, b, :], T[:, b, :], second(Y[:, l], s)[:, b], start=True, stop=True)
                    mm.then_inc(wup, 1)
                    for what in BETWEEN[l][1]:
                        own(what)
                    if l < NLV - 1:
                        pe.wait_ge(w_ready, n * NLV + l + 1)
                        for b in range(B):
                            tr = pe.transpose(Bk[0][:, b, :], W[:, b, :], ident)
                        tr.then_inc(tup, 1)
                if nxt:
                    turn_keys(k_m)
                if more and c == CH - 2:
                    turn_weights(i + 1, 1)
                if c > 0:
                    pe.wait_ge(r_ready, i * (CH - 1) + c)
                    pe.wait_ge(oi_ready, i * (CH - 1) + c)
                else:
                    pe.wait_ge(vb_ready, n + 1)
                    if nxt:
                        pe.wait_ge(d_exp, m + 1)
                pe.wait_ge(w_ready, n * NLV + NLV)
                for b in range(B):
                    mm = pe.matmul(Bk[1][:, b, :], W[:, b, :], (R if c > 0 else Vb)[:, b, :], start=True, stop=True)
                mm.then_inc(u_sum, 1)
                if nxt:
                    query_products(k_m, q_m)
                    turn_products(m)
                    pe.wait_ge(qdiag, m + 1)
                pe.wait_ge(u_ready, n + 1)
                for b in range(B):
                    mm = pe.matmul(Bk[5][:, b, :], PT[:, b, :], U[:, b, :], start=True, stop=True)
                mm.then_inc(o_sum, 1)
                for b in range(B):
                    mm = pe.matmul(Bk[1][:, b, :], Kd[:, b, :], U[:, b, :], start=True, stop=True)
                mm.then_inc(s_sum, 1)
                if more and c == CH - 2:
                    turn_weights(i + 1, 2)
                if nxt:
                    pe.wait_ge(l_ready, m + 1)
                pe.wait_ge(o_ready, n + 2)
                for b in range(B):
                    tr = pe.transpose(Bk[0][:, b, :], o[:, b, :], ident)
                tr.then_inc(o_turned, 1)

            BETWEEN = [((4,), ("values", "chunk")), ((5, 6), (7,)), ((8,), ("state", 9)),
                       (("keys",), (10, 11)), (("queries", 12), ("weights", 13)), ((14, 15), ())]

            pe.wait_ge(cst_in, 16)
            for j in range(4):
                turn_weights(0, j)
            chunk_decays(0)
            project(0, 0, 0, 0, 16)
            key_products(0, of(kT, 0))
            query_squares(0, of(qT, 0))
            query_products(of(kT, 0), of(qT, 0))
            turn_keys(of(kT, 0))
            turn_products(0)
            heads(pe, slot)

        @block.vector
        def _(dve):
            def rest_weights(h, j):
                dve.wait_ge(w_lead, h * 4 + j + 1)
                lead, rest = (part[:, j].rearrange("p k n -> p (k n)") for part in w_parts)
                nc.vector.tensor_tensor(rest, PJ[:, W_BANK[j], :], lead.bitcast(F32), ALU.subtract).then_inc(w_copied, 1)

            def tap(m, parm, j, d):
                if d == 0:
                    dve.wait_ge(halo_done, m + 1)
                    dve.wait_ge(pre_done, m * 3 + j + 1)
                else:
                    dve.wait_ge(tap_done, m * 9 + j * 3 + d)
                nc.vector.scalar_tensor_tensor(out=conv[:, j], in0=pre[:, parm, j, :, d:d + P],
                                               scalar=cur_a[:, 4 * j + d:4 * j + d + 1], in1=conv[:, j],
                                               op0=ALU.mult, op1=ALU.add).then_inc(tap_done, 1)

            def diagonal(m, j, bank, products, done):
                dve.wait_ge(products, m + 1)
                nc.vector.tensor_tensor(diag[:, j], bank[:, :, :], ident.unsqueeze(1).to_broadcast([P, B, P]), ALU.mult).then_inc(done, 1)

            def squared_length(m, j, done):
                dve.wait_ge(done, m + 1)
                nc.vector.tensor_reduce(root[:, j, :], diag[:, j], AX.X, ALU.add).then_inc(lengths2, 1)

            def inverse_norms(m, parm, cm):
                dve.wait_ge(root_done, m + 1)
                nc.vector.tensor_scalar(root[:], root[:], 1e-12, None, ALU.max).then_inc(max_done, 1)
                dve.wait_ge(max_done, m + 1)
                nc.vector.reciprocal(rn[:, parm], root[:]).then_inc(rnorm_done, 1)
                dve.wait_ge(rnorm_done, m + 1)
                for j, col in enumerate((P_BETA, P_NBD)):
                    nc.vector.tensor_tensor(brk[:, j, :], cur_a[:, col + cm * B:col + cm * B + B], rn[:, parm, 0, :], ALU.mult)
                nc.vector.tensor_tensor(grq[:, parm, :], cur_a[:, P_G + cm * B:P_G + cm * B + B], rn[:, parm, 1, :],
                                        ALU.mult).then_inc(brk_ready, 1)

            def level(n, l, between, after):
                s = LEVELS[l]
                dve.wait_ge(y_sum, n * NLV + l + 1)
                mask = cst[:, C_LV + 64 * l:C_LV + 64 * l + 64].rearrange("p (g m) -> p g m", m=s)
                ps = half[2].rearrange("p b (g m) -> p b g m", m=s)
                nc.vector.tensor_tensor(second(Y[:, l], s), ps, mask.unsqueeze(1).to_broadcast([P, B, 64 // s, s]),
                                        ALU.mult).then_inc(y_ready, 1)
                between()
                dve.wait_ge(wup, n * NLV + l + 1)
                nc.vector.tensor_tensor(second(W, s), second(W, s), half[3].rearrange("p b (g m) -> p b g m", m=s),
                                        ALU.add).then_inc(w_ready, 1)
                after()
                if l < NLV - 1:
                    dve.wait_ge(tup, n * (NLV - 1) + l + 1)
                    nc.vector.tensor_copy(first(T, s), first(Bk[0], s)).then_inc(t_next, 1)

            def decayed_products(m):
                dve.wait_ge(kk_done, m + 1)
                dve.wait_ge(dm_ready, m + 1)
                nc.vector.tensor_tensor(AT[:], Bk[4][:, :, :], Dm[:], ALU.mult).then_inc(at_ready, 1)

            def scaled_products(m):
                dve.wait_ge(l_turned, m + 1)
                dve.wait_ge(brk_ready, m + 1)
                nc.vector.tensor_tensor(Lo[:], Bk[0][:, :, :], bc(brk[:, 0, :], P), ALU.mult).then_inc(l_ready, 1)

            def first_inverse(m):
                dve.wait_ge(l_ready, m + 1)
                nc.vector.tensor_tensor(T[:], Lo[:], cst[:, C_M1:C_M1 + P].unsqueeze(1).to_broadcast([P, B, P]), ALU.mult).then_inc(t_mask, 1)
                dve.wait_ge(t_mask, m + 1)
                nc.vector.tensor_tensor(T[:], T[:], ident.unsqueeze(1).to_broadcast([P, B, P]), ALU.add).then_inc(t_ready, 1)

            def query_weights(m):
                dve.wait_ge(kq_done, m + 1)
                nc.vector.tensor_tensor(PT[:], Bk[3][:, :, :], Dm[:], ALU.mult).then_inc(pt_ready, 1)

            def decayed_keys(m):
                dve.wait_ge(k_turned, m + 1)
                nc.vector.tensor_tensor(Kd[:], Bk[2][:, :, :], bc(Dm[:, :, P - 1], P), ALU.mult).then_inc(kd_ready, 1)

            def slot(i, c, nxt, more):
                n = i * CH + c
                m, hm, cm, par, parm = n + 1, (i + 1 if c == CH - 1 else i), (c + 1) % CH, c % 2, (c + 1) % 2

                def targets():
                    if c > 0:
                        dve.wait_ge(vb_ready, n + 1)
                        dve.wait_ge(ks_done, i * (CH - 1) + c)
                        for b in range(B):
                            st = nc.vector.scalar_tensor_tensor(out=R[:, b, :], in0=Bk[4][:, b, :], scalar=brk[:, 1, b:b + 1],
                                                                in1=Vb[:, b, :], op0=ALU.mult, op1=ALU.add)
                        st.then_inc(r_ready, 1)

                def own(what):
                    if what == "targets":
                        targets()
                    elif not nxt:
                        return
                    elif what == "kdiag":
                        diagonal(m, 0, Bk[4], kk_done, kdiag)
                    elif what == "ksum":
                        squared_length(m, 0, kdiag)
                    elif what == "qdiag":
                        diagonal(m, 1, Bk[5], qq_done, qdiag)
                    elif what == "qsum":
                        squared_length(m, 1, qdiag)
                    elif what == "norms":
                        inverse_norms(m, parm, cm)
                    elif what == "weights":
                        if more and c == CH - 2:
                            rest_weights(i + 1, 0)
                    else:
                        tap(m, parm, what // 3, what % 3)

                def several(whats):
                    for what in whats:
                        own(what)

                if more and c == CH - 1:
                    rest_weights(hm, 3)
                dve.wait_ge(w_first, n + 1)
                for l in range(NLV):
                    level(n, l, lambda: several(BETWEEN[l][0]), lambda: several(BETWEEN[l][1]))
                if nxt:
                    decayed_products(m)
                    if more and c == CH - 2:
                        rest_weights(i + 1, 1)
                    scaled_products(m)
                dve.wait_ge(o_sum, n + 1)
                dve.wait_ge(o2_ready, n + 1)
                if c > 0:
                    dve.wait_ge(oi_ready, i * (CH - 1) + c)
                    for b in range(B):
                        st = nc.vector.scalar_tensor_tensor(out=o[:, b, :], in0=Bk[5][:, b, :], scalar=rn[:, par, 1, b:b + 1],
                                                            in1=oi[:, b, :], op0=ALU.mult, op1=ALU.add)
                    st.then_inc(o_ready, 1)
                else:
                    nc.vector.tensor_tensor(o[:], Bk[5][:, :, :], bc(rn[:, par, 1, :], P), ALU.mult).then_inc(o_ready, 1)
                if nxt:
                    first_inverse(m)
                dve.wait_ge(s_sum, n + 1)
                if c > 0:
                    for b in range(B):
                        st = nc.vector.scalar_tensor_tensor(out=S[:, b, :], in0=S[:, b, :], scalar=cur_s[:, par, 1, b:b + 1],
                                                            in1=Bk[1][:, b, :], op0=ALU.mult, op1=ALU.add)
                    st.then_inc(s_ready, 1)
                else:
                    nc.vector.tensor_copy(S[:], Bk[1][:, :, :]).then_inc(s_ready, 1)
                if nxt:
                    decayed_keys(m)
                    query_weights(m)
                dve.wait_ge(o_turned, n + 1)
                dve.wait_ge(og_out[par], i * (8 * CH) + (c // 2) * 16 + 16)
                nc.vector.scalar_tensor_tensor(out=og[:, par, :], in0=Bk[0][:, :, :].rearrange("p b t -> p (b t)"),
                                               scalar=ptab[:, bass.ds(i, 1), PN:PN + 1].rearrange("p o n -> p (o n)"),
                                               in1=gate[:, par, :], op0=ALU.mult, op1=ALU.mult).then_inc(og_ready, 1)
                if more and c == CH - 2:
                    rest_weights(i + 1, 2)
                if nxt:
                    several(AFTER)

            BETWEEN = [((0,), (1,)), ((2,), ()), ((3,), (4, "targets")), ((5,), ("kdiag", "ksum")),
                       (("qdiag",), ("qsum",)), (("norms", "weights", 6), ())]
            AFTER = (7, 8)

            nc.vector.memset(Y[:], 0.0).then_inc(zeroed, 1)
            dve.wait_ge(zeroed, 1)
            for free in (s_ready, o_ready, og_ready):
                dve.sem_inc(free, 1)
            for s in range(2):
                dve.sem_inc(og_out[s], 16)
            dve.wait_ge(cst_in, 16)
            for j in range(4):
                rest_weights(0, j)
            for j in range(3):
                for d in range(3):
                    tap(0, 0, j, d)
            diagonal(0, 0, Bk[4], kk_done, kdiag)
            squared_length(0, 0, kdiag)
            diagonal(0, 1, Bk[5], qq_done, qdiag)
            squared_length(0, 1, qdiag)
            inverse_norms(0, 0, 0)
            decayed_products(0)
            scaled_products(0)
            first_inverse(0)
            query_weights(0)
            decayed_keys(0)
            heads(dve, slot)

        @block.scalar
        def _(act):
            def copy_pre(m, h, parm, cm, j):
                act.wait_ge(projected, m * 4 + j + 1)
                nc.scalar.copy(pre[:, parm, j, :, 3:3 + P], PJ[:, j % 2, :].rearrange("p (b t) -> p b t", b=B))
                if cm == 0:
                    act.wait_ge(head_a, h + 1)
                nc.scalar.activation(conv[:, j], PJ[:, j % 2, :].rearrange("p (b t) -> p b t", b=B), ACT.Identity,
                                     scale=cur_a[:, 4 * j + 3:4 * j + 4], bias=cur_a[:, 12 + j:13 + j]).then_inc(pre_done, 1)

            def lead_weights(h, j):
                act.wait_ge(w_turned, h * 4 + j + 1)
                nc.scalar.copy(w_parts[0][:, j].rearrange("p k n -> p (k n)"), PJ[:, W_BANK[j], :]).then_inc(w_lead, 1)

            def silu(m, j, dst):
                act.wait_ge(tap_done, m * 9 + j * 3 + 3)
                nc.scalar.activation(dst, conv[:, j].rearrange("p b t -> p (b t)"), ACT.Silu).then_inc(silu_done, 1)

            def decays(m):
                act.wait_ge(darg, m + 1)
                nc.scalar.activation(D[:], Bk[1][:, :, :], ACT.Exp).then_inc(d_exp, 1)

            def roots(m):
                act.wait_ge(lengths2, m * 2 + 2)
                nc.scalar.activation(root[:], root[:], ACT.Sqrt).then_inc(root_done, 1)

            def gates(m, parm):
                act.wait_ge(projected, m * 4 + 4)
                nc.scalar.activation(gate[:, parm, :], PJ[:, 1, :], ACT.Silu).then_inc(silu_done, 1)

            def slot(i, c, nxt, more):
                n = i * CH + c
                m, hm, cm, par, parm = n + 1, (i + 1 if c == CH - 1 else i), (c + 1) % CH, c % 2, (c + 1) % 2
                act.wait_ge(w2_turned, n + 1)
                nc.scalar.copy(W[:], Bk[5][:, :, :]).then_inc(w_first, 1)
                silu(n, 2, vT[:, :])
                if more and c == CH - 1:
                    lead_weights(hm, 3)
                if nxt:
                    copy_pre(m, hm, parm, cm, 0)
                act.wait_ge(v_turned, n + 1)
                act.wait_ge(decay_in, n + 1)
                for b in range(B):
                    vb = nc.scalar.activation(Vb[:, b, :], Bk[5][:, b, :], ACT.Copy, scale=cur_s[:, par, 0, b:b + 1])
                vb.then_inc(vb_ready, 1)
                if nxt:
                    decays(m)
                    silu(m, 0, kT[:, parm, :])
                    copy_pre(m, hm, parm, cm, 1)
                if c > 0:
                    act.wait_ge(oi_sum, i * (CH - 1) + c)
                    act.wait_ge(brk_ready, n + 1)
                    for b in range(B):
                        cp = nc.scalar.activation(oi[:, b, :], Bk[1][:, b, :], ACT.Copy, scale=grq[:, par, b:b + 1])
                    cp.then_inc(oi_ready, 1)
                if nxt:
                    silu(m, 1, qT[:, parm, :])
                    copy_pre(m, hm, parm, cm, 2)
                    if more and c == CH - 2:
                        lead_weights(i + 1, 0)
                    roots(m)
                    gates(m, parm)
                    if more and c == CH - 2:
                        lead_weights(i + 1, 1)
                act.wait_ge(u_sum, n + 1)
                nc.scalar.copy(U[:], Bk[1][:, :, :]).then_inc(u_ready, 1)
                act.wait_ge(o_ready, n + 2)
                act.wait_ge(osq_done, n + 1)
                for b in range(B):
                    sq = nc.scalar.activation(osqr[:, b, :], o[:, b, :], ACT.Square, accum_out=o2[:, b:b + 1])
                sq.then_inc(o2_ready, 1)
                if more and c == CH - 2:
                    lead_weights(i + 1, 2)

            act.sem_inc(o2_ready, 1)
            for j in range(4):
                lead_weights(0, j)
            act.wait_ge(halo_done, 1)
            decays(0)
            for j in range(3):
                copy_pre(0, 0, 0, 0, j)
            silu(0, 0, kT[:, 0, :])
            silu(0, 1, qT[:, 0, :])
            gates(0, 0)
            roots(0)
            heads(act, slot)

        @block.gpsimd
        def _(pool):
            def head_params(h):
                nc.gpsimd.tensor_copy(cur_a[:, :], ptab[:, bass.ds(h, 1), 0:PN].rearrange("p o n -> p (o n)")).then_inc(head_a, 1)
                pool.wait_ge(head_a, h + 1)

            def log_decays(parm, cm):
                nc.gpsimd.tensor_tensor(lgm[:], bc(cur_a[:, P_LG + cm * B:P_LG + cm * B + B], P),
                                        later.unsqueeze(1).to_broadcast([P, B, P]), ALU.mult)
                for j, col in enumerate((P_BETA, P_END)):
                    cp = nc.gpsimd.tensor_copy(cur_s[:, parm, j, :], cur_a[:, col + cm * B:col + cm * B + B])
                cp.then_inc(decay_in, 1)

            def halo(parm, cm):
                nxt = pre[:, 1 - parm, :, :, 0:3]
                if cm == CH - 1:
                    nc.gpsimd.memset(nxt, 0.0).then_inc(halo_done, 1)
                else:
                    for j in range(3):
                        cp = nc.gpsimd.tensor_copy(pre[:, 1 - parm, j, :, 0:3], pre[:, parm, j, :, P:P + 3])
                    cp.then_inc(halo_done, 1)

            def next_step(m, parm, cm):
                pool.wait_ge(d_exp, m + 1)
                nc.gpsimd.tensor_tensor(D[:], D[:], upper.unsqueeze(1).to_broadcast([P, B, P]), ALU.mult).then_inc(d_cut, 1)
                pool.wait_ge(rnorm_done, m + 1)
                pool.wait_ge(pre_done, m * 3 + 3)
                pool.wait_ge(d_cut, m + 1)
                nc.gpsimd.tensor_tensor(Dm[:], D[:], bc(rn[:, parm, 0, :], P), ALU.mult).then_inc(dm_ready, 1)
                halo(parm, cm)

            def slot(i, c, nxt, more):
                n = i * CH + c
                m, hm, cm, parm = n + 1, (i + 1 if c == CH - 1 else i), (c + 1) % CH, (c + 1) % 2
                if nxt:
                    if c == CH - 1:
                        head_params(hm)
                    log_decays(parm, cm)
                    next_step(m, parm, cm)
                step_over(n, c, nxt)

            def step_over(n, c, nxt):
                if nxt:
                    pool.wait_ge(kd_ready, n + 2)
                    pool.wait_ge(tap_done, n * 9 + 18)
                    pool.wait_ge(s_ready, n + 2)
                pool.wait_ge(o2_ready, n + 2)
                nc.gpsimd.tensor_tensor(osq[:, :, c], osq[:, :, c], o2[:, :], ALU.add).then_inc(osq_done, 1)

            nc.gpsimd.memset(osq[:], 0.0).then_inc(osq_zero, 1)
            nc.gpsimd.memset(pre[:, 0, :, :, 0:3], 0.0).then_inc(halo_done, 1)
            pool.sem_inc(osq_done, 1)
            pool.wait_ge(osq_zero, 1)
            pool.wait_ge(cst_in, 16)
            head_params(0)
            log_decays(0, 0)
            next_step(0, 0, 0)
            pool.wait_ge(kd_ready, 1)
            pool.wait_ge(tap_done, 9)
            heads(pool, slot)


QH = 4


def delta_out(nc, A, x_dram, const_dram, osq, og_dram, out_dram):
    with ExitStack() as ctx:
        sem = semaphores(nc, ctx, "go")

        def sb(n, s, d=F32):
            return ctx.enter_context(nc.sbuf_tensor(f"go_{n}", s, d))


        ident = sb("ident", [P, P])
        wo = sb("wo", [P, KT, HEADS * P])
        wo_parts = [sb(n, [P, HEADS, DIM], F32R) for n in ("wo_lead", "wo_rest")]
        ogt = sb("ogt", [P, 2, HEADS, P])
        og_parts = [sb(n, [P, 2, HEADS, P], F32R) for n in ("og_lead", "og_rest")]
        xt = sb("xt", [P, 2, DIM])
        yt = sb("yt", [P, 2, DIM])
        eps = sb("eps", [P, 1])
        rs = sb("rs", [P, B, CH])
        psW = [ctx.enter_context(nc.psum_tensor(f"go_psW{k}", [P, DIM], F32)) for k in range(2)]
        psY = [ctx.enter_context(nc.psum_tensor(f"go_psY{k}", [P, DIM], F32)) for k in range(2)]
        cst_in, eps_set = sem("cst_in"), sem("eps_set")
        wo_in = [sem(f"wo_in{j}") for j in range(KT)]
        tile_in, tile_out = [sem("tile_in0"), sem("tile_in1")], [sem("tile_out0"), sem("tile_out1")]
        turned, w_lead, copied, root_done, rs_ready = (sem(x) for x in ("turned", "w_lead", "copied", "root", "rs"))
        lead, rest, y_sum, y_ready = (sem(x) for x in ("lead", "rest", "y_sum", "y_ready"))
        block = ctx.enter_context(nc.Block())
        og_tiles = og_dram.rearrange("(h p) t -> p h t", p=P)
        HQ = HEADS // QH

        def tiles(eng, slot):
            with eng.Fori(0, TILES // 2 - 1) as i:
                for s in range(2):
                    slot(i * 2 + s, i, s, True)
            slot(TILES - 2, TILES // 2 - 1, 0, True)
            slot(TILES - 1, TILES // 2 - 1, 1, False)

        @block.sync
        def _(sp):
            sp.dma_start(ident[:, :], const_dram[:, C_ID:C_ID + P]).then_inc(cst_in, 16)
            for j in range(KT):
                sp.dma_start(wo[:, j, :], A["Wo"][j * P:(j + 1) * P, :]).then_inc(wo_in[j], 16)
            sp.sem_inc(y_ready, 2)

            def slot(t, i, s, nxt):
                sp.wait_ge(y_ready, t + 1)
                sp.dma_start(ogt[:, s], og_tiles[:, :, bass.ds(t * P, P)]).then_inc(tile_in[s], 16)
                sp.dma_start(xt[:, s, :], x_dram[bass.ds(t * P, P), :]).then_inc(tile_in[s], 16)

            tiles(sp, slot)

        @block.tensor
        def _(pe):
            pe.wait_ge(cst_in, 16)
            for j in range(KT):
                pe.wait_ge(wo_in[j], 16)
                for q in range(HQ):
                    n = j * HQ + q
                    if n >= 2:
                        pe.wait_ge(copied, n - 1)
                    for h in range(QH):
                        tr = pe.transpose(psW[n % 2][:, h * P:(h + 1) * P], wo[:, j, (q * QH + h) * P:(q * QH + h + 1) * P], ident[:, :])
                    tr.then_inc(turned, 1)
            pe.wait_ge(copied, KT * HQ)

            def slot(t, i, s, nxt):
                pe.wait_ge(y_ready, t + 1)
                for h in range(HEADS):
                    if h % QH == 0:
                        pe.wait_ge(rest, t * HQ + h // QH + 1)
                    for op, wp in ((1, 0), (0, 1), (0, 0)):
                        mm = pe.matmul(psY[s][:, :], og_parts[op][:, s, h, :], wo_parts[wp][:, h, :],
                                       start=(h == 0 and op == 1), stop=(h == HEADS - 1 and op + wp == 0))
                mm.then_inc(y_sum, 1)

            tiles(pe, slot)

        @block.scalar
        def _(act):
            def leads(t, i, s):
                act.wait_ge(tile_in[s], i * 32 + 32)
                act.wait_ge(y_ready, t + 1)
                for q in range(HQ):
                    hs = slice(q * QH, (q + 1) * QH)
                    nc.scalar.copy(og_parts[0][:, s, hs, :], ogt[:, s, hs, :]).then_inc(lead, 1)

            def slot(t, i, s, nxt):
                if nxt:
                    leads(t + 1, i + s, 1 - s)
                act.wait_ge(y_ready, t + 3)
                act.dma_start(out_dram[bass.ds(t * P, P), :], yt[:, s, :]).then_inc(tile_out[s], 16)

            act.wait_ge(eps_set, 1)
            nc.scalar.activation(rs[:], osq[:, :, :], ACT.Sqrt, bias=eps[:, 0:1], scale=1.0 / (HEADS * P)).then_inc(root_done, 1)
            for n in range(KT * HQ):
                j, q = n // HQ, n % HQ
                act.wait_ge(turned, n + 1)
                nc.scalar.copy(wo_parts[0][:, q * QH:(q + 1) * QH, j * P:(j + 1) * P],
                               psW[n % 2][:, :].rearrange("p (h n) -> p h n", h=QH)).then_inc(w_lead, 1)
            leads(0, 0, 0)
            tiles(act, slot)
            for s in range(2):
                act.wait_ge(tile_out[s], 16 + 8 * TILES)

        @block.vector
        def _(dve):
            def rests(t, s):
                for q in range(HQ):
                    hs = slice(q * QH, (q + 1) * QH)
                    dve.wait_ge(lead, t * HQ + q + 1)
                    nc.vector.tensor_tensor(og_parts[1][:, s, hs, :], ogt[:, s, hs, :], og_parts[0][:, s, hs, :].bitcast(F32),
                                            ALU.subtract).then_inc(rest, 1)

            nc.vector.memset(eps[:, :], RMS_EPS).then_inc(eps_set, 1)
            dve.wait_ge(root_done, 1)
            nc.vector.reciprocal(rs[:], rs[:]).then_inc(rs_ready, 1)
            for s in range(2):
                dve.sem_inc(tile_out[s], 16)
            for n in range(KT * HQ):
                j, q = n // HQ, n % HQ
                piece = (slice(None), slice(q * QH, (q + 1) * QH), slice(j * P, (j + 1) * P))
                dve.wait_ge(w_lead, n + 1)
                nc.vector.tensor_tensor(wo_parts[1][piece], psW[n % 2][:, :].rearrange("p (h n) -> p h n", h=QH),
                                        wo_parts[0][piece].bitcast(F32), ALU.subtract).then_inc(copied, 1)
            dve.wait_ge(rs_ready, 1)
            rs_flat = rs[:].rearrange("p b c -> p (b c)")

            def slot(t, i, s, nxt):
                if nxt:
                    rests(t + 1, 1 - s)
                dve.wait_ge(y_sum, t + 1)
                dve.wait_ge(tile_out[s], i * 16 + 16)
                nc.vector.scalar_tensor_tensor(out=yt[:, s, :], in0=psY[s][:, :], scalar=rs_flat[:, bass.ds(t, 1)],
                                               in1=xt[:, s, :], op0=ALU.mult, op1=ALU.add).then_inc(y_ready, 1)

            rests(0, 0)
            tiles(dve, slot)


def stage_attn(nc, I, const_dram, og_dram, out_dram):
    A = {k[len("L0_attn_"):]: v for k, v in I.items() if k.startswith("L0_attn_")}
    with ExitStack() as ctx:
        osq = ctx.enter_context(nc.sbuf_tensor("osq", [P, B, CH], F32))
        with ExitStack() as inner:
            parts = [inner.enter_context(nc.sbuf_tensor(f"xn_{n}", [P, KT, TOK], F32R)) for n in ("lead", "rest")]
            ptab = inner.enter_context(nc.sbuf_tensor("ptab", [P, HEADS, PW], F32))
            with ExitStack() as gates:
                xnT = gates.enter_context(nc.sbuf_tensor("xnT", [P, KT, TOK], F32))
                layernorm_transposed(nc, "la", I["x"], const_dram, xnT, parts)
                delta_gates(nc, xnT, A, const_dram, ptab)
            delta_heads(nc, parts, A, const_dram, ptab, osq, og_dram)
        delta_out(nc, A, I["x"], const_dram, osq, og_dram, out_dram)


XH, XD = 16, 32
KEYS = 256
KTL = KEYS // P
GR = DIM // P
GH = XH // GR
QMAX, PMAX, SMIN = 127.0, 255.0, 1e-8
LN_PMAX = 5.541263545158426


def cross_setup(nc, X, ctx_dram, x_dram, const_dram, xres, rstd, mean, wq, wp, kbd, vq, bqb, bpb):
    with ExitStack() as ctx:
        sem = semaphores(nc, ctx, "xs")

        def sb(n, s, d=F32):
            return ctx.enter_context(nc.sbuf_tensor(f"xs_{n}", s, d))


        cst = sb("cst", [P, C_W])
        ident = cst[:, C_ID:C_ID + P]
        identb = sb("identb", [P, P], BF16)
        cx = sb("cx", [P, KTL, DIM])
        cxT = sb("cxT", [P, KT, KEYS])
        wkv = sb("wkv", [P, KT, 2 * DIM])
        bkb = sb("bkb", [P, DIM])
        bvc = sb("bvc", [P, GR])
        stats = sb("stats", [P, TILES, 6])
        mv = sb("mv", [P, TILES, 2])
        eps = sb("eps", [P, 1])
        kf = sb("kf", [P, KTL, XH, XD])
        ks = sb("ks", [P, KTL, XH])
        kr = sb("kr", [P, KTL, XH])
        kT = sb("kT", [P, GR, KEYS])
        vT = sb("vT", [P, GR, KEYS])
        vi = sb("vi", [P, GR, KEYS], BF16)
        vs = sb("vs", [P, GR])
        vr = sb("vr", [P, GR])
        parts = [sb(f"part{k}", [P, GR, KEYS], BF16) for k in range(3)]
        bank = [ctx.enter_context(nc.psum_tensor(f"xs_b{k}", [P, DIM], F32)) for k in range(6)]
        bankv = [ctx.enter_context(nc.psum_tensor(f"xs_v{k}", [P, 2 * DIM], BF16)) for k in range(2)]
        cx_in, cst_in, w_in, x_in = sem("cx_in"), sem("cst_in"), sem("w_in"), sem("x_in")
        cx_turned, cxT_ready, k_sum, v_sum, ident_ready = (sem(x) for x in ("cxt", "cxT", "ksum", "vsum", "identb"))
        k_done, k_turned, v_done, v_turned = (sem(x) for x in ("kdone", "kturned", "vdone", "vturned"))
        step, stat, var_done, root, zeroed = (sem(x) for x in ("step", "stat", "var", "root", "zeroed"))
        block = ctx.enter_context(nc.Block())

        @block.sync
        def _(sp):
            sp.dma_start(cst[:, :], const_dram).then_inc(cst_in, 16)
            sp.dma_start(cx[:, :, :], ctx_dram.rearrange("(t p) d -> p t d", p=P)).then_inc(cx_in, 16)
            sp.dma_start(wkv[:, :, :], X["Wkv"].rearrange("(k p) n -> p k n", p=P)).then_inc(w_in, 16)
            sp.dma_start(bkb[:, :], X["bkv"][0:DIM].partition_broadcast(P)).then_inc(w_in, 16)
            sp.dma_start(bvc[:, :], X["bkv"][DIM:2 * DIM].rearrange("(g p) -> p g", p=P), allow_slow_non_contiguous=True).then_inc(w_in, 16)
            sp.dma_start(wp[:, :, :], X["Wp"].rearrange("(g p) n -> p g n", p=P)).then_inc(w_in, 16)
            sp.dma_start(wq[:, :, :], X["Wq"].rearrange("(k p) n -> p k n", p=P)).then_inc(w_in, 16)
            sp.dma_start(bqb[:, :], X["bq"].partition_broadcast(P)).then_inc(w_in, 16)
            sp.dma_start(bpb[:, :], X["bp"].partition_broadcast(P)).then_inc(w_in, 16)
            for b in range(B):
                sp.dma_start(xres[:, b * CH:(b + 1) * CH, :], x_dram[b * SEQ:(b + 1) * SEQ, :].rearrange("(t p) d -> p t d", p=P)).then_inc(x_in, 16)
            sp.wait_ge(w_in, 16 * 7)

        @block.tensor
        def _(pe):
            pe.wait_ge(cst_in, 16)
            pe.wait_ge(cx_in, 16)
            for k in range(KT):
                for t in range(KTL):
                    tr = pe.transpose(bank[k % 2][:, t * P:(t + 1) * P] if k < 2 else bank[k][:, t * P:(t + 1) * P],
                                      cx[:, t, k * P:(k + 1) * P], ident)
                tr.then_inc(cx_turned, 1)
            pe.wait_ge(w_in, 16 * 7)
            pe.wait_ge(cxT_ready, KT)
            for t in range(KTL):
                for k in range(KT):
                    mm = pe.matmul(bank[4 + t][:, :], cxT[:, k, t * P:(t + 1) * P], wkv[:, k, 0:DIM], start=(k == 0), stop=(k == KT - 1))
                mm.then_inc(k_sum, 1)
            for g in range(GR):
                for k in range(KT):
                    mm = pe.matmul(bank[g][:, 0:KEYS], wkv[:, k, DIM + g * P:DIM + (g + 1) * P], cxT[:, k, :], start=(k == 0), stop=(k == KT - 1))
                mm.then_inc(v_sum, 1)
            pe.wait_ge(k_done, 1)
            for g in range(GR):
                for t in range(KTL):
                    tr = pe.transpose(bank[4 + g // 2][:, (g % 2) * KEYS + t * P:(g % 2) * KEYS + (t + 1) * P],
                                      kf[:, t].rearrange("p h d -> p (h d)")[:, g * P:(g + 1) * P], ident)
            tr.then_inc(k_turned, 1)
            pe.wait_ge(v_done, 1)
            pe.wait_ge(ident_ready, 1)
            for t in range(KTL):
                for g in range(GR):
                    tr = pe.transpose(bankv[t][:, g * P:(g + 1) * P], vi[:, g, t * P:(t + 1) * P], identb[:, :])
            tr.then_inc(v_turned, 1)

        @block.scalar
        def _(act):
            for k in range(KT):
                act.wait_ge(cx_turned, k + 1)
                nc.scalar.copy(cxT[:, k, :], bank[k % 2 if k < 2 else k][:, 0:KEYS]).then_inc(cxT_ready, 1)
            act.wait_ge(var_done, TILES)
            nc.scalar.activation(rstd[:, :], mv[:, :, 1], ACT.Sqrt, bias=eps[:, 0:1]).then_inc(root, 1)

        @block.gpsimd
        def _(pool):
            for part in range(3):
                nc.gpsimd.memset(kbd[:, part], 0.0).then_inc(zeroed, 1)

        @block.vector
        def _(dve):
            n = [0]

            def then(ins):
                n[0] += 1
                ins.then_inc(step, 1)
                dve.wait_ge(step, n[0])

            nc.vector.memset(eps[:, :], LN_EPS)
            dve.wait_ge(cst_in, 16)
            nc.vector.tensor_copy(identb[:, :], ident).then_inc(ident_ready, 1)
            dve.wait_ge(k_sum, KTL)
            for t in range(KTL):
                then(nc.vector.tensor_tensor(kf[:, t].rearrange("p h d -> p (h d)"), bank[4 + t][:, :], bkb[:, :], ALU.add))
            then(nc.vector.tensor_reduce(ks[:], kf[:], AX.X, ALU.max, apply_absolute_value=True))
            then(nc.vector.tensor_scalar(ks[:], ks[:], 1.0 / QMAX, SMIN, ALU.mult, ALU.max))
            then(nc.vector.reciprocal(kr[:], ks[:]))
            def all_heads(a):
                return a.rearrange("p t h -> p (t h)").unsqueeze(2).to_broadcast([P, KTL * XH, XD])
            kflat = kf[:].rearrange("p t h d -> p (t h) d")
            then(nc.vector.tensor_tensor(kflat, kflat, all_heads(kr[:]), ALU.mult))
            then(nc.vector.tensor_scalar(kflat, kflat, MAGIC, MAGIC, ALU.add, ALU.subtract))
            then(nc.vector.tensor_tensor(kflat, kflat, all_heads(ks[:]), ALU.mult))
            dve.sem_inc(k_done, 1)
            for g in range(GR):
                dve.wait_ge(v_sum, g + 1)
                then(nc.vector.tensor_scalar(vT[:, g, :], bank[g][:, 0:KEYS], bvc[:, g:g + 1], None, ALU.add))
            then(nc.vector.tensor_reduce(vs[:, :], vT[:], AX.X, ALU.max, apply_absolute_value=True))
            then(nc.vector.tensor_scalar(vs[:, :], vs[:, :], 1.0 / QMAX, SMIN, ALU.mult, ALU.max))
            then(nc.vector.reciprocal(vr[:, :], vs[:, :]))
            then(nc.vector.tensor_tensor(vT[:], vT[:], bc(vr[:, :], KEYS), ALU.mult))
            then(nc.vector.tensor_scalar(vi[:], vT[:], MAGIC, MAGIC, ALU.add, ALU.subtract))
            dve.sem_inc(v_done, 1)
            for g in range(GR):
                nc.vector.tensor_scalar(wp[:, g, :], wp[:, g, :], vs[:, g:g + 1], None, ALU.mult)
            dve.wait_ge(k_turned, 1)
            for h in range(2):
                then(nc.vector.tensor_copy(kT[:, 2 * h:2 * h + 2, :], bank[4 + h][:, :].rearrange("p (g n) -> p g n", g=2)))
            dve.wait_ge(zeroed, 3)
            for part in range(3):
                then(nc.vector.tensor_copy(parts[part][:], kT[:]))
                if part < 2:
                    then(nc.vector.tensor_tensor(kT[:], kT[:], parts[part][:], ALU.subtract))
                for j in range(GH):
                    nc.vector.tensor_copy(kbd[j * XD:(j + 1) * XD, part, :, j * KEYS:(j + 1) * KEYS],
                                          parts[part][j * XD:(j + 1) * XD, :, :])
            dve.wait_ge(v_turned, 1)
            for t in range(KTL):
                nc.vector.tensor_copy(vq[:, t, :], bankv[t][:, 0:DIM])
            for b in range(B):
                dve.wait_ge(x_in, 16 * B)
                for t in range(b * CH, (b + 1) * CH):
                    then(nc.vector.bn_stats(stats[:, t, :], xres[:, t, :]))
                    nc.vector.bn_aggr(mv[:, t, :], stats[:, t, :]).then_inc(var_done, 1)
            dve.wait_ge(var_done, TILES)
            nc.vector.tensor_copy(mean[:, :], mv[:, :, 0])
            dve.wait_ge(root, 1)
            nc.vector.reciprocal(rstd[:, :], rstd[:, :])


def cross_tiles(nc, const_dram, xres, rstd, mean, wq, wp, kbd, vq, bqb, bpb, ahead, out_dram):
    with ExitStack() as ctx:
        sem = semaphores(nc, ctx, "xt")

        def sb(n, s, d=F32):
            return ctx.enter_context(nc.sbuf_tensor(f"xt_{n}", s, d))


        ident = sb("ident", [P, P])
        identb = sb("identb", [P, P], BF16)
        xt = sb("xt", [P, 2, DIM])
        xn = sb("xn", [P, DIM])
        xT = sb("xT", [P, KT, P])
        st = sb("st", [P, 2])
        qf = sb("qf", [P, XH, XD])
        am = sb("am", [P, XH])
        qr = sb("qr", [P, XH])
        qs = sb("qs", [P, 2, XH])
        qi = sb("qi", [P, DIM], BF16)
        qT = sb("qT", [P, 2, GR, P], BF16)
        mx = sb("mx", [P, 2, GH])
        nb = sb("nb", [P, 2, GH])
        E = sb("E", [P, 2, GH, KEYS])
        Pi = sb("Pi", [P, 2, GH * KEYS], BF16)
        PT = sb("PT", [P, 2, GH * KTL, P], BF16)
        sums = sb("sums", [P, 2, XH])
        rec = sb("rec", [P, XH])
        o = sb("o", [P, XH, XD])
        oT = sb("oT", [P, GR, P])
        y = sb("y", [P, 2, DIM])
        psS = [ctx.enter_context(nc.psum_tensor(f"xt_S{k}", [P, GH, KEYS], F32)) for k in range(2)]
        psP = ctx.enter_context(nc.psum_tensor("xt_P", [P, GH * KTL, P], BF16))
        psO = ctx.enter_context(nc.psum_tensor("xt_O", [P, XH, XD], F32))
        psT = ctx.enter_context(nc.psum_tensor("xt_T", [P, DIM], F32))
        psQ = ctx.enter_context(nc.psum_tensor("xt_Q", [P, DIM], F32))
        psTb = psT[:, :].bitcast(BF16)
        ahead_in = sem("ahead_in")
        ident_in, ident_ready, out_done = sem("ident_in"), sem("identb"), [sem("out0"), sem("out1")]
        tile_ready, xn_ready, x_turned, xT_ready, q_sum, qf_ready, am_ready, qs_ready, qr_ready, qn_ready, qi_ready, q_turned, qT_ready = (
            sem(x) for x in ("tile", "xn", "xtr", "xT", "qsum", "qf", "am", "qs", "qr", "qn", "qi", "qtr", "qT"))
        s_sum, mx_ready, nm_ready, nb_ready, exp_done, p_ready, p_turned, pT_ready, pv_sum = (
            sem(x) for x in ("ssum", "mx", "nm", "nb", "exp", "p", "ptr", "pT", "pv"))
        rec_ready, o_ready, o_turned, oT_ready, y_sum, bias_ready, y_ready, st_ready = (
            sem(x) for x in ("rec", "o", "otr", "oT", "ysum", "bias", "y", "st"))
        block = ctx.enter_context(nc.Block())
        SCALE = 1.0 / XD ** 0.5

        def tiles(eng, slot):
            slot(0, 0, 0, False, True)
            with eng.Fori(0, TILES // 2 - 1) as i:
                slot(i * 2 + 1, i, 1, True, True)
                slot(i * 2 + 2, i + 1, 0, True, True)
            slot(TILES - 1, TILES // 2 - 1, 1, True, False)

        @block.sync
        def _(sp):
            sp.dma_start(ident[:, :], const_dram[:, C_ID:C_ID + P]).then_inc(ident_in, 16)
            for dst, src in ahead:
                sp.dma_start(dst, src).then_inc(ahead_in, 16)

            def slot(t, i, s, prev, nxt):
                sp.wait_ge(y_ready, t + 2)
                sp.dma_start(out_dram[bass.ds(t * P, P), :], y[:, s, :]).then_inc(out_done[s], 16)

            tiles(sp, slot)
            if ahead:
                sp.wait_ge(ahead_in, 16 * len(ahead))
            for s in range(2):
                sp.wait_ge(out_done[s], 16 + 8 * TILES)

        @block.gpsimd
        def _(pool):
            def fetch(t, par):
                nc.gpsimd.tensor_tensor(xt[:, par, :], xres[:, bass.ds(t, 1), :].rearrange("p o d -> p (o d)"), bpb[:, :], ALU.add).then_inc(bias_ready, 1)

            def slot(t, i, s, prev, nxt):
                if nxt:
                    pool.wait_ge(y_ready, t + 1)
                    fetch(t + 1, 1 - s)

            pool.wait_ge(ident_in, 16)
            fetch(0, 0)
            tiles(pool, slot)

        @block.tensor
        def _(pe):
            def turn_x(t):
                pe.wait_ge(xn_ready, t + 1)
                for k in range(KT):
                    tr = pe.transpose(psT[:, k * P:(k + 1) * P], xn[:, k * P:(k + 1) * P], ident[:, :])
                tr.then_inc(x_turned, 1)

            def queries(t):
                pe.wait_ge(xT_ready, t + 1)
                for k in range(KT):
                    mm = pe.matmul(psQ[:, :], xT[:, k, :], wq[:, k, :], start=(k == 0), stop=(k == KT - 1))
                mm.then_inc(q_sum, 1)

            def turn_q(t):
                pe.wait_ge(qi_ready, t + 1)
                for g in range(GR):
                    tr = pe.transpose(psTb[:, g * P:(g + 1) * P], qi[:, g * P:(g + 1) * P], identb[:, :])
                tr.then_inc(q_turned, 1)

            def scores(t, par, g):
                for half in range(2):
                    cols = slice(half * DIM, (half + 1) * DIM)
                    for part in range(3):
                        mm = pe.matmul(psS[g % 2][:, :, :].rearrange("p h n -> p (h n)")[:, cols], qT[:, par, g, :],
                                       kbd[:, part, g, cols], start=(part == 0), stop=(part == 2))
                mm.then_inc(s_sum, 1)

            def turn_p(t, g):
                pe.wait_ge(p_ready, t * GR + g + 1)
                pe.wait_ge(pT_ready, t * GR + g + 1)
                for c in range(GH * KTL):
                    tr = pe.transpose(psP[:, c, :], Pi[:, g % 2, c * P:(c + 1) * P], identb[:, :])
                tr.then_inc(p_turned, 1)

            def values(t, g):
                pe.wait_ge(pT_ready, t * GR + g + 2)
                for j in range(GH):
                    h = g * GH + j
                    for k in range(KTL):
                        mm = pe.matmul(psO[:, h, :], PT[:, g % 2, j * KTL + k, :], vq[:, k, h * XD:(h + 1) * XD],
                                       start=(k == 0), stop=(k == KTL - 1))
                mm.then_inc(pv_sum, 1)

            def turn_o(t):
                pe.wait_ge(o_ready, t + 2)
                for g in range(GR):
                    tr = pe.transpose(psT[:, g * P:(g + 1) * P], o[:].rearrange("p h d -> p (h d)")[:, g * P:(g + 1) * P], ident[:, :])
                tr.then_inc(o_turned, 1)

            def project(t):
                pe.wait_ge(oT_ready, t + 1)
                for g in range(GR):
                    mm = pe.matmul(psQ[:, :], oT[:, g, :], wp[:, g, :], start=(g == 0), stop=(g == GR - 1))
                mm.then_inc(y_sum, 1)

            def slot(t, i, s, prev, nxt):
                pe.wait_ge(exp_done, t * GR + 1)
                scores(t, s, 2)
                if prev:
                    pe.wait_ge(qT_ready, t + 1)
                    turn_o(t - 1)
                turn_p(t, 0)
                if nxt:
                    if prev:
                        pe.wait_ge(oT_ready, t)
                    turn_x(t + 1)
                pe.wait_ge(o_ready, t + 1)
                values(t, 0)
                pe.wait_ge(exp_done, t * GR + 2)
                scores(t, s, 3)
                turn_p(t, 1)
                if nxt:
                    if prev:
                        pe.wait_ge(y_ready, t)
                    queries(t + 1)
                values(t, 1)
                turn_p(t, 2)
                if prev:
                    if nxt:
                        pe.wait_ge(qf_ready, t + 2)
                    project(t - 1)
                if nxt:
                    turn_q(t + 1)
                values(t, 2)
                if nxt:
                    pe.wait_ge(qT_ready, t + 2)
                    pe.wait_ge(exp_done, t * GR + 3)
                    scores(t + 1, 1 - s, 0)
                turn_p(t, 3)
                if nxt:
                    pe.wait_ge(exp_done, t * GR + 4)
                    scores(t + 1, 1 - s, 1)
                values(t, 3)

            pe.wait_ge(ident_in, 16)
            pe.wait_ge(ident_ready, 1)
            turn_x(0)
            queries(0)
            turn_q(0)
            pe.wait_ge(qT_ready, 1)
            scores(0, 0, 0)
            scores(0, 0, 1)
            tiles(pe, slot)
            turn_o(TILES - 1)
            project(TILES - 1)

        @block.scalar
        def _(act):
            def copy_xT(t):
                act.wait_ge(x_turned, t + 1)
                nc.scalar.copy(xT[:].rearrange("p k n -> p (k n)"), psT[:, :]).then_inc(xT_ready, 1)

            def copy_qT(t, par):
                act.wait_ge(q_turned, t + 1)
                nc.scalar.copy(qT[:, par].rearrange("p g n -> p (g n)"), psTb[:, 0:DIM]).then_inc(qT_ready, 1)

            def exps(t, s, g):
                act.wait_ge(nb_ready, t * GR + g + 1)
                for j in range(GH):
                    h = g * GH + j
                    ex = nc.scalar.activation(E[:, g % 2, j, :], psS[g % 2][:, j, :], ACT.Exp, scale=qs[:, s, h:h + 1],
                                              bias=nb[:, g % 2, j:j + 1], accum_out=sums[:, s, h:h + 1])
                ex.then_inc(exp_done, 1)

            def copy_p(t, g):
                act.wait_ge(p_turned, t * GR + g + 1)
                nc.scalar.copy(PT[:, g % 2].rearrange("p c n -> p (c n)"), psP[:, :, :].rearrange("p c n -> p (c n)")).then_inc(pT_ready, 1)

            def copy_oT(t):
                act.wait_ge(o_turned, t + 1)
                nc.scalar.copy(oT[:].rearrange("p g n -> p (g n)"), psT[:, :]).then_inc(oT_ready, 1)

            def slot(t, i, s, prev, nxt):
                exps(t, s, 0)
                exps(t, s, 1)
                if prev:
                    copy_oT(t - 1)
                if nxt:
                    copy_xT(t + 1)
                exps(t, s, 2)
                exps(t, s, 3)
                if nxt:
                    copy_qT(t + 1, 1 - s)
                copy_p(t, 3)

            copy_xT(0)
            copy_qT(0, 0)
            tiles(act, slot)
            copy_oT(TILES - 1)

        @block.vector
        def _(dve):
            def normalise(t):
                nc.vector.tensor_copy(st[:, 0:1], mean[:, bass.ds(t, 1)])
                nc.vector.tensor_copy(st[:, 1:2], rstd[:, bass.ds(t, 1)]).then_inc(st_ready, 1)
                dve.wait_ge(st_ready, t + 1)
                nc.vector.tensor_scalar(xn[:, :], xres[:, bass.ds(t, 1), :].rearrange("p o d -> p (o d)"), st[:, 0:1], st[:, 1:2],
                                        ALU.subtract, ALU.mult).then_inc(xn_ready, 1)

            def quantise(t, par):
                dve.wait_ge(q_sum, t + 1)
                nc.vector.tensor_tensor(qf[:].rearrange("p h d -> p (h d)"), psQ[:, :], bqb[:, :], ALU.add).then_inc(qf_ready, 1)
                dve.wait_ge(qf_ready, t + 1)
                nc.vector.tensor_reduce(am[:, :], qf[:], AX.X, ALU.max, apply_absolute_value=True).then_inc(am_ready, 1)
                dve.wait_ge(am_ready, t + 1)
                nc.vector.tensor_scalar(qs[:, par, :], am[:, :], SCALE / QMAX, SMIN, ALU.mult, ALU.max).then_inc(qs_ready, 1)
                dve.wait_ge(qs_ready, t + 1)
                nc.vector.reciprocal(qr[:, :], qs[:, par, :]).then_inc(qr_ready, 1)
                dve.wait_ge(qr_ready, t + 1)
                nc.vector.tensor_tensor(qf[:], qf[:], bc(qr[:, :], XD), ALU.mult).then_inc(qn_ready, 1)
                dve.wait_ge(qn_ready, t * 2 + 1)
                nc.vector.tensor_scalar(qf[:], qf[:], SCALE, MAGIC, ALU.mult, ALU.add).then_inc(qn_ready, 1)
                dve.wait_ge(qn_ready, t * 2 + 2)
                nc.vector.tensor_scalar(qi[:, :], qf[:].rearrange("p h d -> p (h d)"), MAGIC, None, ALU.subtract).then_inc(qi_ready, 1)

            def maxima(t, s, g):
                dve.wait_ge(s_sum, t * GR + g + 1)
                nc.vector.tensor_reduce(mx[:, g % 2, :], psS[g % 2][:, :, :], AX.X, ALU.max).then_inc(mx_ready, 1)
                dve.wait_ge(mx_ready, t * GR + g + 1)
                nc.vector.scalar_tensor_tensor(out=nb[:, g % 2, :], in0=mx[:, g % 2, :], scalar=-1.0,
                                               in1=qs[:, s, g * GH:(g + 1) * GH], op0=ALU.mult, op1=ALU.mult).then_inc(nm_ready, 1)
                dve.wait_ge(nm_ready, t * GR + g + 1)
                nc.vector.tensor_scalar(nb[:, g % 2, :], nb[:, g % 2, :], LN_PMAX, None, ALU.add).then_inc(nb_ready, 1)

            def integers(t, g):
                dve.wait_ge(exp_done, t * GR + g + 1)
                nc.vector.tensor_scalar(Pi[:, g % 2, :], E[:, g % 2].rearrange("p h n -> p (h n)"), MAGIC, MAGIC,
                                        ALU.add, ALU.subtract).then_inc(p_ready, 1)

            def copy_p(t, g):
                dve.wait_ge(p_turned, t * GR + g + 1)
                nc.vector.tensor_copy(PT[:, g % 2], psP[:, :, :]).then_inc(pT_ready, 1)

            def outputs(t):
                dve.wait_ge(rec_ready, t + 1)
                dve.wait_ge(pv_sum, t * GR + GR)
                nc.vector.tensor_tensor(o[:], psO[:, :, :], bc(rec[:, :], XD), ALU.mult).then_inc(o_ready, 1)

            def add(t, i, s):
                dve.wait_ge(y_sum, t + 1)
                dve.wait_ge(bias_ready, t + 1)
                dve.wait_ge(out_done[s], i * 16 + 16)
                nc.vector.tensor_tensor(y[:, s, :], psQ[:, :], xt[:, s, :], ALU.add).then_inc(y_ready, 1)

            def slot(t, i, s, prev, nxt):
                maxima(t, s, 1)
                if nxt:
                    normalise(t + 1)
                if prev:
                    outputs(t - 1)
                integers(t, 0)
                maxima(t, s, 2)
                copy_p(t, 0)
                integers(t, 1)
                maxima(t, s, 3)
                copy_p(t, 1)
                integers(t, 2)
                if nxt:
                    quantise(t + 1, 1 - s)
                integers(t, 3)
                copy_p(t, 2)
                if prev:
                    add(t - 1, i - 1 + s, 1 - s)
                nc.vector.reciprocal(rec[:, :], sums[:, s, :]).then_inc(rec_ready, 1)
                if nxt:
                    maxima(t + 1, 1 - s, 0)

            dve.sem_inc(pT_ready, 1)
            dve.sem_inc(o_ready, 1)
            dve.sem_inc(y_ready, 1)
            for s in range(2):
                dve.sem_inc(out_done[s], 16)
            dve.wait_ge(ident_in, 16)
            nc.vector.tensor_copy(identb[:, :], ident[:, :]).then_inc(ident_ready, 1)
            normalise(0)
            quantise(0, 0)
            maxima(0, 0, 0)
            tiles(dve, slot)
            outputs(TILES - 1)
            add(TILES - 1, TILES // 2 - 1, 1)


def stage_xattn(nc, I, x_dram, const_dram, ahead, out_dram):
    X = {k[len("L0_xattn_"):]: v for k, v in I.items() if k.startswith("L0_xattn_")}
    with ExitStack() as ctx:
        def sb(n, s, d=F32):
            return ctx.enter_context(nc.sbuf_tensor(f"x_{n}", s, d))

        xres, rstd, mean = sb("xres", [P, TILES, DIM]), sb("rstd", [P, TILES]), sb("mean", [P, TILES])
        wq, wp = sb("wq", [P, KT, DIM]), sb("wp", [P, GR, DIM])
        kbd = sb("kbd", [P, 3, GR, GH * KEYS], BF16)
        vq = sb("vq", [P, KTL, DIM], BF16)
        bqb, bpb = sb("bqb", [P, DIM]), sb("bpb", [P, DIM])
        cross_setup(nc, X, I["ctx_2048"], x_dram, const_dram, xres, rstd, mean, wq, wp, kbd, vq, bqb, bpb)
        cross_tiles(nc, const_dram, xres, rstd, mean, wq, wp, kbd, vq, bqb, bpb, ahead, out_dram)


DH = 128
KV = 4
REP = HEADS // KV
ROT = 64
QN = HEADS * DH // DIM
RT = QN + 1
EXPERTS, INNER = 8, 256
IT = INNER // P
E_AT = [P * i * (i + 1) // 2 for i in range(CH)]
E_W = P * CH * (CH + 1) // 2
PT_AT = [0, 4 * P, 8 * P, 7 * P]
S_BANKS = [(0, [(3, 0)]), (1, [(2, 0), (0, 3 * P)]), (2, [(1, 0)])]
P_BANKS = [(3, [0]), (4, [1, 3]), (5, [2])]


def self_setup(nc, F, x_dram, const_dram, stat, wq, wk, wv, qnw, knw):
    with ExitStack() as ctx:
        sem = semaphores(nc, ctx, "ss")

        def sb(n, s, d=F32):
            return ctx.enter_context(nc.sbuf_tensor(f"ss_{n}", s, d))


        xt = sb("xt", [P, CH, DIM])
        bns = sb("bns", [P, TILES, 6])
        mv = sb("mv", [P, TILES, 2])
        ln1 = sb("ln1", [P, KT])
        eps = sb("eps", [P, 2])
        ms = sb("ms", [P, TILES])
        w_in, x_in, bn_done, var_done, step, root, eps_set = (
            sem(x) for x in ("w_in", "x_in", "bn", "var", "step", "root", "eps"))
        block = ctx.enter_context(nc.Block())

        @block.sync
        def _(sp):
            for b in range(B):
                if b > 0:
                    sp.wait_ge(bn_done, b * CH)
                sp.dma_start(xt[:, :, :], x_dram[b * SEQ:(b + 1) * SEQ, :].rearrange("(t p) d -> p t d", p=P)).then_inc(x_in, 16)
            sp.wait_ge(w_in, 16 * 3)

        @block.scalar
        def _(act):
            act.dma_start(ln1[:, :], F["ln1_w"].rearrange("(k p) -> p k", p=P), allow_slow_non_contiguous=True).then_inc(w_in, 16)
            act.dma_start(qnw[:, :], F["qnorm_w"].partition_broadcast(P)).then_inc(w_in, 16)
            act.dma_start(knw[:, :], F["knorm_w"].partition_broadcast(P)).then_inc(w_in, 16)
            act.wait_ge(eps_set, 1)
            act.wait_ge(var_done, TILES)
            nc.scalar.activation(stat[:, 1, :], mv[:, :, 1], ACT.Sqrt, bias=eps[:, 0:1]).then_inc(root, 1)
            act.wait_ge(step, 3)
            nc.scalar.activation(ms[:, :], ms[:, :], ACT.Sqrt, bias=eps[:, 1:2]).then_inc(root, 1)

        @block.vector
        def _(dve):
            nc.vector.memset(eps[:, 0:1], LN_EPS)
            nc.vector.memset(eps[:, 1:2], RMS_EPS).then_inc(eps_set, 1)
            dve.wait_ge(w_in, 16 * 3)
            for w in (wq, wk, wv):
                for k in range(KT):
                    nc.vector.tensor_scalar(w[:, k, :], w[:, k, :], ln1[:, k:k + 1], None, ALU.mult)
            for b in range(B):
                dve.wait_ge(x_in, 16 * (b + 1))
                for t in range(CH):
                    nc.vector.bn_stats(bns[:, b * CH + t, :], xt[:, t, :]).then_inc(bn_done, 1)
                for t in range(b * CH, (b + 1) * CH):
                    dve.wait_ge(bn_done, t + 1)
                    nc.vector.bn_aggr(mv[:, t, :], bns[:, t, :]).then_inc(var_done, 1)
            dve.wait_ge(var_done, TILES)
            nc.vector.tensor_copy(stat[:, 0, :], mv[:, :, 0])
            dve.wait_ge(root, 1)
            nc.vector.reciprocal(stat[:, 1, :], stat[:, 1, :]).then_inc(step, 1)
            dve.wait_ge(step, 1)
            nc.vector.tensor_tensor(ms[:, :], stat[:, 1, :], stat[:, 1, :], ALU.mult).then_inc(step, 1)
            dve.wait_ge(step, 2)
            nc.vector.tensor_tensor(ms[:, :], ms[:, :], mv[:, :, 1], ALU.mult).then_inc(step, 1)
            dve.wait_ge(root, 2)
            nc.vector.reciprocal(stat[:, 2, :], ms[:, :])


def self_attention(nc, F, x_dram, const_dram, rope_dram, stat, wq, wk, wv, qnw, knw, x1_dram):
    turns = [("h", 0, 0), ("h", 1, 0)]
    for i in range(CH):
        if i >= 1:
            turns += [("h", i + 1, 0)] * (i + 1 < CH) + [("q", i - 1, r) for r in range(RT)]
    turns += [("q", CH - 1, r) for r in range(RT)]
    at = {x: n for n, x in enumerate(turns)}
    NT = len(turns)
    with ExitStack() as ctx:
        sem = semaphores(nc, ctx, "sa")

        def sb(n, s, d=F32):
            return ctx.enter_context(nc.sbuf_tensor(f"sa_{n}", s, d))


        ident = sb("ident", [P, P])
        identb = sb("identb", [P, P], BF16)
        negb = sb("negb", [P, P], BF16)
        rope = sb("rope", [P, CH, 2, ROT])
        st = sb("st", [P, 3, CH])
        xt = sb("xt", [P, CH, DIM])
        hn = sb("hn", [P, 2, DIM])
        hT = sb("hT", [P, 2, KT, P])
        ssq = sb("ssq", [P, RT])
        qss = sb("qss", [P, 1])
        rq = sb("rq", [P, 2])
        qk = sb("qk", [P, HEADS + KV, DH])
        qT = sb("qT", [P, HEADS, SEQ])
        kT = sb("kT", [P, KV, SEQ])
        v = sb("v", [P, CH, KV * DH])
        nmax = sb("nmax", [P, 2, CH])
        E = sb("E", [P, 2, E_W])
        sums = sb("sums", [P, 2, CH])
        rec = sb("rec", [P, CH])
        PT = sb("PT", [P, 2, E_W])
        neg, sqo = PT[:, 1, 0:P], E[:, 0, 0:DIM]
        sw = PT[:, 0, 0:(HEADS + KV) * ROT].rearrange("p (h n) -> p h n", h=HEADS + KV)
        x1 = sb("x1", [P, 2, DIM])
        wo = sb("wo", [P, HEADS, DIM])
        eps = sb("eps", [P, 2])
        o_parts, wo_parts = sb("o_parts", [P, 2, 2, SEQ], F32R), sb("wo_parts", [P, 2, 2, DIM], F32R)
        Bk = [ctx.enter_context(nc.psum_tensor(f"sa_B{k}", [P, DIM], F32)) for k in range(8)]

        def part(buffer, h, rest):
            return buffer[:, h % 2, rest, :]

        cst_in, cst_ready, x_in = sem("cst_in"), sem("cst"), sem("x_in")
        x1_out, wo_in = [sem("x1_out0"), sem("x1_out1")], sem("wo_in")
        st_ready, xn_ready, h_ready, turned, turn_copied = (sem(x) for x in ("st", "xn", "h", "turned", "turncp"))
        q_sum, k_sum, v_sum, sq_done, ss_ready, root, rq_ready, qw_ready, v_ready = (
            sem(x) for x in ("qsum", "ksum", "vsum", "sq", "ss", "root", "rq", "qw", "v"))
        swapped, cosined, rotated = sem("swapped"), sem("cosined"), sem("rotated")
        s_sum, nmax_ready, exp_done, rec_ready, e_ready, p_turned, pt_ready, o_sum, o_ready = (
            sem(x) for x in ("ssum", "nmax", "exp", "rec", "e", "ptr", "pt", "osum", "o"))
        leads, rests, multiplied = sem("leads"), sem("rests"), sem("multiplied")
        y_sum, x1_ready = sem("ysum"), sem("x1")
        block = ctx.enter_context(nc.Block())

        @block.sync
        def _(sp):
            sp.dma_start(ident[:, :], const_dram[:, C_ID:C_ID + P]).then_inc(cst_in, 16)
            sp.dma_start(neg[:, :], const_dram[:, C_NEG:C_NEG + P]).then_inc(cst_in, 16)
            sp.dma_start(rope[:, :, :, :], rope_dram.rearrange("(t p) a n -> p t a n", p=P)).then_inc(cst_in, 16)
            with sp.Fori(0, B) as b:
                sp.wait_ge(x1_ready, b * CH + CH)
                sp.dma_start(xt[:, :, :], x_dram[bass.ds(b * SEQ, SEQ), :].rearrange("(t p) d -> p t d", p=P)).then_inc(x_in, 16)
                for i in range(CH):
                    sp.wait_ge(x1_ready, b * CH + i + 1 + CH)
                    sp.dma_start(x1_dram[bass.ds(b * SEQ + i * P, P), :], x1[:, i % 2, :]).then_inc(x1_out[i % 2], 16)
            for s in range(2):
                sp.wait_ge(x1_out[s], 16 + 8 * TILES)

        @block.tensor
        def _(pe):
            def bank_of_turn(b, n):
                pe.wait_ge(turn_copied, b * NT + n + 1)
                return Bk[6 + n % 2]

            def turn_h(b, i):
                n = at["h", i, 0]
                pe.wait_ge(h_ready, b * CH + i + 1)
                bank = bank_of_turn(b, n)
                for k in range(KT):
                    tr = pe.transpose(bank[:, k * P:(k + 1) * P], hn[:, i % 2, k * P:(k + 1) * P], ident[:, :])
                tr.then_inc(turned, 1)

            def turn_qk(b, i):
                pe.wait_ge(rotated, b * CH + i + 1)
                for r in range(RT):
                    bank = bank_of_turn(b, at["q", i, r])
                    for j in range(REP):
                        tr = pe.transpose(bank[:, j * P:(j + 1) * P], qk[:, r * REP + j, :], ident[:, :])
                    tr.then_inc(turned, 1)

            def project(bank, i, w):
                for k in range(KT):
                    mm = pe.matmul(bank[:, :], hT[:, i % 2, k, :], w[:, k], start=(k == 0), stop=(k == KT - 1))
                return mm

            def scores(n, h):
                for r, (bank, tiles) in enumerate(S_BANKS):
                    pe.wait_ge(exp_done, n * 3 + r + 1)
                    for i, col in tiles:
                        w = (i + 1) * P
                        pe.matmul(Bk[bank][:, col:col + w], qT[:, h, i * P:(i + 1) * P], kT[:, h // REP, 0:w], start=True, stop=False)
                        mm = pe.matmul(Bk[bank][:, col + i * P:col + w], identb[:, :], negb[:, :], start=False, stop=True)
                    mm.then_inc(s_sum, 1)

            def turn_p(n, par):
                pe.wait_ge(e_ready, n + 1)
                for r, (bank, keys) in enumerate(P_BANKS):
                    pe.wait_ge(pt_ready, n * 3 + r + 1)
                    for kk in keys:
                        col = PT_AT[kk] - PT_AT[keys[0]]
                        for i in range(kk, CH):
                            tr = pe.transpose(Bk[bank][:, col + (i - kk) * P:col + (i - kk + 1) * P],
                                              E[:, par, E_AT[i] + kk * P:E_AT[i] + (kk + 1) * P], ident[:, :])
                    tr.then_inc(p_turned, 1)

            def values(n, h):
                pe.wait_ge(pt_ready, n * 3 + 6)
                pe.wait_ge(o_ready, n + 1)
                kv = h // REP
                for kk in range(CH):
                    w = (CH - kk) * P
                    mm = pe.matmul(Bk[6 + h % 2][:, kk * P:SEQ], v[:, kk, kv * DH:(kv + 1) * DH], PT[:, h % 2, PT_AT[kk]:PT_AT[kk] + w],
                                   start=(kk == 0), stop=(kk == CH - 1), skip_group_check=True)
                mm.then_inc(o_sum, 1)

            pe.wait_ge(cst_in, 48)
            pe.wait_ge(cst_ready, 1)
            with pe.Fori(0, B) as b:
                turn_h(b, 0)
                turn_h(b, 1)
                for i in range(CH):
                    pe.wait_ge(turn_copied, b * NT + at["h", i, 0] + 3)
                    pe.wait_ge(x1_ready, b * CH + CH)
                    pe.wait_ge(qw_ready, (b * CH + i) * RT + RT)
                    for s in range(QN):
                        project(Bk[s], i, wq[:, :, s * DIM:(s + 1) * DIM]).then_inc(q_sum, 1)
                    if 1 <= i and i + 1 < CH:
                        turn_h(b, i + 1)
                    if i >= 1:
                        turn_qk(b, i - 1)
                    project(Bk[4], i, wk).then_inc(k_sum, 1)
                    pe.wait_ge(v_ready, b * CH + i + 1)
                    project(Bk[5], i, wv).then_inc(v_sum, 1)
                turn_qk(b, CH - 1)
                pe.wait_ge(turn_copied, b * NT + NT + 2)
                pe.wait_ge(v_ready, b * CH + CH + 1)
                scores(b * HEADS, 0)
                for h in range(HEADS):
                    n = b * HEADS + h
                    if h + 1 < HEADS:
                        scores(n + 1, h + 1)
                    turn_p(n, h % 2)
                    if h >= 1:
                        values(n - 1, h - 1)
                values(b * HEADS + HEADS - 1, HEADS - 1)
                pe.wait_ge(o_ready, b * HEADS + HEADS + 2)
                for h in range(HEADS):
                    pe.wait_ge(rests, b * 2 * HEADS + 2 * h + 2)
                    for i in range(CH):
                        for op, wp in ((1, 0), (0, 1), (0, 0)):
                            mm = pe.matmul(Bk[i][:, :], part(o_parts, h, op)[:, i * P:(i + 1) * P], part(wo_parts, h, wp),
                                           start=(h == 0 and op == 1), stop=(h == HEADS - 1 and op + wp == 0))
                        if h == HEADS - 1:
                            mm.then_inc(y_sum, 1)
                    if h < HEADS - 1:
                        mm.then_inc(multiplied, 1)

        @block.scalar
        def _(act):
            def copy_turn(b, x):
                kind, i, r = x
                n = at[x]
                act.wait_ge(turned, b * NT + n + 1)
                src = Bk[6 + n % 2][:, :]
                if kind == "h":
                    dst = hT[:, i % 2].rearrange("p k n -> p (k n)")
                else:
                    dst = (qT[:, r * REP:(r + 1) * REP, i * P:(i + 1) * P] if r < QN else kT[:, :, i * P:(i + 1) * P])
                    src = src.rearrange("p (h n) -> p h n", h=REP)
                nc.scalar.copy(dst, src).then_inc(turn_copied, 1)

            def square(t, src, col):
                if col > 0:
                    act.wait_ge(sq_done, t * RT + col)
                nc.scalar.activation(sqo[:, :], src, ACT.Square, accum_out=ssq[:, col:col + 1]).then_inc(sq_done, 1)

            def exps(n, par):
                for r, (bank, tiles) in enumerate(S_BANKS):
                    act.wait_ge(nmax_ready, n * 3 + r + 1)
                    for i, col in tiles:
                        w = (i + 1) * P
                        ex = nc.scalar.activation(E[:, par, E_AT[i]:E_AT[i] + w], Bk[bank][:, col:col + w], ACT.Exp,
                                                  bias=nmax[:, par, i:i + 1], accum_out=sums[:, par, i:i + 1])
                    ex.then_inc(exp_done, 1)

            def copy_p(n, par):
                act.wait_ge(p_turned, n * 3 + 2)
                act.wait_ge(pt_ready, n * 3 + 4)
                nc.scalar.copy(PT[:, par, 4 * P:8 * P], Bk[4][:, :]).then_inc(pt_ready, 1)

            def copy_out(n, h):
                act.wait_ge(o_sum, n + 1)
                nc.scalar.copy(qT[:, h, :], Bk[6 + h % 2][:, :]).then_inc(o_ready, 1)

            act.wait_ge(x_in, 16)
            act.dma_start(wo[:, :, :], F["wo"].rearrange("(h p) n -> p h n", p=P)).then_inc(wo_in, 16)
            act.sem_inc(turn_copied, 2)
            act.sem_inc(v_ready, 1)
            act.sem_inc(exp_done, 3)
            act.sem_inc(o_ready, 2)
            act.wait_ge(cst_ready, 1)
            with act.Fori(0, B) as b:
                copy_turn(b, ("h", 0, 0))
                copy_turn(b, ("h", 1, 0))
                for i in range(CH):
                    t = b * CH + i
                    for s in range(QN):
                        act.wait_ge(q_sum, t * QN + s + 1)
                        square(t, Bk[s][:, :], s)
                    act.wait_ge(ss_ready, t + 1)
                    nc.scalar.activation(rq[:, 0:1], qss[:, 0:1], ACT.Sqrt, scale=DH / (HEADS * DH), bias=eps[:, 0:1]).then_inc(root, 1)
                    if 1 <= i and i + 1 < CH:
                        copy_turn(b, ("h", i + 1, 0))
                    if i >= 1:
                        for r in range(RT):
                            copy_turn(b, ("q", i - 1, r))
                    act.wait_ge(k_sum, t + 1)
                    square(t, Bk[4][:, :], QN)
                    act.wait_ge(sq_done, t * RT + RT)
                    nc.scalar.activation(rq[:, 1:2], ssq[:, QN:RT], ACT.Sqrt, scale=1.0 / (KV * DH), bias=eps[:, 1:2]).then_inc(root, 1)
                    act.wait_ge(v_sum, t + 1)
                    nc.scalar.copy(v[:, i, :], Bk[5][:, :]).then_inc(v_ready, 1)
                for r in range(RT):
                    copy_turn(b, ("q", CH - 1, r))
                for h in range(HEADS):
                    n = b * HEADS + h
                    exps(n, h % 2)
                    if h >= 1:
                        copy_p(n - 1, (h - 1) % 2)
                    if h >= 2:
                        copy_out(n - 2, h - 2)
                copy_p(b * HEADS + HEADS - 1, (HEADS - 1) % 2)
                for h in (HEADS - 2, HEADS - 1):
                    copy_out(b * HEADS + h, h)
                act.wait_ge(o_ready, b * HEADS + HEADS + 2)
                act.wait_ge(wo_in, 16)
                for h in range(HEADS):
                    if h >= 2:
                        act.wait_ge(multiplied, b * (HEADS - 1) + h - 1)
                    nc.scalar.copy(part(o_parts, h, 0), qT[:, h, :]).then_inc(leads, 1)
                    nc.scalar.copy(part(wo_parts, h, 0), wo[:, h, :]).then_inc(leads, 1)

        @block.gpsimd
        def _(pool):
            half = ROT // 2
            with pool.Fori(0, B) as b:
                for i in range(CH):
                    t = b * CH + i
                    pool.wait_ge(qw_ready, t * RT + RT + RT)
                    for lo, hi in ((0, half), (half, ROT)):
                        src = (lo + half) % ROT
                        tt = nc.gpsimd.tensor_tensor(sw[:, :, lo:hi], qk[:, :, src:src + half],
                                                     rope[:, i, 1, lo:hi].unsqueeze(1).to_broadcast([P, HEADS + KV, half]), ALU.mult)
                    tt.then_inc(swapped, 1)
                    pool.wait_ge(swapped, t + 1)
                    nc.gpsimd.tensor_tensor(qk[:, :, 0:ROT], qk[:, :, 0:ROT],
                                            rope[:, i, 0, :].unsqueeze(1).to_broadcast([P, HEADS + KV, ROT]), ALU.mult).then_inc(cosined, 1)
                    pool.wait_ge(cosined, t + 1)
                    nc.gpsimd.tensor_tensor(qk[:, :, 0:ROT], qk[:, :, 0:ROT], sw[:, :, :], ALU.add).then_inc(rotated, 1)

        @block.vector
        def _(dve):
            def norms(b, i):
                t = b * CH + i
                nc.vector.tensor_scalar(xt[:, i, :], xt[:, i, :], st[:, 0, i:i + 1], st[:, 1, i:i + 1],
                                        ALU.subtract, ALU.mult).then_inc(xn_ready, 1)
                dve.wait_ge(xn_ready, t + 1)
                nc.vector.tensor_scalar(hn[:, i % 2, :], xt[:, i, :], st[:, 2, i:i + 1], None, ALU.mult).then_inc(h_ready, 1)

            def weigh(b, i):
                t = b * CH + i
                dve.wait_ge(sq_done, t * RT + QN)
                nc.vector.tensor_reduce(qss[:, 0:1], ssq[:, 0:QN], AX.X, ALU.add).then_inc(ss_ready, 1)
                dve.wait_ge(root, t * 2 + 1)
                nc.vector.reciprocal(rq[:, 0:1], rq[:, 0:1]).then_inc(rq_ready, 1)
                dve.wait_ge(rq_ready, t * 2 + 1)
                if i > 0:
                    dve.wait_ge(turned, b * NT + at["q", i - 1, RT - 1] + 1)
                flat = qk[:].rearrange("p h d -> p (h d)")
                for s in range(QN):
                    nc.vector.scalar_tensor_tensor(out=flat[:, s * DIM:(s + 1) * DIM], in0=Bk[s][:, :], scalar=rq[:, 0:1],
                                                   in1=qnw[:, s * DIM:(s + 1) * DIM], op0=ALU.mult, op1=ALU.mult).then_inc(qw_ready, 1)
                dve.wait_ge(root, t * 2 + 2)
                nc.vector.reciprocal(rq[:, 1:2], rq[:, 1:2]).then_inc(rq_ready, 1)
                dve.wait_ge(rq_ready, t * 2 + 2)
                nc.vector.scalar_tensor_tensor(out=flat[:, QN * DIM:RT * DIM], in0=Bk[4][:, :], scalar=rq[:, 1:2],
                                               in1=knw[:, :], op0=ALU.mult, op1=ALU.mult).then_inc(qw_ready, 1)

            def maxima(n, par):
                for r, (bank, tiles) in enumerate(S_BANKS):
                    dve.wait_ge(s_sum, n * 3 + r + 1)
                    for i, col in tiles:
                        mx = nc.vector.tensor_reduce(nmax[:, par, i:i + 1], Bk[bank][:, col:col + (i + 1) * P], AX.X, ALU.max, negate=True)
                    mx.then_inc(nmax_ready, 1)

            def copy_p(n, par):
                dve.wait_ge(p_turned, n * 3 + 1)
                nc.vector.tensor_copy(PT[:, par, 0:4 * P], Bk[3][:, :]).then_inc(pt_ready, 1)
                dve.wait_ge(p_turned, n * 3 + 3)
                dve.wait_ge(pt_ready, n * 3 + 5)
                nc.vector.tensor_copy(PT[:, par, 8 * P:10 * P], Bk[5][:, 0:2 * P]).then_inc(pt_ready, 1)

            def probabilities(n, par):
                dve.wait_ge(exp_done, n * 3 + 6)
                nc.vector.reciprocal(rec[:, :], sums[:, par, :]).then_inc(rec_ready, 1)
                dve.wait_ge(rec_ready, n + 1)
                for i in range(CH):
                    cols = slice(E_AT[i], E_AT[i] + (i + 1) * P)
                    ts = nc.vector.tensor_scalar(E[:, par, cols], E[:, par, cols], rec[:, i:i + 1], None, ALU.mult)
                ts.then_inc(e_ready, 1)

            dve.wait_ge(cst_in, 48)
            nc.vector.memset(eps[:, 0:1], DH * RMS_EPS)
            nc.vector.memset(eps[:, 1:2], RMS_EPS)
            nc.vector.tensor_copy(identb[:, :], ident[:, :])
            nc.vector.tensor_copy(negb[:, :], neg[:, :]).then_inc(cst_ready, 1)
            dve.sem_inc(qw_ready, RT)
            dve.sem_inc(pt_ready, 3)
            dve.sem_inc(x1_ready, CH)
            for s in range(2):
                dve.sem_inc(x1_out[s], 16)
            with dve.Fori(0, B) as b:
                dve.wait_ge(x1_ready, b * CH + CH)
                nc.vector.tensor_copy(st[:], stat[:, :, bass.ds(b * CH, CH)]).then_inc(st_ready, 1)
                dve.wait_ge(st_ready, b + 1)
                dve.wait_ge(x_in, b * 16 + 16)
                norms(b, 0)
                norms(b, 1)
                for i in range(CH):
                    weigh(b, i)
                    if i + 2 < CH:
                        dve.wait_ge(turned, b * NT + at["h", i, 0] + 1)
                        norms(b, i + 2)
                for h in range(HEADS):
                    n = b * HEADS + h
                    maxima(n, h % 2)
                    if h >= 1:
                        copy_p(n - 1, (h - 1) % 2)
                    probabilities(n, h % 2)
                copy_p(b * HEADS + HEADS - 1, (HEADS - 1) % 2)
                for h in range(HEADS):
                    for j, (buffer, whole) in enumerate(((o_parts, qT), (wo_parts, wo))):
                        dve.wait_ge(leads, b * 2 * HEADS + 2 * h + j + 1)
                        nc.vector.tensor_tensor(part(buffer, h, 1), whole[:, h, :], part(buffer, h, 0).bitcast(F32),
                                                ALU.subtract).then_inc(rests, 1)
                for i in range(CH):
                    dve.wait_ge(y_sum, b * CH + i + 1)
                    dve.wait_ge(x1_out[i % 2], b * 32 + (i // 2) * 16 + 16)
                    nc.vector.tensor_tensor(x1[:, i % 2, :], Bk[i][:, :], xt[:, i, :], ALU.add).then_inc(x1_ready, 1)


def moe_route(nc, F, x_dram, x1_dram, const_dram, h2_parts, acc, sig):
    with ExitStack() as ctx:
        sem = semaphores(nc, ctx, "mr")

        def sb(n, s, d=F32):
            return ctx.enter_context(nc.sbuf_tensor(f"mr_{n}", s, d))


        ident = sb("ident", [P, P])
        ln2 = sb("ln2", [P, KT])
        rw = sb("rw", [P, KT, EXPERTS])
        x1 = sb("x1", [P, TILES, DIM])
        hn = sb("hn", [P, CH, DIM])
        h2T = sb("h2T", [P, KT, TOK])
        sqo = sb("sqo", [P, DIM])
        ms = sb("ms", [P, TILES])
        rs = sb("rs", [P, TILES])
        eps = sb("eps", [P, 1])
        psT = [ctx.enter_context(nc.psum_tensor(f"mr_T{k}", [P, SEQ], F32)) for k in range(2)]
        psL = ctx.enter_context(nc.psum_tensor("mr_L", [P, TILES, EXPERTS, 4], F32))
        small_in, x_in = sem("small_in"), sem("x_in")
        x1_in = [sem(f"x1_in{b}") for b in range(B)]
        eps_set, sq_done, root, rs_ready, hn_ready, turned, copied, logits, sig_done, added, lead, rest = (
            sem(x) for x in ("eps", "sq", "root", "rs", "hn", "turned", "copied", "logits", "sig", "added", "lead", "rest"))
        block = ctx.enter_context(nc.Block())

        def tiles(b):
            return slice(b * CH, (b + 1) * CH)

        def tokens(b):
            return slice(b * SEQ, (b + 1) * SEQ)

        @block.sync
        def _(sp):
            for b in range(B):
                sp.dma_start(x1[:, tiles(b), :], x1_dram[tokens(b), :].rearrange("(t p) d -> p t d", p=P)).then_inc(x1_in[b], 16)
                if b == 0:
                    sp.dma_start(ident[:, :], const_dram[:, C_ID:C_ID + P]).then_inc(small_in, 16)
                    sp.dma_start(rw[:, :, :], F["router_w"].rearrange("(k p) e -> p k e", p=P)).then_inc(small_in, 16)
                    sp.dma_start(ln2[:, :], F["ln2_w"].rearrange("(k p) -> p k", p=P), allow_slow_non_contiguous=True).then_inc(small_in, 16)
            sp.dma_start(acc[:, :, :], x_dram.rearrange("(t p) d -> p t d", p=P)).then_inc(x_in, 16)
            sp.wait_ge(small_in, 48)

        @block.gpsimd
        def _(pool):
            pool.wait_ge(x_in, 16)
            for b in range(B):
                pool.wait_ge(x1_in[b], 16)
                nc.gpsimd.tensor_tensor(acc[:, tiles(b), :], acc[:, tiles(b), :], x1[:, tiles(b), :], ALU.add).then_inc(added, 1)

        @block.scalar
        def _(act):
            def lengths(b):
                act.wait_ge(x1_in[b], 16)
                for t in range(b * CH, (b + 1) * CH):
                    if t > 0:
                        act.wait_ge(sq_done, t)
                    nc.scalar.activation(sqo[:, :], x1[:, t, :], ACT.Square, accum_out=ms[:, t:t + 1]).then_inc(sq_done, 1)
                act.wait_ge(sq_done, b * CH + CH)
                nc.scalar.activation(ms[:, tiles(b)], ms[:, tiles(b)], ACT.Sqrt, scale=1.0 / DIM, bias=eps[:, 0:1]).then_inc(root, 1)

            act.wait_ge(eps_set, 1)
            lengths(0)
            act.wait_ge(small_in, 48)
            for b in range(B):
                if b + 1 < B:
                    lengths(b + 1)
                for k in range(KT):
                    act.wait_ge(turned, b * KT + k + 1)
                    h2 = h2T[:, k, tokens(b)]
                    nc.scalar.activation(h2, psT[k % 2][:, :], ACT.Copy, scale=ln2[:, k:k + 1]).then_inc(copied, 1)
                    act.wait_ge(copied, b * KT + k + 1)
                    nc.scalar.copy(h2_parts[0][:, k, tokens(b)], h2).then_inc(lead, 1)
            act.wait_ge(logits, 1)
            nc.scalar.activation(sig[:], psL[:, :, :, 0], ACT.Sigmoid).then_inc(sig_done, 1)

        @block.tensor
        def _(pe):
            def route(b):
                pe.wait_ge(copied, (b + 1) * KT)
                for t in range(b * CH, (b + 1) * CH):
                    for k in range(KT):
                        mm = pe.matmul(psL[:, t, :, 0], h2T[:, k, t * P:(t + 1) * P], rw[:, k, :], start=(k == 0), stop=(k == KT - 1))
                return mm

            pe.wait_ge(small_in, 48)
            for b in range(B):
                pe.wait_ge(hn_ready, (b + 1) * CH)
                for k in range(KT):
                    n = b * KT + k
                    if n >= 2:
                        pe.wait_ge(copied, n - 1)
                    for t in range(CH):
                        tr = pe.transpose(psT[k % 2][:, t * P:(t + 1) * P], hn[:, t, k * P:(k + 1) * P], ident[:, :])
                    tr.then_inc(turned, 1)
                if b > 0:
                    route(b - 1)
            route(B - 1).then_inc(logits, 1)

        @block.vector
        def _(dve):
            def rests(b):
                for k in range(KT):
                    dve.wait_ge(lead, b * KT + k + 1)
                    nc.vector.tensor_tensor(h2_parts[1][:, k, tokens(b)], h2T[:, k, tokens(b)],
                                            h2_parts[0][:, k, tokens(b)].bitcast(F32), ALU.subtract).then_inc(rest, 1)

            nc.vector.memset(eps[:, :], RMS_EPS).then_inc(eps_set, 1)
            for b in range(B):
                dve.wait_ge(root, b + 1)
                nc.vector.reciprocal(rs[:, tiles(b)], ms[:, tiles(b)]).then_inc(rs_ready, 1)
                dve.wait_ge(rs_ready, b + 1)
                if b > 0:
                    dve.wait_ge(turned, b * KT)
                for t in range(CH):
                    nc.vector.tensor_scalar(hn[:, t, :], x1[:, b * CH + t, :], rs[:, b * CH + t:b * CH + t + 1], None, ALU.mult).then_inc(hn_ready, 1)
                if b > 0:
                    rests(b - 1)
            rests(B - 1)


def moe_experts(nc, F, h2_parts, acc, sig, out_dram):
    with ExitStack() as ctx:
        sem = semaphores(nc, ctx, "me")

        def sb(n, s, d=F32):
            return ctx.enter_context(nc.sbuf_tensor(f"me_{n}", s, d))


        EW = 2 * KT * INNER + IT * DIM
        raw = sb("raw", [P, EW])
        parts = [sb(n, [P, 2, EW], F32R) for n in ("lead", "rest")]

        def gate_or_up(ap, j):
            return ap[:, j * KT * INNER:(j + 1) * KT * INNER].rearrange("p (k n) -> p k n", k=KT)

        def down_weights(ap):
            return ap[:, 2 * KT * INNER:EW].rearrange("p (k n) -> p k n", k=IT)

        sg = sb("sg", [P, IT, SEQ])
        rb = sb("rb", [P, EXPERTS])
        rank = sb("rank", [P, EXPERTS])
        gsh = [P, TILES, EXPERTS]
        key, eq, pick, two, comb = (sb(n, gsh) for n in ("key", "eq", "pick", "two", "comb"))
        top = sb("top", [P, TILES])
        a = sb("a", [P, IT, SEQ])
        a_parts = [sb(n, [P, 2, IT, SEQ], F32R) for n in ("a_lead", "a_rest")]
        psG = [ctx.enter_context(nc.psum_tensor(f"me_G{k}", [P, SEQ], F32)) for k in range(IT)]
        psU = [ctx.enter_context(nc.psum_tensor(f"me_U{k}", [P, SEQ], F32)) for k in range(IT)]
        psD = [ctx.enter_context(nc.psum_tensor(f"me_D{k}", [P, DIM], F32)) for k in range(4)]
        w_in, w_lead, w_ready = sem("w_in"), sem("w_lead"), sem("w_ready")
        rb_in, rank_set, step = sem("rb_in"), sem("rank"), sem("step")
        g_sum, u_sum, silu_done, a_done, a_lead, a_ready, d_sum, added, out_done = (
            sem(x) for x in ("gsum", "usum", "silu", "adone", "alead", "a", "dsum", "added", "out"))
        block = ctx.enter_context(nc.Block())
        STEPS = EXPERTS * B
        WP = EW // DIM
        TERMS = ((1, 0), (0, 1), (0, 0))

        @block.sync
        def _(sp):
            def load(e):
                for j, name in enumerate(("wg", "wu")):
                    sp.dma_start(gate_or_up(raw, j), F[name][bass.ds(e, 1)].rearrange("o (k p) n -> p (o k) n", p=P)).then_inc(w_in, 16)
                sp.dma_start(down_weights(raw), F["wd"][bass.ds(e, 1)].rearrange("o (k p) n -> p (o k) n", p=P)).then_inc(w_in, 16)

            load(0)
            sp.dma_start(rb[:, :], F["router_bias"].partition_broadcast(P)).then_inc(rb_in, 16)
            with sp.Fori(0, EXPERTS - 1) as e:
                sp.wait_ge(w_ready, (e + 1) * WP)
                load(e + 1)
            for b in range(B):
                sp.wait_ge(added, (STEPS - B + b + 1) * CH + CH)
                sp.dma_start(out_dram[b * SEQ:(b + 1) * SEQ, :].rearrange("(t p) d -> p t d", p=P), acc[:, b * CH:(b + 1) * CH, :]).then_inc(out_done, 16)
            sp.wait_ge(out_done, 16 * B)

        @block.tensor
        def _(pe):
            def up(i, s, b):
                e = i * 2 + s
                n = e * B + b
                for w, bank, done, used in ((0, psG, g_sum, silu_done), (1, psU, u_sum, a_done)):
                    if b == 0:
                        pe.wait_ge(w_ready, e * WP + (w + 1) * KT * INNER // DIM)
                    for j in range(IT):
                        pe.wait_ge(used, n * IT + j + 1)
                        for k in range(KT):
                            for wp, hp in TERMS:
                                mm = pe.matmul(bank[j][:, :], gate_or_up(parts[wp][:, s], w)[:, k, j * P:(j + 1) * P],
                                               h2_parts[hp][:, k, b * SEQ:(b + 1) * SEQ],
                                               start=(k == 0 and wp == 1), stop=(k == KT - 1 and wp + hp == 0))
                        mm.then_inc(done, 1)

            def down(i, s, b):
                n = (i * 2 + s) * B + b
                if b == 0:
                    pe.wait_ge(w_ready, (i * 2 + s) * WP + WP)
                pe.wait_ge(a_ready, n * IT + 2 * IT)
                for t in range(CH):
                    pe.wait_ge(added, n * CH + t + 1)
                    for j in range(IT):
                        for ap, wp in TERMS:
                            mm = pe.matmul(psD[t][:, :], a_parts[ap][:, b % 2, j, t * P:(t + 1) * P],
                                           down_weights(parts[wp][:, s])[:, j, :],
                                           start=(j == 0 and ap == 1), stop=(j == IT - 1 and wp + ap == 0))
                    mm.then_inc(d_sum, 1)

            def pair(i, more):
                for s in range(2):
                    for b in range(B):
                        if s == 1 or b > 0:
                            up(i, s, b)
                        prev = (i, s, b - 1) if b else (i, 0, B - 1)
                        if s == 1 or b > 0:
                            down(*prev)
                if more:
                    up(i + 1, 0, 0)
                down(i, 1, B - 1)

            up(0, 0, 0)
            with pe.Fori(0, EXPERTS // 2 - 1) as i:
                pair(i, True)
            pair(EXPERTS // 2 - 1, False)

        @block.scalar
        def _(act):
            def lead_weights(e, s):
                act.wait_ge(w_in, e * 48 + 48)
                for q in range(WP):
                    nc.scalar.copy(parts[0][:, s, q * DIM:(q + 1) * DIM], raw[:, q * DIM:(q + 1) * DIM]).then_inc(w_lead, 1)

            def gates(i, s, b):
                n = (i * 2 + s) * B + b
                for j in range(IT):
                    act.wait_ge(g_sum, n * IT + j + 1)
                    act.wait_ge(a_done, n * IT + j + 1)
                    nc.scalar.activation(sg[:, j, :], psG[j][:, :], ACT.Silu).then_inc(silu_done, 1)

            def pair(i, more):
                for s in range(2):
                    for b in range(B):
                        gates(i, s, b)
                        if b == 1 and (s == 0 or more):
                            act.wait_ge(d_sum, (i * 2 + s) * B * CH + CH)
                            lead_weights(i * 2 + s + 1, 1 - s)

            act.sem_inc(silu_done, IT)
            lead_weights(0, 0)
            with act.Fori(0, EXPERTS // 2 - 1) as i:
                pair(i, True)
            pair(EXPERTS // 2 - 1, False)

        @block.gpsimd
        def _(pool):
            def rest_weights(e, s):
                for q in range(WP):
                    cols = slice(q * DIM, (q + 1) * DIM)
                    pool.wait_ge(w_lead, e * WP + q + 1)
                    nc.gpsimd.tensor_tensor(parts[1][:, s, cols], raw[:, cols], parts[0][:, s, cols].bitcast(F32),
                                            ALU.subtract).then_inc(w_ready, 1)

            for e in range(EXPERTS):
                nc.gpsimd.memset(rank[:, e:e + 1], float(EXPERTS - e)).then_inc(rank_set, 1)
            with pool.Fori(0, EXPERTS // 2) as i:
                for s in range(2):
                    rest_weights(i * 2 + s, s)

        @block.vector
        def _(dve):
            def gated(i, s, b):
                n = (i * 2 + s) * B + b
                for j in range(IT):
                    dve.wait_ge(silu_done, n * IT + j + 1 + IT)
                    dve.wait_ge(u_sum, n * IT + j + 1)
                    dve.wait_ge(a_ready, n * IT + j + 1)
                    nc.vector.tensor_tensor(a[:, j, :], psU[j][:, :], sg[:, j, :], ALU.mult).then_inc(a_done, 1)
                for j in range(IT):
                    dve.wait_ge(a_done, n * IT + j + 1 + IT)
                    nc.vector.tensor_copy(a_parts[0][:, b % 2, j, :], a[:, j, :]).then_inc(a_lead, 1)
                for j in range(IT):
                    dve.wait_ge(a_lead, n * IT + j + 1)
                    nc.vector.tensor_tensor(a_parts[1][:, b % 2, j, :], a[:, j, :], a_parts[0][:, b % 2, j, :].bitcast(F32),
                                            ALU.subtract).then_inc(a_ready, 1)

            def add(i, s, b):
                e = i * 2 + s
                n = e * B + b
                for t in range(CH):
                    dve.wait_ge(d_sum, n * CH + t + 1)
                    tile = b * CH + t
                    nc.vector.scalar_tensor_tensor(out=acc[:, tile, :], in0=psD[t][:, :], scalar=comb[:, tile, bass.ds(e, 1)],
                                                   in1=acc[:, tile, :], op0=ALU.mult, op1=ALU.add).then_inc(added, 1)

            def pair(i, more):
                for s in range(2):
                    for b in range(B):
                        if s == 1 or b > 0:
                            gated(i, s, b)
                            add(*((i, s, b - 1) if b else (i, 0, B - 1)))
                if more:
                    gated(i + 1, 0, 0)
                add(i, 1, B - 1)

            n = [0]

            def then(ins):
                n[0] += 1
                ins.then_inc(step, 1)
                dve.wait_ge(step, n[0])

            def per_expert(a):
                return a[:, :].unsqueeze(1).to_broadcast(gsh)

            def shares():
                dve.wait_ge(rb_in, 16)
                dve.wait_ge(rank_set, EXPERTS)
                then(nc.vector.tensor_tensor(key[:], sig[:], per_expert(rb), ALU.add))
                for turn in range(2):
                    then(nc.vector.tensor_reduce(top[:, :], key[:], AX.X, ALU.max))
                    then(nc.vector.tensor_tensor(eq[:], key[:], bc(top[:, :], EXPERTS), ALU.is_equal))
                    then(nc.vector.tensor_tensor(eq[:], eq[:], per_expert(rank), ALU.mult))
                    then(nc.vector.tensor_reduce(top[:, :], eq[:], AX.X, ALU.max))
                    then(nc.vector.tensor_tensor(pick[:], eq[:], bc(top[:, :], EXPERTS), ALU.is_equal))
                    if turn == 0:
                        then(nc.vector.tensor_copy(two[:], pick[:]))
                        then(nc.vector.tensor_scalar(pick[:], pick[:], -1e30, None, ALU.mult))
                        then(nc.vector.tensor_tensor(key[:], key[:], pick[:], ALU.add))
                    else:
                        then(nc.vector.tensor_tensor(two[:], two[:], pick[:], ALU.add))
                then(nc.vector.tensor_tensor(two[:], two[:], sig[:], ALU.mult))
                then(nc.vector.tensor_reduce(top[:, :], two[:], AX.X, ALU.add))
                then(nc.vector.reciprocal(top[:, :], top[:, :]))
                then(nc.vector.tensor_tensor(comb[:], two[:], bc(top[:, :], EXPERTS), ALU.mult))

            dve.sem_inc(a_done, IT)
            dve.sem_inc(a_ready, IT)
            shares()
            dve.sem_inc(added, CH)
            gated(0, 0, 0)
            with dve.Fori(0, EXPERTS // 2 - 1) as i:
                pair(i, True)
            pair(EXPERTS // 2 - 1, False)


def projections(nc, ctx):
    return [ctx.enter_context(nc.sbuf_tensor(f"f_{n}", [P, KT, w], F32)) for n, w in
            (("wq", HEADS * DH), ("wk", KV * DH), ("wv", KV * DH))]


def stage_self(nc, I, x_dram, const_dram, rope_dram, weights, x1_dram):
    F = {k[len("L0_ffn_"):]: v for k, v in I.items() if k.startswith("L0_ffn_")}
    wq, wk, wv = weights
    with ExitStack() as ctx:
        def sb(n, s, d=F32):
            return ctx.enter_context(nc.sbuf_tensor(f"f_{n}", s, d))

        stat = sb("stat", [P, 3, TILES])
        qnw, knw = sb("qnw", [P, HEADS * DH]), sb("knw", [P, KV * DH])
        self_setup(nc, F, x_dram, const_dram, stat, wq, wk, wv, qnw, knw)
        self_attention(nc, F, x_dram, const_dram, rope_dram, stat, wq, wk, wv, qnw, knw, x1_dram)


def stage_moe(nc, I, x_dram, const_dram, x1_dram, out_dram):
    F = {k[len("L0_ffn_"):]: v for k, v in I.items() if k.startswith("L0_ffn_")}
    with ExitStack() as ctx:
        h2_parts = [ctx.enter_context(nc.sbuf_tensor(f"m_{n}", [P, KT, TOK], F32R)) for n in ("lead", "rest")]
        acc = ctx.enter_context(nc.sbuf_tensor("m_acc", [P, TILES, DIM], F32))
        sig = ctx.enter_context(nc.sbuf_tensor("m_sig", [P, TILES, EXPERTS], F32))
        moe_route(nc, F, x_dram, x1_dram, const_dram, h2_parts, acc, sig)
        moe_experts(nc, F, h2_parts, acc, sig, out_dram)


def build(nc, I, out):
    og_dram = nc.dram_tensor("gated_outputs", (HEADS * P, TOK), F32, kind="Internal").ap()
    xa_dram, xb_dram, x1_dram = (nc.dram_tensor(n, (TOK, DIM), F32, kind="Internal").ap() for n in ("after_delta", "after_cross", "x1"))
    stage_attn(nc, I, I["const"], og_dram, xa_dram)
    with ExitStack() as ctx:
        weights = projections(nc, ctx)
        ahead = [(w[:, :, :], I["L0_ffn_" + n].rearrange("(k p) n -> p k n", p=P)) for w, n in zip(weights, ("wq", "wk", "wv"))]
        stage_xattn(nc, I, xa_dram, I["const"], ahead, xb_dram)
        stage_self(nc, I, xb_dram, I["const"], I["rope"], weights, x1_dram)
    stage_moe(nc, I, xb_dram, I["const"], x1_dram, out)


def shape_constants():
    import numpy as np
    r = np.arange(P)
    c = np.zeros((P, C_W), np.float32)
    c[:, C_ID:C_ID + P] = np.eye(P)
    c[:, C_UP:C_UP + P] = r[:, None] <= r[None, :]
    c[:, C_GT:C_GT + P] = r[:, None] > r[None, :]
    c[:, C_M1:C_M1 + P] = -((r[:, None] == r[None, :] + 1) & (r[:, None] % 2 == 1)).astype(np.float32)
    for l, m in enumerate(LEVELS):
        cols = r[(r // m) % 2 == 1]
        hit = (r[:, None] // (2 * m) == cols[None, :] // (2 * m)) & ((r[:, None] // m) % 2 == 0)
        c[:, C_LV + 64 * l:C_LV + 64 * l + 64] = -hit.astype(np.float32)
    c[:, C_ONE:C_ONE + P] = 1.0
    c[:, C_NEG:C_NEG + P] = np.where(r[None, :] > r[:, None], np.float32(-1e30), np.float32(0))
    return c


def rope_table():
    import numpy as np
    half = np.arange(0, 64, 2, dtype=np.float32) / np.float32(64)
    freq = np.float32(1.0) / np.power(np.float32(1000000.0), half)
    ang = np.arange(SEQ, dtype=np.float32)[:, None] * freq[None, :].astype(np.float32)
    cos, sin = np.cos(ang), np.sin(ang)
    return np.stack([np.concatenate([cos, cos], 1), np.concatenate([-sin, sin], 1)], 1).astype(np.float32)


def kernel(**inputs):
    import numpy as np
    import concourse.bacc as bacc
    from concourse.bass_utils import run_bass_kernel_spmd as run

    nc = bacc.Bacc("TRN2", target_bir_lowering=False, num_devices=1)
    arrays, I = {}, {}

    def give(name, a):
        arrays[f"in_{name}"] = a
        I[name] = nc.dram_tensor(f"in_{name}", a.shape, mybir.dt.from_np(a.dtype), kind="ExternalInput").ap()

    for name, a in inputs.items():
        a = np.ascontiguousarray(a)
        if name in ("x", "ctx_2048"):
            a = a.reshape(-1, DIM)
        give(name, a)
    give("const", shape_constants())
    give("rope", rope_table())
    out = nc.dram_tensor("out", (TOK, DIM), F32, kind="ExternalOutput").ap()
    build(nc, I, out)
    got = run(nc, [arrays], core_ids=[0]).results[0]["out"]
    return got.reshape(B, SEQ, DIM)
```
